# Optimizing a Trainium2 kernel written in Bass

```python
import numpy as np
import jax
import jax.numpy as jnp

def _softmax(x, axis=-1):
    return jax.nn.softmax(x, axis=axis)

def _gelu(x):
    return jax.nn.gelu(x, approximate=True)

def _silu(x):
    return jax.nn.silu(x)

def _sigmoid(x):
    return jax.nn.sigmoid(x)

def _layernorm(x, axis=-1, eps=1e-05):
    m = jnp.mean(x, axis=axis, keepdims=True)
    v = jnp.var(x, axis=axis, keepdims=True)
    return (x - m) / jnp.sqrt(v + eps)

def _scatter_add(tgt, idx, src, axis=0):
    return tgt.at[idx].add(src)

def _segment_sum(src, seg, n):
    return jax.ops.segment_sum(src, seg, n)
kernel_name = 'mk_xattn_ffn_d2_seqx_r8_50ddb7'

def setup_inputs(seed: int=0):
    np.random.seed(seed)
    _w = jnp.asarray

    def _rec_inputs():
        import jax
        import jax.numpy as jnp
        _rk = jax.random.key(seed)
        x = -0.0002928 + 1 * jax.random.normal(jax.random.fold_in(_rk, 1), (16, 256, 128), jnp.float32)
        _lenS = 256 - jax.random.randint(jax.random.fold_in(_rk, 7), (16,), 0, max(1, 256 // 4) + 1, jnp.int32)
        _lenS2 = 64 - jax.random.randint(jax.random.fold_in(_rk, 8), (16,), 0, max(1, 64 // 4) + 1, jnp.int32)
        _ctx_512P = jax.random.normal(jax.random.fold_in(_rk, 11), (16, 16, 64), jnp.float32)
        _ctx_512c = jax.random.dirichlet(jax.random.fold_in(_rk, 511), 0.3 * jnp.ones((16,), jnp.float32), (16, 64))
        _ctx_512t = jnp.einsum('bsk,bkd->bsd', _ctx_512c, _ctx_512P)
        _ctx_512t = _ctx_512t * jax.lax.rsqrt(jnp.mean(jnp.square(_ctx_512t)) + 1e-12) * 0.953939
        ctx_512 = 0.00222621 + 0.99962 * (_ctx_512t + 0.3 * jax.random.normal(jax.random.fold_in(_rk, 611), (16, 64, 64), jnp.float32))
        return (x, ctx_512)
    x, ctx_512 = _rec_inputs()

    def _L0_xattn_setup():
        import jax, jax.numpy as jnp
        import numpy as np
        B, T, TC, C, CC, H = (2, 256, 64, 128, 64, 16)
        D = C // H

        def _heads(t):
            b, l, _ = t.shape
            return t.reshape(b, l, H, D).transpose(0, 2, 1, 3)
        key = jax.random.key(seed)
        ks = jax.random.split(key, 18)
        w = lambda k, i, o: jax.random.normal(k, (i, o), jnp.float32) / np.sqrt(i).astype(np.float32)
        return {'x': jax.random.normal(ks[0], (B, T, C), jnp.float32), 'cross_input': jax.random.normal(ks[1], (B, TC, CC), jnp.float32), 'Wk': w(ks[2], C, C), 'bk': jnp.zeros((C,), jnp.float32), 'Wq': w(ks[3], C, C), 'bq': jnp.zeros((C,), jnp.float32), 'Wv': w(ks[4], C, C), 'bv': jnp.zeros((C,), jnp.float32), 'Wck': w(ks[5], CC, C), 'bck': jnp.zeros((C,), jnp.float32), 'Wcq': w(ks[6], C, C), 'bcq': jnp.zeros((C,), jnp.float32), 'Wcv': w(ks[7], CC, C), 'bcv': jnp.zeros((C,), jnp.float32), 'Wp': w(ks[8], C, C), 'bp': jnp.zeros((C,), jnp.float32)}
    _L0_xattn_all = _L0_xattn_setup()
    _L0_xattn_in = {k: v for k, v in _L0_xattn_all.items() if k in ('Wk', 'bk', 'Wq', 'bq', 'Wv', 'bv', 'Wck', 'bck', 'Wcq', 'bcq', 'Wcv', 'bcv', 'Wp', 'bp')}
    del _L0_xattn_all

    def _L0_ffn_setup():
        import jax, jax.numpy as jnp
        import numpy as np
        TOP_K = 2
        key = jax.random.key(seed)
        ks = jax.random.split(key, 6)
        B, S, D, E = (8, 512, 128, 8)
        s = 1.0 / np.sqrt(D)
        return {'x': jax.random.normal(ks[0], (B, S, D), dtype=jnp.float32), 'Wr': jax.random.normal(ks[1], (D, E), dtype=jnp.float32) * s, 'br': jnp.zeros((E,), dtype=jnp.float32), 'W1': jax.random.normal(ks[2], (E, D, D), dtype=jnp.float32) * s, 'b1': jnp.zeros((E, D), dtype=jnp.float32), 'W2': jax.random.normal(ks[3], (E, D, D), dtype=jnp.float32) * s, 'b2': jnp.zeros((E, D), dtype=jnp.float32)}
    _L0_ffn_all = _L0_ffn_setup()
    _L0_ffn_in = {k: v for k, v in _L0_ffn_all.items() if k in ('Wr', 'br', 'W1', 'b1', 'W2', 'b2')}
    del _L0_ffn_all

    def _L1_xattn_setup():
        import jax, jax.numpy as jnp
        import numpy as np
        B, LQ, LK = (8, 256, 256)
        QD, KD, VD = (128, 64, 64)
        key = jax.random.key(seed)
        ks = jax.random.split(key, 9)
        s = 0.02
        return {'query': jax.random.normal(ks[0], (B, LQ, QD), jnp.float32), 'key': jax.random.normal(ks[1], (B, LK, KD), jnp.float32), 'value': jax.random.normal(ks[2], (B, LK, VD), jnp.float32), 'Wq': jax.random.normal(ks[3], (QD, QD), jnp.float32) * s, 'bq': jnp.zeros((QD,), jnp.float32), 'Wk': jax.random.normal(ks[4], (KD, QD), jnp.float32) * s, 'bk': jnp.zeros((QD,), jnp.float32), 'Wv': jax.random.normal(ks[5], (VD, QD), jnp.float32) * s, 'bv': jnp.zeros((QD,), jnp.float32)}
    _L1_xattn_all = _L1_xattn_setup()
    _L1_xattn_in = {k: v for k, v in _L1_xattn_all.items() if k in ('Wq', 'bq', 'Wk', 'bk', 'Wv', 'bv')}
    del _L1_xattn_all

    def _L1_ffn_setup():
        import jax, jax.numpy as jnp
        import numpy as np
        TOP_K = 2
        CAP_FACTOR = 1.25

        def _gelu(x):
            return 0.5 * x * (1.0 + jnp.tanh(jnp.sqrt(2.0 / jnp.pi) * (x + 0.044715 * x ** 3)))
        key = jax.random.key(seed)
        ks = jax.random.split(key, 6)
        B, S, D, F, E = (4, 256, 128, 512, 8)
        return {'hidden_states': jax.random.normal(ks[0], (B, S, D), dtype=jnp.float32), 'wr': jax.random.normal(ks[1], (E, D), dtype=jnp.float32) * 0.02, 'w1': jax.random.normal(ks[2], (E, D, F), dtype=jnp.float32) * 0.02, 'b1': jnp.zeros((E, F), dtype=jnp.float32), 'w2': jax.random.normal(ks[3], (E, F, D), dtype=jnp.float32) * 0.02, 'b2': jnp.zeros((E, D), dtype=jnp.float32)}
    _L1_ffn_all = _L1_ffn_setup()
    _L1_ffn_in = {k: v for k, v in _L1_ffn_all.items() if k in ('wr', 'w1', 'b1', 'w2', 'b2')}
    del _L1_ffn_all
    return {'x': x, 'ctx_512': ctx_512, 'L0_xattn_Wk': _L0_xattn_in['Wk'], 'L0_xattn_bk': _L0_xattn_in['bk'], 'L0_xattn_Wq': _L0_xattn_in['Wq'], 'L0_xattn_bq': _L0_xattn_in['bq'], 'L0_xattn_Wv': _L0_xattn_in['Wv'], 'L0_xattn_bv': _L0_xattn_in['bv'], 'L0_xattn_Wck': _L0_xattn_in['Wck'], 'L0_xattn_bck': _L0_xattn_in['bck'], 'L0_xattn_Wcq': _L0_xattn_in['Wcq'], 'L0_xattn_bcq': _L0_xattn_in['bcq'], 'L0_xattn_Wcv': _L0_xattn_in['Wcv'], 'L0_xattn_bcv': _L0_xattn_in['bcv'], 'L0_xattn_Wp': _L0_xattn_in['Wp'], 'L0_xattn_bp': _L0_xattn_in['bp'], 'L0_ffn_Wr': _L0_ffn_in['Wr'], 'L0_ffn_br': _L0_ffn_in['br'], 'L0_ffn_W1': _L0_ffn_in['W1'], 'L0_ffn_b1': _L0_ffn_in['b1'], 'L0_ffn_W2': _L0_ffn_in['W2'], 'L0_ffn_b2': _L0_ffn_in['b2'], 'L1_xattn_Wq': _L1_xattn_in['Wq'], 'L1_xattn_bq': _L1_xattn_in['bq'], 'L1_xattn_Wk': _L1_xattn_in['Wk'], 'L1_xattn_bk': _L1_xattn_in['bk'], 'L1_xattn_Wv': _L1_xattn_in['Wv'], 'L1_xattn_bv': _L1_xattn_in['bv'], 'L1_ffn_wr': _L1_ffn_in['wr'], 'L1_ffn_w1': _L1_ffn_in['w1'], 'L1_ffn_b1': _L1_ffn_in['b1'], 'L1_ffn_w2': _L1_ffn_in['w2'], 'L1_ffn_b2': _L1_ffn_in['b2']}

def reference(x, ctx_512, L0_xattn_Wk, L0_xattn_bk, L0_xattn_Wq, L0_xattn_bq, L0_xattn_Wv, L0_xattn_bv, L0_xattn_Wck, L0_xattn_bck, L0_xattn_Wcq, L0_xattn_bcq, L0_xattn_Wcv, L0_xattn_bcv, L0_xattn_Wp, L0_xattn_bp, L0_ffn_Wr, L0_ffn_br, L0_ffn_W1, L0_ffn_b1, L0_ffn_W2, L0_ffn_b2, L1_xattn_Wq, L1_xattn_bq, L1_xattn_Wk, L1_xattn_bk, L1_xattn_Wv, L1_xattn_bv, L1_ffn_wr, L1_ffn_w1, L1_ffn_b1, L1_ffn_w2, L1_ffn_b2):
    import jax
    import jax.numpy as jnp

    def _L0_xattn_ref(x, cross_input, Wk, bk, Wq, bq, Wv, bv, Wck, bck, Wcq, bcq, Wcv, bcv, Wp, bp):
        import jax, jax.numpy as jnp
        import numpy as np
        B, T, TC, C, CC, H = (2, 256, 64, 128, 64, 16)
        D = C // H

        def _heads(t):
            b, l, _ = t.shape
            return t.reshape(b, l, H, D).transpose(0, 2, 1, 3)
        scale = np.float32(1.0 / np.sqrt(D))
        q = _heads(x @ Wq + bq)
        k = _heads(x @ Wk + bk)
        v = _heads(x @ Wv + bv)
        att = jnp.einsum('bhqd,bhkd->bhqk', q, k) * scale
        causal = jnp.tril(jnp.ones((T, T), bool))
        att = jnp.where(causal[None, None], att, -jnp.inf)
        y = jnp.einsum('bhqk,bhkd->bhqd', jax.nn.softmax(att, axis=-1), v)
        qc = _heads(x @ Wcq + bcq)
        kc = _heads(cross_input @ Wck + bck)
        vc = _heads(cross_input @ Wcv + bcv)
        attc = jnp.einsum('bhqd,bhkd->bhqk', qc, kc) * scale
        y = y + jnp.einsum('bhqk,bhkd->bhqd', jax.nn.softmax(attc, axis=-1), vc)
        y = y.transpose(0, 2, 1, 3).reshape(x.shape[0], T, C)
        return y @ Wp + bp

    def _L0_ffn_ref(x, Wr, br, W1, b1, W2, b2):
        import jax, jax.numpy as jnp
        import numpy as np
        TOP_K = 2
        k = TOP_K
        scores0 = x[:, 0, :] @ Wr + br
        _, idx = jax.lax.top_k(scores0, k)
        W1g, b1g = (W1[idx], b1[idx])
        W2g, b2g = (W2[idx], b2[idx])
        h = jnp.einsum('bsd,bkde->bkse', x, W1g) + b1g[:, :, None, :]
        h = jax.nn.gelu(h, approximate=False)
        o = jnp.einsum('bkse,bkef->bksf', h, W2g) + b2g[:, :, None, :]
        return jnp.sum(o, axis=1) / k

    def _L1_xattn_ref(query, key, value, Wq, bq, Wk, bk, Wv, bv):
        import jax, jax.numpy as jnp
        import numpy as np
        B, LQ, LK = (8, 256, 256)
        QD, KD, VD = (128, 64, 64)
        q = jnp.einsum('bld,de->ble', query, Wq) + bq
        k = jnp.einsum('bld,de->ble', key, Wk) + bk
        v = jnp.einsum('bld,de->ble', value, Wv) + bv
        scores = jnp.einsum('bqe,bke->bqk', q, k)
        attn = jax.nn.softmax(scores, axis=-1)
        out = jnp.einsum('bqk,bke->bqe', attn, v)
        return out

    def _L1_ffn_ref(hidden_states, wr, w1, b1, w2, b2):
        import jax, jax.numpy as jnp
        import numpy as np
        TOP_K = 2
        CAP_FACTOR = 1.25

        def _gelu(x):
            return 0.5 * x * (1.0 + jnp.tanh(jnp.sqrt(2.0 / jnp.pi) * (x + 0.044715 * x ** 3)))
        B, S, D = hidden_states.shape
        E = wr.shape[0]
        x = hidden_states.reshape(-1, D)
        T = x.shape[0]
        logits = x @ wr.T
        vals, idx = jax.lax.top_k(logits, TOP_K)
        sparse = jnp.full((T, E), -jnp.inf, dtype=logits.dtype)
        sparse = sparse.at[jnp.arange(T)[:, None], idx].set(vals)
        gating = jax.nn.softmax(sparse, axis=-1)
        cap = max(8, int(max(1, T * TOP_K // E) * CAP_FACTOR))
        mask = (idx[:, :, None] == jnp.arange(E)).any(axis=1)
        pos = jnp.cumsum(mask.astype(jnp.int32), axis=0) - 1
        keep = mask & (pos < cap)
        slot = jnp.where(keep, pos, cap)
        e_grid = jnp.broadcast_to(jnp.arange(E)[None, :], (T, E))
        t_grid = jnp.broadcast_to(jnp.arange(T)[:, None], (T, E))
        dispatch = jnp.full((E, cap + 1), T, dtype=jnp.int32)
        dispatch = dispatch.at[e_grid, slot].set(t_grid)[:, :cap]
        x_pad = jnp.concatenate([x, jnp.zeros((1, D), x.dtype)], axis=0)
        g_pad = jnp.concatenate([gating, jnp.zeros((1, E), gating.dtype)], axis=0)
        xg = x_pad[dispatch]
        h = _gelu(jnp.einsum('ecd,edf->ecf', xg, w1) + b1[:, None, :])
        y = jnp.einsum('ecf,efd->ecd', h, w2) + b2[:, None, :]
        g = g_pad[dispatch, jnp.arange(E)[:, None]]
        wy = y * g[..., None]
        out = jax.ops.segment_sum(wy.reshape(-1, D), dispatch.reshape(-1), num_segments=T + 1)[:T]
        return out.reshape(B, S, D)
    x = x + _L0_xattn_ref(_layernorm(x, axis=-1), ctx_512, L0_xattn_Wk, L0_xattn_bk, L0_xattn_Wq, L0_xattn_bq, L0_xattn_Wv, L0_xattn_bv, L0_xattn_Wck, L0_xattn_bck, L0_xattn_Wcq, L0_xattn_bcq, L0_xattn_Wcv, L0_xattn_bcv, L0_xattn_Wp, L0_xattn_bp)
    x = x + _L0_ffn_ref(_layernorm(x, axis=-1), L0_ffn_Wr, L0_ffn_br, L0_ffn_W1, L0_ffn_b1, L0_ffn_W2, L0_ffn_b2)
    x = x + _L1_xattn_ref(_layernorm(x, axis=-1), ctx_512, ctx_512, L1_xattn_Wq, L1_xattn_bq, L1_xattn_Wk, L1_xattn_bk, L1_xattn_Wv, L1_xattn_bv)
    x = x + _L1_ffn_ref(_layernorm(x, axis=-1), L1_ffn_wr, L1_ffn_w1, L1_ffn_b1, L1_ffn_w2, L1_ffn_b2)
    return x

_drawn_inputs = setup_inputs


def setup_inputs(seed=0):
    import zlib

    import numpy as np

    out = dict(_drawn_inputs(seed))
    spreads = {'L0_xattn_bk': (0.0, 0.8),
     'L0_xattn_bq': (0.0, 0.409),
     'L0_xattn_bv': (0.0, 0.1),
     'L0_xattn_bck': (0.0, 0.8),
     'L0_xattn_bcq': (0.0, 0.1),
     'L0_xattn_bcv': (0.0, 0.1),
     'L0_xattn_bp': (0.0, 0.1),
     'L0_ffn_br': (0.0, 0.1),
     'L0_ffn_b1': (0.0, 0.1),
     'L0_ffn_b2': (0.0, 0.1),
     'L1_xattn_bq': (0.0, 0.8),
     'L1_xattn_bk': (0.0, 0.8),
     'L1_xattn_bv': (0.0, 0.1),
     'L1_ffn_b1': (0.0, 0.603),
     'L1_ffn_b2': (0.0, 0.1)}
    factors = {'L1_xattn_Wq': 4.23, 'L1_xattn_Wk': 4.084}
    for name, (base, spread) in spreads.items():
        noise = np.random.default_rng([zlib.crc32(name.encode()), seed]).standard_normal(out[name].shape)
        drawn = base * np.exp(spread * noise) if base else spread * noise
        out[name] = jnp.asarray(drawn.astype(out[name].dtype))
    for name, factor in factors.items():
        out[name] = (out[name] * factor).astype(out[name].dtype)
    return out
```

```python
from contextlib import ExitStack

import numpy as np
import concourse.bass as bass
from concourse import mybir

ALU = mybir.AluOpType
ACT = mybir.ActivationFunctionType
AX = mybir.AxisListType
F32 = mybir.dt.float32
F32R = mybir.dt.float32r
BF16 = mybir.dt.bfloat16
U32 = mybir.dt.uint32

P = 128
NB = 16
T = 256
TC = 64
CC = 64
H0 = 16
HD = 8
NG = 4
HG = 4
GC = HG * HD
NSTACK = 3 * GC
NROW = NSTACK + HG
SCALE = float(np.float32(1.0 / np.sqrt(HD)))
EPS = 1e-5
NEG = -1e30
RING = 3



def steps(g, prev, nxt, nxt2):
    ahead = g < 2 or nxt
    u = []
    if ahead:
        u += ["S0", "S1"]
    if g == 3 and prev:
        u += ["O"]
    if g < 3 or nxt:
        u += ["M"]
    if nxt:
        u += ["K"]
    if ahead:
        u += ["S2"]
    if nxt:
        u += ["Q"]
    if ahead:
        u += ["S3"]
    if nxt:
        u += ["C"]
    if g == 0 and nxt:
        u += ["V0"]
    if g == 1:
        u += (["T1"] if prev else []) + (["V1"] if nxt else [])
    if g == 2:
        u += (["YT"] if prev else []) + (["X"] if nxt2 else [])
    if g == 3:
        u += ["T0"]
    return u


START = ([("CT", 0), ("CT", 1), ("X", 0), ("V0", 0), ("V1", 0)] + [("KC", i) for i in range(8)]
         + [(k, g) for g in range(NG) for k in "KQC"] + [("VC", i) for i in range(4)] + [("X", 1)]
         + [(f"S{j}", n) for n in range(2) for j in range(4)] + [("M", 0)])
LOOPED = NB - 3


def ring_plan():
    parts = [("start", START)]
    for part, prev, nxt, nxt2 in (("first", 0, 1, 1), ("loop", 1, 1, 1), ("before last", 1, 1, 0), ("last", 1, 0, 0)):
        parts.append((part, [(u, g) for g in range(NG) for u in steps(g, prev, nxt, nxt2)]))
    parts.append(("end", [("T1", 0), ("YT", 0), ("O", 0)]))
    where, at = {}, 0
    for part, uses in parts:
        where[part] = {u: at + i for i, u in enumerate(uses)}
        at += len(uses) * (LOOPED if part == "loop" else 1)
    return where


WHERE = ring_plan()
PER_SEQ = len(WHERE["loop"])
assert PER_SEQ % RING == 0
BEFORE = {"first": "start", "loop": "loop", "before last": "loop", "last": "before last"}


class Seq:

    def __init__(self, b, part, prev=True, nxt=True, nxt2=True, slot=0):
        self.b, self.part, self.slot = b, part, slot
        self.prev, self.nxt, self.nxt2 = prev, nxt, nxt2

    def at(self, position):
        before = position // RING
        if self.part == "loop":
            before = before + (self.b - 1) * (PER_SEQ // RING)
        return position % RING, before

    def ring(self, name, g):
        return self.at(WHERE[self.part][(name, g)])

    def maxima(self, g):
        if g:
            return self.ring("M", g - 1)
        last = WHERE[BEFORE[self.part]]
        back = len(last) - list(last).index(("M", 0 if self.part == "first" else 3))
        return self.at(min(WHERE[self.part].values()) - back)


def sequences(eng, body):
    body(Seq(0, "first", prev=False, slot=0))
    with eng.Fori(1, NB - 3, 2) as i:
        body(Seq(i, "loop", slot=1))
        body(Seq(i + 1, "loop", slot=0))
    body(Seq(NB - 3, "loop", slot=1))
    body(Seq(NB - 2, "before last", nxt2=False, slot=0))
    body(Seq(NB - 1, "last", nxt=False, nxt2=False, slot=1))


def attention0(nc, io, X, ident, identb):
    st = ExitStack()

    def sb(name, shape, dt=F32):
        return st.enter_context(nc.sbuf_tensor(name, shape, dt))

    def sem(name):
        return st.enter_context(nc.semaphore(name))

    with st:
        ones = sb("ones", [P, P])
        causal = sb("causal", [P, HG, P], BF16)
        stats = sb("stats", [P, 2 * NB, 6])
        mv = sb("mv", [P, 2 * NB, 2])
        rstd = sb("rstd", [P, 2 * NB])
        power = sb("power", [P, 2 * NB])
        half = sb("half", [P, 2 * NB])
        shift = sb("shift", [P, 2 * NB])
        XN = sb("XN", [P, 2, 2, P])
        W = {k: sb("w" + k, [P, P]) for k in ("K", "Q", "C", "V", "P")}
        WC = {k: sb("wc" + k, [CC, P]) for k in ("K", "V")}
        WS = {k: sb("ws" + k, [P, 2, NG, 3, GC], F32R) for k in ("K", "Q", "C")}
        WCS = sb("wcs", [CC, 2, NG, 3, GC], F32R)
        WV = sb("wv", [P, 2, P], F32R)
        BS = {k: sb("bs" + k, [NSTACK, NG]) for k in ("K", "Q", "C", "KC")}
        BL = {k: sb("bl" + k, [NSTACK, NG]) for k in ("K", "Q", "C", "KC")}
        lowk = sb("lowk", [NSTACK, 1])
        lowq = sb("lowq", [NSTACK, 1])
        headrow = sb("headrow", [P, HG])
        bvb = sb("bvb", [P, P])
        bcvb = sb("bcvb", [P, P])
        bpb = sb("bpb", [P, 2, P])
        ctxs = sb("ctxs", [P, 8, CC])
        CT = sb("CT", [CC, NB * TC])
        CTR = sb("CTR", [CC, 2, NB * TC], F32R)
        KC = sb("KC", [NSTACK, NG, NB * TC], F32R)
        VCA = sb("VCA", [P, NB, P])
        XR = sb("XR", [P, 2, 2, T], F32R)
        LO = sb("LO", [NSTACK, 4, T], F32R)
        KS = sb("KS", [NSTACK, 2, T], F32R)
        KM = sb("KM", [NROW, 2 * NG, HG, T], F32R)
        KCM = sb("KCM", [NROW, 2, NG, HG, TC], F32R)
        QC = sb("QC", [NROW, 2 * NG, 2, T], F32R)
        VS = sb("VS", [P, 2, 2, H0, 4 * HD])
        VC = sb("VC", [P, 2, H0 // 2, 8 * HD])
        MG = sb("MG", [P, 2, 4, NROW])
        PT = sb("PT", [P, 2, 2048])
        NV = sb("NV", [P, 2, 512])
        RD = sb("RD", [P, 4, HG, 2])
        YN = sb("YN", [P, 4, 2, HG, HD])
        Y = sb("Y", [P, 2, P])
        YT = sb("YT", [P, T])

        ps_ring = [st.enter_context(nc.psum_tensor(f"ring{i}", [P, 512], F32)) for i in range(RING)]
        ps_pv = st.enter_context(nc.psum_tensor("ps_pv", [P, 512], F32))
        ps_st = st.enter_context(nc.psum_tensor("ps_st", [P, 2048], F32))

        ld_x = [sem(f"ld_x{i}") for i in range(4)]
        ld_w, ld_b, ld_s, ld_c = sem("ld_w"), sem("ld_b"), sem("ld_s"), sem("ld_c")
        ring_full = [sem(f"ring_full{i}") for i in range(RING)]
        ring_free = [sem(f"ring_free{i}") for i in range(RING)]
        zeros_set, consts_set = sem("zeros_set"), sem("consts_set")
        low_masks_set, weights_set = sem("low_masks_set"), sem("weights_set")
        waited = sem("waited")
        stats_set, var_set, rstd_set, shift_set = sem("stats_set"), sem("var_set"), sem("rstd_set"), sem("shift_set")
        chain = sem("chain")
        xn_set, xb_set, xhigh_set, ctxt_set = sem("xn_set"), sem("xb_set"), sem("xhigh_set"), sem("ctxt_set")
        low_set, km_set, kcm_set, vc_set = sem("low_set"), sem("km_set"), sem("kcm_set"), sem("vc_set")
        max_set, rd_set, y_set = sem("max_set"), sem("rd_set"), sem("y_set")
        st_full, exp_done, sel_done, pv_done, nv_set = (
            sem("st_full"), sem("exp_done"), sem("sel_done"), sem("pv_done"), sem("nv_set"))

        block = st.enter_context(nc.Block())
        start = Seq(0, "start")
        end = Seq(NB, "end")

        def wait_full(eng, s, name, g):
            bank, before = s.ring(name, g)
            eng.wait_ge(ring_full[bank], before + 1)
            return ps_ring[bank], ring_free[bank]

        def wait_drained(eng, s, name, g):
            bank, before = s.ring(name, g)
            eng.wait_ge(ring_free[bank], before + 1)

        def pair(b):
            return X[:, bass.ds(2 * b, 2), :]

        @block.sync
        def _(sp):
            xv = io["x"].rearrange("b (t p) c -> p (b t) c", p=P)
            for q in range(4):
                sp.dma_start(X[:, 8 * q:8 * q + 8, :], xv[:, 8 * q:8 * q + 8, :]).then_inc(ld_x[q], 16)
            sp.dma_start(W["P"][:, :], io["L0_xattn_Wp"]).then_inc(ld_w, 16)

            def row(name):
                return io[name].rearrange("(a c) -> a c", a=1).to_broadcast([P, P])

            sp.dma_start(bvb[:, :], row("L0_xattn_bv")).then_inc(ld_b, 16)
            sp.dma_start(bcvb[:, :], row("L0_xattn_bcv")).then_inc(ld_b, 16)
            for t in range(2):
                sp.dma_start(bpb[:, t, :], row("L0_xattn_bp")).then_inc(ld_b, 16)

        @block.scalar
        def _(act):
            act.dma_start(ctxs[:, :, :], io["ctx_512"].rearrange("(o u) s c -> (u s) o c", u=2)).then_inc(ld_c, 16)
            for k, name in (("K", "Wk"), ("Q", "Wq"), ("C", "Wcq"), ("V", "Wv")):
                act.dma_start(W[k][:, :], io["L0_xattn_" + name]).then_inc(ld_w, 16)
            for k, name in (("K", "Wck"), ("V", "Wcv")):
                act.dma_start(WC[k][:, :], io["L0_xattn_" + name]).then_inc(ld_w, 16)
            act.preload_act_table(ACT.Exp)

            def low(s, kind, g):
                bank, _ = wait_full(act, s, kind, g)
                mask = lowk if kind == "K" else lowq
                nc.scalar.activation(LO[:, "KQC".index(kind), :], bank[0:NSTACK, 0:T], ACT.Identity,
                                     bias=BL[kind][:, g:g + 1], scale=mask[:, 0:1]).then_inc(low_set, 1)

            def x_high(s, g, slot):
                bank, _ = wait_full(act, s, "X", g)
                nc.scalar.copy(XR[:, slot, 0, :], bank[:, 0:T]).then_inc(xhigh_set, 1)

            def maxima(s, g, at):
                bank, free = wait_full(act, s, "M", g)
                nc.scalar.copy(QC[NSTACK:NROW, at, :, :].rearrange("p a t -> p (a t)"),
                               bank[NSTACK:NROW, :]).then_inc(free, 1)

            for i in range(2):
                bank, _ = wait_full(act, start, "CT", i)
                nc.scalar.copy(CT[:, 512 * i:512 * i + 512], bank[0:CC, :]).then_inc(ctxt_set, 1)
                nc.scalar.copy(CTR[:, 0, 512 * i:512 * i + 512], bank[0:CC, :]).then_inc(ctxt_set, 1)
            x_high(start, 0, 0)
            act.wait_ge(low_masks_set, 1)
            for i in range(8):
                bank, _ = wait_full(act, start, "KC", i)
                if i >= 2:
                    wait_drained(act, start, "KC", i - 2)
                at = 2 * (i % 2)
                nc.scalar.activation(LO[:, at:at + 2, :].rearrange("p a t -> p (a t)"), bank[0:NSTACK, :], ACT.Identity,
                                     bias=BL["KC"][:, i // 2:i // 2 + 1], scale=lowk[:, 0:1]).then_inc(low_set, 1)
            wait_drained(act, start, "KC", 7)
            for g in range(NG):
                for kind in "KQC":
                    if g:
                        wait_drained(act, start, kind, g - 1)
                    low(start, kind, g)
            x_high(start, 1, 1)
            maxima(start, 0, 0)

            def body(s):
                for g in range(NG):
                    n = 4 * s.b + g
                    for h in range(2):
                        act.wait_ge(st_full, 2 * n + h + 1)
                        nc.scalar.activation(PT[:, g % 2, 1024 * h:1024 * h + 1024], ps_st[:, 1024 * h:1024 * h + 1024],
                                             ACT.Exp, scale=SCALE).then_inc(exp_done, 1)
                    if g == 2 or (g == 0 and s.prev):
                        act.wait_ge(pv_done, n)
                        nc.scalar.copy(NV[:, 1 - g // 2, :], ps_pv[:, :]).then_inc(nv_set, 1)
                    if g < 3 or s.nxt:
                        maxima(s, g, (4 * s.slot + g + 1) % 8)
                    if s.nxt:
                        for kind in "KQC":
                            low(s, kind, g)
                    if g == 2 and s.prev:
                        bank, free = wait_full(act, s, "YT", g)
                        nc.scalar.copy(YT[:, :], bank[:, 0:T]).then_inc(free, 1)
                    if g == 2 and s.nxt2:
                        x_high(s, g, s.slot)

            sequences(act, body)
            act.wait_ge(pv_done, 4 * NB)
            nc.scalar.copy(NV[:, 1, :], ps_pv[:, :]).then_inc(nv_set, 1)
            bank, free = wait_full(act, end, "YT", 0)
            nc.scalar.copy(YT[:, :], bank[:, 0:T]).then_inc(free, 1)

        @block.gpsimd
        def _(pool):
            with nc.allow_non_contiguous_dma(reason="biases onto the stacks' rows"):
                for k, name in (("K", "bk"), ("Q", "bq"), ("C", "bcq"), ("KC", "bck")):
                    for j in range(3):
                        pool.dma_start(BS[k][GC * j:GC * j + GC, :],
                                       io["L0_xattn_" + name].rearrange("(g c) -> c g", g=NG)).then_inc(ld_s, 16)
            nc.gpsimd.memset(ones[:, :], 1.0).then_inc(zeros_set, 1)
            nc.gpsimd.memset(causal[:, :, :], 0.0).then_inc(zeros_set, 1)
            pool.wait_ge(zeros_set, 2)
            nc.gpsimd.affine_select(out=ident[:, :], in_=ones[:, :], compare_op=ALU.is_equal, fill=0.0, base=0,
                                    pattern=[[-1, P]], channel_multiplier=1).then_inc(consts_set, 1)
            nc.gpsimd.affine_select(out=causal[:, :, :], in_=causal[:, :, :], compare_op=ALU.is_ge, fill=NEG, base=0,
                                    pattern=[[0, HG], [-1, P]], channel_multiplier=1).then_inc(consts_set, 1)
            nc.gpsimd.memset(power[:, :], -0.5)
            nc.gpsimd.memset(MG[:, :, :, :], 0.0).then_inc(zeros_set, 1)
            nc.gpsimd.memset(VS[:, :, :, :, :], 0.0).then_inc(zeros_set, 1)
            nc.gpsimd.memset(VC[:, :, :, :], 0.0).then_inc(zeros_set, 1)
            pool.wait_ge(zeros_set, 5)
            pool.wait_ge(stats_set, 1)
            nc.gpsimd.tensor_scalar(rstd[:, :], mv[:, :, 1], EPS, 1.0, ALU.add, ALU.mult).then_inc(var_set, 1)
            pool.wait_ge(var_set, 1)
            nc.gpsimd.tensor_tensor(rstd[:, :], rstd[:, :], power[:, :], ALU.pow).then_inc(rstd_set, 1)
            def wait(semaphore, value):
                pool.wait_ge(semaphore, value)
                if not isinstance(value, int):
                    pool.sem_inc(waited, 1)

            def normalise(b, slot):
                at = bass.ds(2 * b, 2)
                nc.gpsimd.tensor_tensor(XN[:, slot, :, :], pair(b), rstd[:, at].unsqueeze(2).to_broadcast([P, 2, P]),
                                        ALU.mult).then_inc(xn_set, 1)
                wait(xn_set, 2 * b + 1)
                nc.gpsimd.tensor_tensor(XN[:, slot, :, :], XN[:, slot, :, :],
                                        shift[:, at].unsqueeze(2).to_broadcast([P, 2, P]), ALU.add).then_inc(xn_set, 1)
                nc.gpsimd.tensor_tensor(pair(b), pair(b), bpb[:, :, :], ALU.add).then_inc(xb_set, 1)

            def keys_by_head(s, g, n, at):
                bank, before = s.ring("K", g)
                wait(ring_free[bank], before + 1)
                for r in range(HG):
                    nc.gpsimd.tensor_scalar(KM[0:NSTACK, at, r, :], KS[:, g % 2, :], headrow[0:NSTACK, r:r + 1], 1.0,
                                            ALU.mult, ALU.mult).then_inc(km_set, 1)

            def context_keys(b, slot):
                for r in range(HG):
                    own = headrow[0:NSTACK, r:r + 1].unsqueeze(2).to_broadcast([NSTACK, NG, TC])
                    nc.gpsimd.tensor_tensor(KCM[0:NSTACK, slot, :, r, :], KC[:, :, bass.ds(TC * b, TC)], own,
                                            ALU.mult).then_inc(kcm_set, 1)

            pool.wait_ge(shift_set, 1)
            for q in range(4):
                pool.wait_ge(ld_x[q], 16)
            pool.wait_ge(ld_b, 16 * 4)
            normalise(0, 0)
            normalise(1, 1)
            pool.wait_ge(low_masks_set, 2)
            for g in range(NG):
                keys_by_head(start, g, g, g)
            wait_drained(pool, start, "KC", 7)
            context_keys(0, 0)

            def body(s):
                for g in range(NG):
                    n = 4 * s.b + g
                    for h in range(2):
                        wait(exp_done, 2 * n + h + 1)
                        if h == 0:
                            diagonal = PT[:, g % 2, 0:1024].rearrange("p (r q) -> p r q", r=HG)[:, :, 0:P]
                        else:
                            diagonal = PT[:, g % 2, 1024:1536].rearrange("p (r q) -> p r q", r=HG)
                        nc.gpsimd.affine_select(out=diagonal, in_=diagonal, compare_op=ALU.is_ge, fill=0.0, base=0,
                                                pattern=[[0, HG], [1, P]], channel_multiplier=-1).then_inc(sel_done, 1)
                    if s.nxt:
                        keys_by_head(s, g, n + 4, (4 * s.slot + g + 4) % 8)
                    if g == 0 and s.nxt:
                        context_keys(s.b + 1, 1 - s.slot)
                    if g == 0 and s.nxt2:
                        normalise(s.b + 2, s.slot)

            sequences(pool, body)

        @block.vector
        def _(dve):
            count = [0]

            def then(ins):
                count[0] += 1
                ins.then_inc(chain, 1)
                dve.wait_ge(chain, count[0])

            for q in range(4):
                dve.wait_ge(ld_x[q], 16)
                for t in range(8 * q, 8 * q + 8):
                    last = nc.vector.bn_stats(stats[:, t, :], X[:, t, :])
            then(last)
            for t in range(2 * NB):
                last = nc.vector.bn_aggr(mv[:, t, :], stats[:, t, :])
            last.then_inc(stats_set, 1)
            nc.vector.memset(lowk[:, :], 0.0)
            then(nc.vector.memset(lowq[:, :], 0.0))
            nc.vector.memset(lowk[GC:2 * GC, :], 1.0)
            then(nc.vector.memset(lowq[2 * GC:3 * GC, :], 1.0))
            dve.wait_ge(ld_b, 16 * 4)
            dve.wait_ge(ld_s, 16 * 12)
            for k in ("K", "Q", "C", "KC"):
                mask = lowk if k in ("K", "KC") else lowq
                last = nc.vector.tensor_scalar(BL[k][:, :], BS[k][:, :], mask[:, 0:1], None, ALU.mult)
            last.then_inc(low_masks_set, 1)
            dve.wait_ge(rstd_set, 1)
            nc.vector.scalar_tensor_tensor(out=shift[:, :], in0=mv[:, :, 0], scalar=-1.0, in1=rstd[:, :],
                                           op0=ALU.mult, op1=ALU.mult).then_inc(shift_set, 1)
            dve.wait_ge(consts_set, 2)
            dve.wait_ge(zeros_set, 5)
            for gp in range(2):
                v = VS[:, :, :, :, :].rearrange("p s k (a e r) c -> p (s k) a e r c", a=2, e=2)
                w = VC[:, :, :, :].rearrange("p s (a e u) c -> p s a e u c", a=2, e=2)
                for a in range(2):
                    nc.vector.memset(v[:, :, a, gp, :, 2 * HD + gp], 1.0)
                    nc.vector.memset(w[0:TC, :, a, gp, :, 2 * HD + gp], 1.0)
                    nc.vector.memset(w[TC:P, :, a, gp, :, 6 * HD + gp], 1.0)
            nc.vector.tensor_copy(identb[:, :], ident[:, :])
            nc.vector.tensor_reduce(headrow[:, :], ident[:, :].rearrange("p (j r d) -> p r j d", j=4, r=HG),
                                    AX.XY, ALU.add).then_inc(low_masks_set, 1)
            for r in range(HG):
                one = ident[NSTACK:NROW, NSTACK + r:NSTACK + r + 1].unsqueeze(2)
                nc.vector.tensor_copy(KM[NSTACK:NROW, :, r, :], one.to_broadcast([HG, 2 * NG, T]))
                nc.vector.tensor_copy(KCM[NSTACK:NROW, :, :, r, :].rearrange("p s g t -> p (s g) t"),
                                      one.to_broadcast([HG, 2 * NG, TC]))
            dve.wait_ge(ld_w, 16 * 7)
            stacks = [(WS[k], W[k], P) for k in ("K", "Q", "C")] + [(WCS, WC["K"], CC)]

            def copies(w, g, rows):
                return w[:, GC * g:GC * g + GC].unsqueeze(1).to_broadcast([rows, 3, GC])

            for ws, w, rows in stacks:
                for g in range(NG):
                    nc.vector.tensor_copy(ws[:, 0, g, :, :], copies(w, g, rows))
            then(nc.vector.tensor_copy(WV[:, 0, :], W["V"][:, :]))
            for ws, w, rows in stacks:
                for g in range(NG):
                    nc.vector.tensor_tensor(ws[:, 1, g, :, :], copies(w, g, rows), ws[:, 0, g, :, :], ALU.subtract)
            nc.vector.tensor_tensor(WV[:, 1, :], W["V"][:, :], WV[:, 0, :], ALU.subtract).then_inc(weights_set, 1)

            def x_low(s, g, b, slot):
                bank, free = wait_full(dve, s, "X", g)
                dve.wait_ge(xhigh_set, b + 1)
                nc.vector.tensor_tensor(XR[:, slot, 1, :], bank[:, 0:T], XR[:, slot, 0, :], ALU.subtract).then_inc(free, 1)

            def stack(s, kind, g, n, at):
                bank, free = wait_full(dve, s, kind, g)
                j = "KQC".index(kind)
                dve.wait_ge(low_set, 8 + 3 * n + j + 1)
                if kind == "K":
                    if not (isinstance(n, int) and n < 2):
                        dve.wait_ge(km_set, HG * (n - 1))
                    to = KS[:, g % 2, :]
                else:
                    to = QC[0:NSTACK, at, j - 1, :]
                nc.vector.scalar_tensor_tensor(out=to, in0=bank[0:NSTACK, 0:T], scalar=BS[kind][:, g:g + 1],
                                               in1=LO[:, j, :], op0=ALU.add, op1=ALU.subtract).then_inc(free, 1)

            def values(s, t, g, slot):
                bank, free = wait_full(dve, s, f"V{t}", g)
                v = bank[:, 0:P].rearrange("p (a e r d) -> p a e r d", a=2, e=2, r=HG)
                bias = bvb[:, :].rearrange("p (a e r d) -> p a e r d", a=2, e=2, r=HG)
                to = VS[:, slot, t, :, :].rearrange("p (a e r) c -> p a e r c", a=2, e=2)
                for gp in range(2):
                    last = nc.vector.tensor_tensor(to[:, :, gp, :, HD * gp:HD * gp + HD], v[:, :, gp], bias[:, :, gp], ALU.add)
                last.then_inc(free, 1)

            def context_values(b, slot):
                src = VCA[:, bass.ds(b, 1), :].rearrange("p s (a e u w d) -> p (s a) e u w d", a=2, e=2, u=2, w=2)
                to = VC[:, slot, :, :].rearrange("p (a e u) c -> p a e u c", a=2, e=2)
                for gp in range(2):
                    for w in range(2):
                        rows = slice(TC * w, TC * w + TC)
                        col = 4 * HD * w + HD * gp
                        last = nc.vector.tensor_copy(to[rows, :, gp, :, col:col + HD], src[rows, :, gp, :, w, :])
                last.then_inc(vc_set, 1)

            def maximum(s, j, g, at2):
                bank, free = wait_full(dve, s, f"S{j}", g)
                if j == 0:
                    src, to = bank[:, :].rearrange("p (r k) -> p r k", r=HG), MG[:, at2, 0, NSTACK:NROW]
                elif j < 3:
                    at = NSTACK + 2 * (j - 1)
                    src, to = bank[:, :].rearrange("p (r k) -> p r k", r=2), MG[:, at2, 1, at:at + 2]
                else:
                    src, to = (bank[:, :].rearrange("p (t r k) -> p t r k", t=2, r=HG), MG[:, at2, 2:4, NSTACK:NROW])
                nc.vector.tensor_reduce(to, src, AX.X, ALU.max, negate=True).then_inc(free, 1)

            def divide(s, a, g, b):
                bank, free = wait_full(dve, s, f"T{a}", g)
                v = bank[:, :].rearrange("p (k r w) -> p k r w", k=4, r=HG)
                nc.vector.reciprocal(RD[:, :, :, :], v[:, :, :, 2 * HD:2 * HD + 2]).then_inc(rd_set, 1)
                dve.wait_ge(rd_set, 2 * b + a + 1)
                for gp in range(2):
                    last = nc.vector.tensor_tensor(YN[:, :, gp, :, :], v[:, :, :, HD * gp:HD * gp + HD],
                                                   RD[:, :, :, gp:gp + 1].to_broadcast([P, 4, HG, HD]), ALU.mult)
                last.then_inc(free, 1)
                wait_drained(dve, s, f"T{a}", g)
                yn = YN[:, :, :, :, :].rearrange("p k e r d -> p k (e r d)")
                nc.vector.tensor_tensor(Y[:, :, 2 * GC * a:2 * GC * a + 2 * GC], yn[:, 0:2, :], yn[:, 2:4, :],
                                        ALU.add).then_inc(y_set, 1)

            def add_to_x(s, g, b):
                bank, free = wait_full(dve, s, "O", g)
                dve.wait_ge(xb_set, b + 1)
                nc.vector.tensor_tensor(pair(b), pair(b), bank[:, 0:T].rearrange("p (t c) -> p t c", t=2),
                                        ALU.add).then_inc(free, 1)

            dve.wait_ge(ctxt_set, 4)
            for i in range(2):
                bank, free = wait_full(dve, start, "CT", i)
                nc.vector.tensor_tensor(CTR[:, 1, 512 * i:512 * i + 512], bank[0:CC, :], CTR[:, 0, 512 * i:512 * i + 512],
                                        ALU.subtract).then_inc(free, 1)
            x_low(start, 0, 0, 0)
            values(start, 0, 0, 0)
            values(start, 1, 0, 0)
            for i in range(8):
                g, h = i // 2, i % 2
                bank, free = wait_full(dve, start, "KC", i)
                dve.wait_ge(low_set, i + 1)
                at = 2 * h
                nc.vector.scalar_tensor_tensor(out=KC[:, g, 512 * h:512 * h + 512], in0=bank[0:NSTACK, :],
                                               scalar=BS["KC"][:, g:g + 1],
                                               in1=LO[:, at:at + 2, :].rearrange("p a t -> p (a t)"),
                                               op0=ALU.add, op1=ALU.subtract).then_inc(free, 1)
            for g in range(NG):
                for kind in "KQC":
                    stack(start, kind, g, g, g)
            for i in range(4):
                bank, free = wait_full(dve, start, "VC", i)
                nc.vector.tensor_tensor(VCA[:, 4 * i:4 * i + 4, :], bank[:, :].rearrange("p (b c) -> p b c", b=4),
                                        bcvb[:, :].unsqueeze(1).to_broadcast([P, 4, P]), ALU.add).then_inc(free, 1)
            wait_drained(dve, start, "VC", 3)
            context_values(0, 0)
            x_low(start, 1, 1, 1)
            for n in range(2):
                for j in range(4):
                    maximum(start, j, n, n % 2)

            def body(s):
                for g in range(NG):
                    n = 4 * s.b + g
                    ahead = g < 2 or s.nxt
                    if ahead:
                        maximum(s, 0, g, g % 2)
                        maximum(s, 1, g, g % 2)
                    if g == 3 and s.prev:
                        add_to_x(s, g, s.b - 1)
                    at = (4 * s.slot + g + 4) % 8
                    if s.nxt:
                        stack(s, "K", g, n + 4, at)
                    if ahead:
                        maximum(s, 2, g, g % 2)
                    if s.nxt:
                        stack(s, "Q", g, n + 4, at)
                    if ahead:
                        maximum(s, 3, g, g % 2)
                    if s.nxt:
                        stack(s, "C", g, n + 4, at)
                    if g == 0 and s.nxt:
                        values(s, 0, g, 1 - s.slot)
                    if g == 1 and s.prev:
                        divide(s, 1, g, s.b - 1)
                    if g == 1 and s.nxt:
                        values(s, 1, g, 1 - s.slot)
                        context_values(s.b + 1, 1 - s.slot)
                    if g == 2 and s.nxt2:
                        x_low(s, g, s.b + 2, s.slot)
                    if g == 3:
                        divide(s, 0, g, s.b)

            sequences(dve, body)
            divide(end, 1, 0, NB - 1)
            add_to_x(end, 0, NB - 1)

        @block.tensor
        def _(pe):
            def take(s, name, g):
                bank, before = s.ring(name, g)
                if not (isinstance(before, int) and before == 0):
                    pe.wait_ge(ring_free[bank], before)
                return ps_ring[bank], ring_full[bank]

            def split(to, stationary, moving):
                for i, (a, b) in enumerate(((0, 0), (1, 0), (0, 1))):
                    last = nc.tensor.matmul(to, stationary(a), moving(b), start=(i == 0), stop=(i == 2))
                return last

            def transpose_x(s, g, b, slot):
                bank, full = take(s, "X", g)
                pe.wait_ge(xn_set, 2 * b + 2)
                for t in range(2):
                    last = nc.tensor.transpose(bank[:, P * t:P * t + P], XN[:, slot, t, :], ident[:, :])
                last.then_inc(full, 1)

            def project(s, kind, g, slot):
                bank, full = take(s, kind, g)
                split(bank[0:NSTACK, 0:T], lambda a: WS[kind][:, a, g, :, :].rearrange("p j c -> p (j c)"),
                      lambda b: XR[:, slot, b, :]).then_inc(full, 1)

            def project_values(s, t, g, slot):
                bank, full = take(s, f"V{t}", g)
                split(bank[:, 0:P], lambda a: XR[:, slot, a, P * t:P * t + P], lambda b: WV[:, b, :]).then_inc(full, 1)

            def scores_for_max(s, j, g, gn, n, slot, b):
                bank, full = take(s, f"S{j}", g)
                at = 4 * slot + gn
                if j == 0:
                    pe.wait_ge(km_set, HG * (n + 1))
                    nc.tensor.matmul(bank[:, :], QC[0:NSTACK, at, 0, 0:P], KM[0:NSTACK, at, :, 0:P], start=True, stop=False)
                    last = nc.tensor.matmul(bank[:, :], identb[:, :], causal[:, :, :], start=False, stop=True)
                elif j < 3:
                    r = 2 * (j - 1)
                    v = bank[:, :].rearrange("p (r k) -> p r k", r=2)
                    nc.tensor.matmul(v[:, :, P:T], identb[:, :], causal[:, 0:2, :], start=True, stop=False,
                                     skip_group_check=True)
                    last = nc.tensor.matmul(bank[:, :], QC[0:NSTACK, at, 0, P:T], KM[0:NSTACK, at, r:r + 2, :],
                                            start=False, stop=True, skip_group_check=True)
                else:
                    if gn == 0:
                        pe.wait_ge(kcm_set, HG * (b + 1))
                    for t in range(2):
                        last = nc.tensor.matmul(bank[:, T * t:T * t + T], QC[0:NSTACK, at, 1, P * t:P * t + P],
                                                KCM[0:NSTACK, slot, gn, :, :], start=True, stop=True)
                last.then_inc(full, 1)

            def transpose_max(s, g, n, at2):
                bank, full = take(s, "M", g)
                for k in range(4):
                    last = nc.tensor.transpose(bank[0:NROW, P * k:P * k + P], MG[:, at2, k, :], ident[:, :])
                last.then_inc(full, 1)

            def scores(s, g, h, n):
                at = 4 * s.slot + g
                if h == 0:
                    bank, before = s.maxima(g)
                    pe.wait_ge(ring_free[bank], before + 1)
                if not (isinstance(n, int) and n == 0):
                    pe.wait_ge(exp_done, 2 * n - 1 + h)
                if h == 0:
                    for r in range(HG):
                        last = nc.tensor.matmul(ps_st[:, T * r:T * r + T], KM[:, at, r, 0:P], QC[:, at, 0, :],
                                                start=True, stop=True)
                else:
                    for r in range(HG):
                        nc.tensor.matmul(ps_st[:, 1024 + P * r:1024 + P * r + P], KM[:, at, r, P:T], QC[:, at, 0, P:T],
                                         start=True, stop=True)
                    for u in range(2):
                        last = nc.tensor.matmul(ps_st[:, 1536 + T * u:1536 + T * u + T],
                                                KCM[:, s.slot, g, 2 * u:2 * u + 2, :].rearrange("p r t -> p (r t)"),
                                                QC[:, at, 1, :], start=True, stop=True)
                last.then_inc(st_full, 1)

            def sums(h, g, n, slot, pairs, b):
                pe.wait_ge(sel_done, 2 * n + h + 1)
                if h == 0:
                    if g % 2 == 0 and not (isinstance(pairs, int) and pairs == 0):
                        pe.wait_ge(nv_set, pairs)
                    for r in range(HG):
                        nc.tensor.matmul(ps_pv[GC * r:GC * r + GC, 0:T], VS[:, slot, 0, HG * g + r, :],
                                         PT[:, g % 2, T * r:T * r + T], start=(g % 2 == 0), stop=False,
                                         tile_position=(0, GC * r), skip_group_check=True)
                    return
                if g == 0:
                    pe.wait_ge(vc_set, b + 1)
                for r in range(HG):
                    nc.tensor.matmul(ps_pv[GC * r:GC * r + GC, P:T], VS[:, slot, 1, HG * g + r, :],
                                     PT[:, g % 2, 1024 + P * r:1024 + P * r + P], start=False, stop=(g % 2 == 1),
                                     tile_position=(0, GC * r), skip_group_check=True)
                for u in range(2):
                    last = nc.tensor.matmul(ps_pv[2 * GC * u:2 * GC * u + 2 * GC, T:2 * T], VC[:, slot, 2 * g + u, :],
                                            PT[:, g % 2, 1536 + T * u:1536 + T * u + T], start=False, stop=(g % 2 == 1),
                                            tile_position=(0, 2 * GC * u), skip_group_check=True)
                last.then_inc(pv_done, 1)

            def transpose_sums(s, a, g, b):
                bank, full = take(s, f"T{a}", g)
                pe.wait_ge(nv_set, 2 * b + a + 1)
                for k in range(4):
                    last = nc.tensor.transpose(bank[:, P * k:P * k + P], NV[:, a, P * k:P * k + P], ident[:, :])
                last.then_inc(full, 1)

            def transpose_y(s, g, b):
                bank, full = take(s, "YT", g)
                pe.wait_ge(y_set, 2 * b + 2)
                for t in range(2):
                    last = nc.tensor.transpose(bank[:, P * t:P * t + P], Y[:, t, :], ident[:, :])
                last.then_inc(full, 1)

            def project_out(s, g, gy):
                bank, full = take(s, "O", g)
                wait_drained(pe, s, "YT", gy)
                for t in range(2):
                    last = nc.tensor.matmul(bank[:, P * t:P * t + P], YT[:, P * t:P * t + P], W["P"][:, :],
                                            start=True, stop=True)
                last.then_inc(full, 1)

            pe.wait_ge(consts_set, 2)
            pe.wait_ge(ld_c, 16)
            for i in range(2):
                bank, full = take(start, "CT", i)
                for o in range(4):
                    last = nc.tensor.transpose(bank[0:CC, P * o:P * o + P], ctxs[:, 4 * i + o, :], ident[:, :])
                last.then_inc(full, 1)
            transpose_x(start, 0, 0, 0)
            pe.wait_ge(weights_set, 1)
            wait_drained(pe, start, "X", 0)
            project_values(start, 0, 0, 0)
            project_values(start, 1, 0, 0)
            for i in range(8):
                g, h = i // 2, i % 2
                bank, full = take(start, "KC", i)
                split(bank[0:NSTACK, :], lambda a: WCS[:, a, g, :, :].rearrange("p j c -> p (j c)"),
                      lambda b: CTR[:, b, 512 * h:512 * h + 512]).then_inc(full, 1)
            for g in range(NG):
                for kind in "KQC":
                    project(start, kind, g, 0)
            for i in range(4):
                bank, full = take(start, "VC", i)
                for o in range(4):
                    b = 4 * i + o
                    for w in range(2):
                        last = nc.tensor.matmul(bank[TC * w:TC * w + TC, P * o:P * o + P], CT[:, TC * b:TC * b + TC],
                                                WC["V"][:, :], start=True, stop=True)
                last.then_inc(full, 1)
            transpose_x(start, 1, 1, 1)
            for n in range(2):
                for j in range(4):
                    scores_for_max(start, j, n, n, n, 0, 0)
            wait_drained(pe, start, "S3", 0)
            transpose_max(start, 0, 0, 0)

            def body(s):
                for g in range(NG):
                    n = 4 * s.b + g
                    ahead = g < 2 or s.nxt
                    gn, sn, bn = (g + 2, s.slot, s.b) if g < 2 else (g - 2, 1 - s.slot, s.b + 1)
                    gp, sp_, bp = (g - 1, s.slot, s.b) if g else (3, 1 - s.slot, s.b - 1)
                    pairs = 2 * s.b + g // 2 if g else 2 * s.b
                    before = g or s.prev

                    def ahead_scores(j):
                        if ahead:
                            scores_for_max(s, j, g, gn, n + 2, sn, bn)

                    scores(s, g, 0, n)
                    ahead_scores(0)
                    if before:
                        sums(0, gp, n - 1, sp_, pairs, bp)
                    scores(s, g, 1, n)
                    ahead_scores(1)
                    if g == 3 and s.prev:
                        project_out(s, g, 2)
                    if before:
                        sums(1, gp, n - 1, sp_, pairs, bp)
                    if g < 3 or s.nxt:
                        pe.wait_ge(*max_wait(s, g))
                        transpose_max(s, g, n + 1, (g + 1) % 2)
                    if s.nxt:
                        project(s, "K", g, 1 - s.slot)
                    ahead_scores(2)
                    if s.nxt:
                        project(s, "Q", g, 1 - s.slot)
                    ahead_scores(3)
                    if s.nxt:
                        project(s, "C", g, 1 - s.slot)
                    if g == 0 and s.nxt:
                        project_values(s, 0, g, 1 - s.slot)
                    if g == 1 and s.prev:
                        transpose_sums(s, 1, g, s.b - 1)
                    if g == 1 and s.nxt:
                        project_values(s, 1, g, 1 - s.slot)
                    if g == 2 and s.prev:
                        transpose_y(s, g, s.b - 1)
                    if g == 2 and s.nxt2:
                        transpose_x(s, g, s.b + 2, s.slot)
                    if g == 3:
                        transpose_sums(s, 0, g, s.b)

            def max_wait(s, g):
                last = WHERE[BEFORE[s.part]] if g == 0 else WHERE[s.part]
                if g == 0:
                    back = len(last) - list(last).index(("S3", 1 if s.part == "first" else 3))
                    bank, before = s.at(min(WHERE[s.part].values()) - back)
                else:
                    bank, before = s.ring("S3", g - 1)
                return ring_free[bank], before + 1

            sequences(pe, body)
            sums(0, 3, 4 * NB - 1, 1, 2 * NB - 1, NB - 1)
            sums(1, 3, 4 * NB - 1, 1, 2 * NB - 1, NB - 1)
            transpose_sums(end, 1, 0, NB - 1)
            transpose_y(end, 0, NB - 1)
            project_out(end, 0, 0)


def wait(eng, semaphore, value):
    if not (isinstance(value, int) and value <= 0):
        eng.wait_ge(semaphore, value)


def pipeline(eng, count, depth, unroll, body):
    lo = -(-depth // unroll) * unroll
    hi = lo + (count - lo) // unroll * unroll
    for j in range(lo):
        body(j, j % unroll, lambda s, j=j: 0 <= j - s < count)
    with eng.Fori(lo, hi - unroll + 1, unroll) as i:
        for u in range(unroll):
            body(i + u, u, lambda s: True)
    for j in range(hi, count + depth):
        body(j, j % unroll, lambda s, j=j: 0 <= j - s < count)


class Norm:

    def __init__(self, nc, st, name):
        def sb(what, shape):
            return st.enter_context(nc.sbuf_tensor(f"{name}_{what}", shape, F32))

        def sem(what):
            return st.enter_context(nc.semaphore(f"{name}_{what}"))

        self.nc = nc
        self.stats, self.mv = sb("stats", [P, 2, 2, 6]), sb("mv", [P, 2, 2, 2])
        self.rstd, self.shift = sb("rstd", [P, 2, 2]), sb("shift", [P, 2, 2])
        self.power = sb("power", [P, 2])
        self.stats_set, self.mv_set, self.var_set = sem("stats_set"), sem("mv_set"), sem("var_set")
        self.rstd_set, self.shift_set, self.xn_set = sem("rstd_set"), sem("shift_set"), sem("xn_set")
        self.power_set = sem("power_set")
        self.waited = sem("waited")

    def wait(self, eng, semaphore, value):
        eng.wait_ge(semaphore, value)
        if not isinstance(value, int):
            eng.sem_inc(self.waited, 1)

    def statistics(self, dve, x, b, slot):
        nc = self.nc
        for t in range(2):
            last = nc.vector.bn_stats(self.stats[:, slot, t, :], x(t))
        last.then_inc(self.stats_set, 1)
        self.wait(dve, self.stats_set, b + 1)
        for t in range(2):
            last = nc.vector.bn_aggr(self.mv[:, slot, t, :], self.stats[:, slot, t, :])
        last.then_inc(self.mv_set, 1)
        dve.wait_ge(self.mv_set, b + 1)
        nc.vector.tensor_scalar(self.rstd[:, slot, :], self.mv[:, slot, :, 1], EPS, 1.0,
                                ALU.add, ALU.mult).then_inc(self.var_set, 1)

    def prepare(self, pool):
        self.nc.gpsimd.memset(self.power[:, :], -0.5).then_inc(self.power_set, 1)
        pool.wait_ge(self.power_set, 1)

    def root(self, pool, b, slot):
        self.wait(pool, self.var_set, b + 1)
        self.nc.gpsimd.tensor_tensor(self.rstd[:, slot, :], self.rstd[:, slot, :], self.power[:, :],
                                     ALU.pow).then_inc(self.rstd_set, 1)

    def normalise(self, dve, x, xn, b, slot, free):
        nc = self.nc
        dve.wait_ge(self.rstd_set, b + 1)
        nc.vector.scalar_tensor_tensor(self.shift[:, slot, :], self.mv[:, slot, :, 0], -1.0, self.rstd[:, slot, :],
                                       ALU.mult, ALU.mult).then_inc(self.shift_set, 1)
        wait(dve, *free)
        self.wait(dve, self.shift_set, b + 1)
        for t in range(2):
            last = nc.vector.tensor_scalar(xn(t), x(t), self.rstd[:, slot, t:t + 1], self.shift[:, slot, t:t + 1],
                                           ALU.mult, ALU.add)
        last.then_inc(self.xn_set, 1)


def ffn0(nc, io, X, XT, ident, zeros_to):
    st = ExitStack()
    WSLOTS = 4

    def sb(name, shape, dt=F32):
        return st.enter_context(nc.sbuf_tensor(name, shape, dt))

    def sem(name):
        return st.enter_context(nc.semaphore(name))

    with st:
        X2T = sb("X2T", [P, NB, T])
        XN = sb("f_xn", [P, 2, 2, P])
        Wr, brb = sb("f_wr", [P, 8]), sb("f_brb", [NB, 8])
        sc, top = sb("f_scores", [NB, 8]), sb("f_top", [NB, 8])
        chosen = sb("f_chosen", [NB, 8], U32)
        row = sb("f_row", [1, 2 * NB], U32)
        ones2 = sb("f_ones", [2, P])
        zeros = sb("f_zeros", [P, 10, P])
        W1, W2 = sb("f_w1", [P, WSLOTS, 2, P]), sb("f_w2", [P, WSLOTS, 2, P])
        b1, b2 = sb("f_b1", [P, WSLOTS, 2]), sb("f_b2", [2, WSLOTS, P])
        HT = sb("f_ht", [P, 2, 2, T])
        ps_tr = [st.enter_context(nc.psum_tensor(f"f_tr{i}", [P, 512], F32)) for i in range(2)]
        ps_h = [st.enter_context(nc.psum_tensor(f"f_h{i}", [P, 512], F32)) for i in range(2)]
        ps_o = [st.enter_context(nc.psum_tensor(f"f_o{i}", [P, 512], F32)) for i in range(2)]
        ps_r = st.enter_context(nc.psum_tensor("f_r", [P, 512], F32))

        ln2, ln3 = Norm(nc, st, "ln2"), Norm(nc, st, "ln3")
        ld_r, ones_set, zeros_set, zeros_out = sem("f_ld_r"), sem("f_ones_set"), sem("f_zeros_set"), sem("f_zeros_out")
        ld_w = [sem(f"f_ld_w{i}") for i in range(WSLOTS)]
        tr2_full, x2t_set, tr3_full, xt_set = sem("f_tr2_full"), sem("f_x2t_set"), sem("f_tr3_full"), sem("f_xt_set")
        r_full, sc_set, top_set, chosen_set, row_set = (
            sem("f_r_full"), sem("f_sc_set"), sem("f_top_set"), sem("f_chosen_set"), sem("f_row_set"))
        h_full, ht_set, o_full, added = sem("f_h_full"), sem("f_ht_set"), sem("f_o_full"), sem("f_added")
        block = st.enter_context(nc.Block())
        DEPTH = 3

        @block.sync
        def _(sp):
            sp.dma_start(Wr[:, :], io["L0_ffn_Wr"]).then_inc(ld_r, 16)
            sp.dma_start(brb[:, :], io["L0_ffn_br"].rearrange("(a c) -> a c", a=1).to_broadcast([NB, 8])).then_inc(ld_r, 16)
            sp.wait_ge(zeros_set, 1)
            for e in range(8):
                sp.dma_start(zeros_to[1280 * e:1280 * e + 1280, :].rearrange("(p t) c -> p t c", p=P),
                             zeros[:, :, :]).then_inc(zeros_out, 16)
            sp.wait_ge(chosen_set, 1)
            with nc.allow_non_contiguous_dma(reason="two of eight"):
                sp.dma_start(row[:, :], chosen[:, 0:2]).then_inc(row_set, 16)
            sp.wait_ge(row_set, 16)

            def body(j, place, on):
                wait(sp, o_full, j - WSLOTS + 1)
                for k in range(2):
                    e = sp.value_load(row[0:1, bass.ds(2 * j + k, 1)], min_val=0, max_val=7)
                    sp.dma_start(W1[:, place, k, :], io["L0_ffn_W1"][bass.ds(e, 1), :, :].rearrange("a c d -> (a c) d")).then_inc(ld_w[place], 16)
                    sp.dma_start(W2[:, place, k, :], io["L0_ffn_W2"][bass.ds(e, 1), :, :].rearrange("a c d -> (a c) d")).then_inc(ld_w[place], 16)
                    with nc.allow_non_contiguous_dma(reason="a bias onto the partitions"):
                        sp.dma_start(b1[:, place, k:k + 1], io["L0_ffn_b1"][bass.ds(e, 1), :].rearrange("a c -> c a")).then_inc(ld_w[place], 16)
                    sp.dma_start(b2[k:k + 1, place, :], io["L0_ffn_b2"][bass.ds(e, 1), :]).then_inc(ld_w[place], 16)

            for j in range(WSLOTS):
                body(j, j, None)
            with sp.Fori(WSLOTS, NB - WSLOTS + 1, WSLOTS) as i:
                for u in range(WSLOTS):
                    body(i + u, u, None)
            sp.wait_ge(zeros_out, 16 * 8)

        @block.gpsimd
        def _(pool):
            nc.gpsimd.memset(zeros[:, :, :], 0.0).then_inc(zeros_set, 1)
            nc.gpsimd.memset(ones2[:, :], 1.0).then_inc(ones_set, 1)
            ln2.prepare(pool)
            ln3.prepare(pool)
            pipeline(pool, NB, 0, 2, lambda b, place, on: ln2.root(pool, b, place))
            pipeline(pool, NB, 0, 2, lambda b, place, on: ln3.root(pool, b, place))

        @block.scalar
        def _(act):
            act.preload_act_table(ACT.Gelu)

            def normed(j, place, on):
                act.wait_ge(tr2_full, j + 1)
                nc.scalar.copy(X2T[:, bass.ds(j, 1), :].rearrange("p a t -> p (a t)"),
                               ps_tr[place % 2][:, 0:T]).then_inc(x2t_set, 1)

            pipeline(act, NB, 0, 2, normed)

            def body(j, place, on):
                if on(0):
                    act.wait_ge(h_full, j + 1)
                    wait(act, o_full, j - 1)
                    for k in range(2):
                        last = nc.scalar.activation(HT[:, place % 2, k, :], ps_h[place % 2][:, T * k:T * k + T], ACT.Gelu,
                                                    bias=b1[:, place, k:k + 1])
                    last.then_inc(ht_set, 1)
                if on(3):
                    b = j - 3
                    act.wait_ge(tr3_full, b + 1)
                    nc.scalar.copy(XT[:, bass.ds(b, 1), :].rearrange("p a t -> p (a t)"),
                                   ps_tr[(place + 1) % 2][:, 0:T]).then_inc(xt_set, 1)

            pipeline(act, NB, DEPTH, WSLOTS, body)

        @block.tensor
        def _(pe):
            def normed(j, place, on):
                pe.wait_ge(ln2.xn_set, j + 1)
                wait(pe, x2t_set, j - 1)
                for t in range(2):
                    last = nc.tensor.transpose(ps_tr[place][:, P * t:P * t + P], XN[:, place, t, :], ident[:, :])
                last.then_inc(tr2_full, 1)

            pipeline(pe, NB, 2, 2, lambda j, place, on: on(0) and normed(j, place, on))
            pe.wait_ge(x2t_set, NB)
            pe.wait_ge(ld_r, 32)
            nc.tensor.matmul(ps_r[0:NB, 0:8], X2T[:, :, 0], Wr[:, :], start=True, stop=True).then_inc(r_full, 1)
            pe.wait_ge(ones_set, 1)

            def body(j, place, on):
                if on(0):
                    pe.wait_ge(ld_w[place], 32 * (j - place) + 128)
                    wait(pe, ht_set, j - 1)
                    for k in range(2):
                        last = nc.tensor.matmul(ps_h[place % 2][:, T * k:T * k + T], W1[:, place, k, :],
                                                X2T[:, bass.ds(j, 1), :].rearrange("p a t -> p (a t)"), start=True, stop=True)
                    last.then_inc(h_full, 1)
                if on(1):
                    b, slot, s2 = j - 1, (place - 1) % WSLOTS, (place - 1) % 2
                    pe.wait_ge(ht_set, b + 1)
                    wait(pe, added, b - 1)
                    for t in range(2):
                        to = ps_o[s2][:, P * t:P * t + P]
                        nc.tensor.matmul(to, ones2[:, :], b2[:, slot, :], start=True, stop=False)
                        for k in range(2):
                            last = nc.tensor.matmul(to, HT[:, s2, k, P * t:P * t + P], W2[:, slot, k, :], start=False, stop=(k == 1))
                    last.then_inc(o_full, 1)
                if on(3):
                    b, s2 = j - 3, (place + 1) % 2
                    pe.wait_ge(ln3.xn_set, b + 1)
                    wait(pe, xt_set, b - 1)
                    for t in range(2):
                        last = nc.tensor.transpose(ps_tr[s2][:, P * t:P * t + P], XN[:, s2, t, :], ident[:, :])
                    last.then_inc(tr3_full, 1)

            pipeline(pe, NB, DEPTH, WSLOTS, body)

        @block.vector
        def _(dve):
            def x(b):
                return lambda t: X[:, bass.ds(2 * b + t, 1), :].rearrange("p a c -> p (a c)")

            def normed(j, place, on):
                if on(0):
                    ln2.statistics(dve, x(j), j, place)
                if on(1):
                    b, other = j - 1, 1 - place
                    ln2.normalise(dve, x(b), lambda t: XN[:, other, t, :], b, other, (tr2_full, b - 1))

            pipeline(dve, NB, 3, 2, lambda j, place, on: normed(j, place, on))
            dve.wait_ge(r_full, 1)
            nc.vector.tensor_tensor(sc[:, :], ps_r[0:NB, 0:8], brb[:, :], ALU.add).then_inc(sc_set, 1)
            dve.wait_ge(sc_set, 1)
            nc.vector.max(top[:, :], sc[:, :]).then_inc(top_set, 1)
            dve.wait_ge(top_set, 1)
            nc.vector.max_index(chosen[:, :], top[:, :], sc[:, :]).then_inc(chosen_set, 1)

            def body(j, place, on):
                if on(1):
                    b, s2 = j - 1, (place - 1) % 2
                    dve.wait_ge(o_full, b + 1)
                    at = X[:, bass.ds(2 * b, 2), :].rearrange("p a c -> p (a c)")
                    nc.vector.scalar_tensor_tensor(at, ps_o[s2][:, 0:T], 0.5, at, ALU.mult, ALU.add).then_inc(added, 1)
                    ln3.wait(dve, added, b + 1)
                    ln3.statistics(dve, x(b), b, s2)
                if on(2):
                    b, s2 = j - 2, place % 2
                    ln3.normalise(dve, x(b), lambda t: XN[:, s2, t, :], b, s2, (tr3_full, b - 1))

            pipeline(dve, NB, DEPTH, WSLOTS, body)


def attention1(nc, io, X, XT, X4, LG, ident):
    st = ExitStack()

    def sb(name, shape, dt=F32):
        return st.enter_context(nc.sbuf_tensor(name, shape, dt))

    def sem(name):
        return st.enter_context(nc.semaphore(name))

    with st:
        ctxs, CT = sb("a_ctx", [P, 8, CC]), sb("a_ct", [CC, NB * TC])
        Wq, Wk, Wv, wr = sb("a_wq", [P, P]), sb("a_wk", [CC, P]), sb("a_wv", [CC, P]), sb("a_wr", [8, P])
        wrT = sb("a_wrt", [P, 8])
        bq, bk, bvb = sb("a_bq", [P, 1]), sb("a_bk", [P, 1]), sb("a_bvb", [P, 4, P])
        KT = sb("a_kt", [P, NB, TC])
        V = sb("a_v", [P, NB, 2, P])
        QT = sb("a_qt", [P, 2, T])
        negmax, total, inverse = sb("a_negmax", [P, 2, 2]), sb("a_total", [P, 2, 2]), sb("a_inverse", [P, 2, 2])
        E, ET = sb("a_e", [P, 2, 2 * TC]), sb("a_et", [P, 2, P])
        XN4S = sb("a_xn4", [P, 2, 2, P])
        XN4T = sb("a_x4t", [P, 2, T])
        ps_q, ps_e, ps_x, ps_l = (st.enter_context(nc.psum_tensor(f"a_ps_{k}", [P, 512], F32)) for k in "qexl")
        ps_s, ps_o = ([st.enter_context(nc.psum_tensor(f"a_ps_{k}{i}", [P, 512], F32)) for i in range(2)] for k in "so")
        ln4 = Norm(nc, st, "ln4")
        ld_a, ct_full, ct_set, k_full, kt_set = sem("a_ld"), sem("a_ct_full"), sem("a_ct_set"), sem("a_k_full"), sem("a_kt_set")
        ld_b, zero_set = sem("a_ld_b"), sem("a_zero_set")
        v_full, v_set, q_full, qt_set = sem("a_v_full"), sem("a_v_set"), sem("a_q_full"), sem("a_qt_set")
        s_full, max_set, exp_set, e_full, et_set = sem("a_s_full"), sem("a_max_set"), sem("a_exp_set"), sem("a_e_full"), sem("a_et_set")
        inverse_set, o_full, added = sem("a_inverse_set"), sem("a_o_full"), sem("a_added")
        x_full, xt_set, l_full, l_set = sem("a_x_full"), sem("a_xt_set"), sem("a_l_full"), sem("a_l_set")
        block = st.enter_context(nc.Block())
        DEPTH = 6

        @block.sync
        def _(sp):
            sp.dma_start(ctxs[:, :, :], io["ctx_512"].rearrange("(o u) s c -> (u s) o c", u=2)).then_inc(ld_a, 16)
            sp.dma_start(Wk[:, :], io["L1_xattn_Wk"]).then_inc(ld_a, 16)
            sp.dma_start(Wv[:, :], io["L1_xattn_Wv"]).then_inc(ld_a, 16)
            sp.dma_start(Wq[:, :], io["L1_xattn_Wq"]).then_inc(ld_a, 16)
            sp.dma_start(wr[:, :], io["L1_ffn_wr"]).then_inc(ld_a, 16)
            with nc.allow_non_contiguous_dma(reason="biases onto the partitions"):
                sp.dma_start(bq[:, :], io["L1_xattn_bq"].rearrange("(c a) -> c a", a=1)).then_inc(ld_b, 16)
                sp.dma_start(bk[:, :], io["L1_xattn_bk"].rearrange("(c a) -> c a", a=1)).then_inc(ld_b, 16)
            for o in range(4):
                sp.dma_start(bvb[:, o, :], io["L1_xattn_bv"].rearrange("(a c) -> a c", a=1).to_broadcast([P, P])).then_inc(ld_b, 16)

        @block.gpsimd
        def _(pool):
            ln4.prepare(pool)
            pipeline(pool, NB, 0, 2, lambda b, place, on: ln4.root(pool, b, place))

        @block.scalar
        def _(act):
            act.preload_act_table(ACT.Exp)
            for i in range(2):
                act.wait_ge(ct_full, i + 1)
                nc.scalar.copy(CT[:, 512 * i:512 * i + 512], ps_s[i][0:CC, :]).then_inc(ct_set, 1)
            act.wait_ge(ld_b, 16 * 6)
            for i in range(2):
                act.wait_ge(k_full, i + 1)
                nc.scalar.activation(KT[:, 8 * i:8 * i + 8, :].rearrange("p b t -> p (b t)"), ps_o[i][:, :], ACT.Identity,
                                     bias=bk[:, 0:1]).then_inc(kt_set, 1)
            act.wait_ge(l_full, 1)
            nc.scalar.copy(wrT[:, :], ps_l[:, 0:8]).then_inc(l_set, 1)

            def body(j, place, on):
                other = 1 - place
                if on(0):
                    act.wait_ge(q_full, j + 1)
                    wait(act, s_full, j - 1)
                    nc.scalar.activation(QT[:, place, :], ps_q[:, 0:T], ACT.Identity,
                                         bias=bq[:, 0:1]).then_inc(qt_set, 1)
                if on(1):
                    b = j - 1
                    act.wait_ge(max_set, b + 1)
                    wait(act, e_full, b - 1)
                    wait(act, added, b - 1)
                    for t in range(2):
                        last = nc.scalar.activation(E[:, other, TC * t:TC * t + TC], ps_s[other][:, TC * t:TC * t + TC], ACT.Exp,
                                                    bias=negmax[:, other, t:t + 1], accum_out=total[:, other, t:t + 1])
                    last.then_inc(exp_set, 1)
                if on(2):
                    b = j - 2
                    act.wait_ge(e_full, b + 1)
                    wait(act, o_full, b - 1)
                    nc.scalar.copy(ET[:, place, :], ps_e[:, 0:P]).then_inc(et_set, 1)
                if on(5):
                    b = j - 5
                    act.wait_ge(x_full, b + 1)
                    nc.scalar.copy(X4[:, bass.ds(2 * b, 2), :], XN4S[:, other, :, :])
                    wait(act, l_full, b)
                    nc.scalar.copy(XN4T[:, other, :], ps_x[:, 0:T]).then_inc(xt_set, 1)

            pipeline(act, NB, DEPTH, 2, body)

        @block.tensor
        def _(pe):
            pe.wait_ge(ld_a, 16 * 5)
            for i in range(2):
                for o in range(4):
                    last = nc.tensor.transpose(ps_s[i][0:CC, P * o:P * o + P], ctxs[:, 4 * i + o, :], ident[:, :])
                last.then_inc(ct_full, 1)
            nc.tensor.transpose(ps_l[:, 0:8], wr[:, :], ident[0:8, 0:8]).then_inc(l_full, 1)
            pe.wait_ge(ct_set, 2)
            for i in range(2):
                nc.tensor.matmul(ps_o[i][:, :], Wk[:, :], CT[:, 512 * i:512 * i + 512], start=True, stop=True).then_inc(k_full, 1)
            banks = [ps_s[0], ps_s[1], ps_o[0], ps_o[1]]
            pe.wait_ge(kt_set, 2)
            for i in range(4):
                for o in range(4):
                    b = 4 * i + o
                    for w in range(2):
                        last = nc.tensor.matmul(banks[i][TC * w:TC * w + TC, P * o:P * o + P], CT[:, TC * b:TC * b + TC],
                                                Wv[:, :], start=True, stop=True)
                last.then_inc(v_full, 1)
            pe.wait_ge(v_set, 4)
            pe.wait_ge(l_set, 1)

            def body(j, place, on):
                other = 1 - place
                if on(0):
                    wait(pe, qt_set, j)
                    nc.tensor.matmul(ps_q[:, 0:T], Wq[:, :], XT[:, bass.ds(j, 1), :].rearrange("p a t -> p (a t)"),
                                     start=True, stop=True).then_inc(q_full, 1)
                if on(1):
                    b = j - 1
                    pe.wait_ge(qt_set, b + 1)
                    wait(pe, exp_set, b - 1)
                    for t in range(2):
                        last = nc.tensor.matmul(ps_s[other][:, TC * t:TC * t + TC], QT[:, other, P * t:P * t + P],
                                                KT[:, bass.ds(b, 1), :].rearrange("p a t -> p (a t)"), start=True, stop=True)
                    last.then_inc(s_full, 1)
                if on(2):
                    b = j - 2
                    pe.wait_ge(exp_set, b + 1)
                    wait(pe, et_set, b)
                    nc.tensor.transpose(ps_e[:, 0:P], E[:, place, :], ident[:, :]).then_inc(e_full, 1)
                if on(3):
                    b = j - 3
                    pe.wait_ge(et_set, b + 1)
                    wait(pe, added, b - 1)
                    nc.tensor.matmul(ps_o[other][:, 0:T], ET[:, other, :], V[:, bass.ds(b, 1), :, :].rearrange("p a t c -> p (a t c)"),
                                     start=True, stop=True).then_inc(o_full, 1)
                if on(5):
                    b = j - 5
                    pe.wait_ge(ln4.xn_set, b + 1)
                    wait(pe, xt_set, b)
                    for t in range(2):
                        last = nc.tensor.transpose(ps_x[:, P * t:P * t + P], XN4S[:, other, t, :], ident[:, :])
                    last.then_inc(x_full, 1)
                if on(6):
                    b = j - 6
                    pe.wait_ge(xt_set, b + 1)
                    pe.wait_ge(l_set, b + 1)
                    for t in range(2):
                        last = nc.tensor.matmul(ps_l[:, 8 * t:8 * t + 8], XN4T[:, place, P * t:P * t + P], wrT[:, :],
                                                start=True, stop=True)
                    last.then_inc(l_full, 1)

            pipeline(pe, NB, DEPTH, 2, body)

        @block.vector
        def _(dve):
            banks = [ps_s[0], ps_s[1], ps_o[0], ps_o[1]]
            nc.vector.memset(V[:, :, :, :], 0.0).then_inc(zero_set, 1)
            dve.wait_ge(zero_set, 1)
            dve.wait_ge(ld_b, 16 * 6)
            for i in range(4):
                dve.wait_ge(v_full, i + 1)
                for t in range(2):
                    half = slice(TC * t, TC * t + TC)
                    last = nc.vector.tensor_tensor(V[half, 4 * i:4 * i + 4, t, :], banks[i][half, :].rearrange("p (b c) -> p b c", b=4),
                                                   bvb[half, :, :], ALU.add)
                last.then_inc(v_set, 1)

            def x(b):
                return lambda t: X[:, bass.ds(2 * b + t, 1), :].rearrange("p a c -> p (a c)")

            def body(j, place, on):
                other = 1 - place
                if on(1):
                    b = j - 1
                    dve.wait_ge(s_full, b + 1)
                    wait(dve, exp_set, b - 1)
                    nc.vector.tensor_reduce(negmax[:, other, :], ps_s[other][:, 0:P].rearrange("p (t k) -> p t k", t=2), AX.X, ALU.max,
                                            negate=True).then_inc(max_set, 1)
                if on(3):
                    b = j - 3
                    dve.wait_ge(exp_set, b + 1)
                    nc.vector.reciprocal(inverse[:, other, :], total[:, other, :]).then_inc(inverse_set, 1)
                    dve.wait_ge(inverse_set, b + 1)
                    dve.wait_ge(o_full, b + 1)
                    for t in range(2):
                        at = X[:, bass.ds(2 * b + t, 1), :].rearrange("p a c -> p (a c)")
                        last = nc.vector.scalar_tensor_tensor(at, ps_o[other][:, P * t:P * t + P], inverse[:, other, t:t + 1], at,
                                                              ALU.mult, ALU.add)
                    last.then_inc(added, 1)
                    ln4.wait(dve, added, b + 1)
                    ln4.statistics(dve, x(b), b, other)
                if on(4):
                    b = j - 4
                    ln4.normalise(dve, x(b), lambda t: XN4S[:, place, t, :], b, place, (xt_set, b - 1))
                if on(6):
                    b = j - 6
                    dve.wait_ge(l_full, b + 2)
                    nc.vector.tensor_copy(LG[:, bass.ds(2 * b, 2), :], ps_l[:, 0:16].rearrange("p (t e) -> p t e", t=2)).then_inc(l_set, 1)

            pipeline(dve, NB, DEPTH, 2, body)


EXPERTS = 8
CAP = max(8, int(max(1, NB * T * 2 // EXPERTS) * 1.25))
FF = 512
NF = FF // P
TILES = 2 * NB
CT_ = CAP // P
CHUNKS = CT_ // 2
DROPPED = 1 << 20


def moe(nc, io, out, X, X4, LG, ident, rows_in, rows_out):
    st = ExitStack()

    def sb(name, shape, dt=F32):
        return st.enter_context(nc.sbuf_tensor(name, shape, dt))

    def sem(name):
        return st.enter_context(nc.semaphore(name))

    with st:
        top, picked = sb("m_top", [P, TILES, 8]), sb("m_picked", [P, TILES, 8], U32)
        expert = sb("m_expert", [P, 2, TILES])
        numbers = sb("m_numbers", [P, TILES, EXPERTS])
        own = sb("m_own", [P, 2, TILES, EXPERTS])
        mask = sb("m_mask", [P, TILES * EXPERTS], BF16)
        before = sb("m_before", [P, P], BF16)
        onesb = sb("m_onesb", [P, P], BF16)
        ones_f = sb("m_ones", [P, P])
        counts = sb("m_counts", [P, 2, TILES, EXPERTS])
        position = sb("m_position", [P, TILES, EXPERTS])
        place_of = sb("m_place", [P, 2, TILES])
        late = sb("m_late", [P, 2, TILES])
        base = sb("m_base", [P, 2, TILES])
        to_f, from_f = sb("m_to_f", [P, 2, TILES]), sb("m_from_f", [P, 2, TILES])
        to, frm = sb("m_to", [P, 2, TILES], U32), sb("m_from", [P, 2, TILES], U32)
        gate = sb("m_gate", [P, 2, TILES])
        gap, grown, denominator = sb("m_gap", [P, TILES]), sb("m_grown", [P, TILES]), sb("m_denominator", [P, TILES])
        in_index, in_rows = sb("m_in_index", [P, 2, 4, 2], U32), sb("m_in_rows", [P, 2, 4, P])
        out_index, out_rows = sb("m_out_index", [P, 2, 4, 2], U32), sb("m_out_rows", [P, 2, 4, 2, P])
        b1r, b1T = sb("m_b1r", [EXPERTS * NF, P]), sb("m_b1t", [P, EXPERTS * NF])
        w1, w2 = sb("m_w1", [P, 2, FF]), sb("m_w2", [P, 2, NF, P])
        b2b = sb("m_b2b", [P, 2, 2, P])
        b1c = sb("m_b1c", [P, 2, NF])
        XG = sb("m_xg", [P, 2, CT_, P])
        XGT = sb("m_xgt", [P, 2, CAP])
        HT = sb("m_ht", [P, 2, NF, T])
        Y = sb("m_y", [P, 2, CT_, P])
        ps_h = [st.enter_context(nc.psum_tensor(f"m_h{i}", [P, NF, T], F32)) for i in range(2)]
        ps_y = [st.enter_context(nc.psum_tensor(f"m_y{i}", [P, 512], F32)) for i in range(2)]
        ps_t = [st.enter_context(nc.psum_tensor(f"m_t{i}", [P, 512], F32)) for i in range(2)]

        ones_set, consts_set, top_set, picked_set = sem("m_ones_set"), sem("m_consts_set"), sem("m_top_set"), sem("m_picked_set")
        chain = sem("m_chain")
        mask_set, counted, gap_set, grown_set = sem("m_mask_set"), sem("m_counted"), sem("m_gap_set"), sem("m_grown_set")
        in_set, scattered = sem("m_in_set"), [sem(f"m_scattered{i}") for i in range(2)]
        ld_b, b1_full, b1_set = sem("m_ld_b"), sem("m_b1_full"), sem("m_b1_set")
        ld_w, ld_x = [sem(f"m_ld_w{i}") for i in range(2)], [sem(f"m_ld_x{i}") for i in range(2)]
        t_full, xgt_set, h_full, ht_set = sem("m_t_full"), sem("m_xgt_set"), sem("m_h_full"), sem("m_ht_set")
        y_full, y_set, y_stored = sem("m_y_full"), sem("m_y_set"), [sem(f"m_y_stored{i}") for i in range(2)]
        out_index_set, gathered, half_added, added = (
            sem("m_out_index_set"), [sem(f"m_gathered{i}") for i in range(2)], sem("m_half_added"), sem("m_added"))
        stored = sem("m_stored")
        waited = sem("m_waited")
        block = st.enter_context(nc.Block())
        ALL = EXPERTS * CHUNKS

        def rows(x, e):
            return x[bass.ds(CAP * e, CAP), :].rearrange("(t p) c -> p t c", p=P)

        @block.sync
        def _(sp):
            sp.dma_start(b1r[:, :], io["L1_ffn_b1"].rearrange("e (f c) -> (e f) c", c=P)).then_inc(ld_b, 16)

            def load_weights(e, slot):
                wait(sp, y_full, CHUNKS * (e - 1))
                sp.dma_start(w1[:, slot, :], io["L1_ffn_w1"][bass.ds(e, 1), :, :].rearrange("a c f -> (a c) f")).then_inc(ld_w[slot], 16)
                sp.dma_start(w2[:, slot, :, :], io["L1_ffn_w2"][bass.ds(e, 1), :, :].rearrange("a (f p) c -> p (a f) c", p=P)).then_inc(ld_w[slot], 16)
                wait(sp, y_set, CHUNKS * (e - 1))
                for t in range(2):
                    sp.dma_start(b2b[:, slot, t, :], io["L1_ffn_b2"][bass.ds(e, 1), :].to_broadcast([P, P])).then_inc(ld_w[slot], 16)

            def load_tokens(e, slot):
                wait(sp, xgt_set, CHUNKS * (e - 1))
                sp.dma_start(XG[:, slot, :, :], rows(rows_in, e)).then_inc(ld_x[slot], 16)

            def store(e, slot):
                sp.wait_ge(y_set, CHUNKS * (e + 1))
                sp.dma_start(rows(rows_out, e), Y[:, slot, :, :]).then_inc(y_stored[slot], 16)

            load_weights(0, 0)
            load_weights(1, 1)
            for i in range(2):
                sp.wait_ge(scattered[i], 16 * 8 * 4)
            load_tokens(0, 0)
            load_tokens(1, 1)
            with sp.Fori(0, EXPERTS - 3, 2) as e:
                for u in range(2):
                    load_tokens(e + u + 2, u)
                    store(e + u, u)
                    load_weights(e + u + 2, u)
            for e in range(EXPERTS - 2, EXPERTS):
                store(e, e % 2)
            ov = out.rearrange("b (t p) c -> p (b t) c", p=P)
            with sp.Fori(0, 8, 1) as g:
                sp.wait_ge(added, g + 1)
                sp.dma_start(ov[:, bass.ds(4 * g, 4), :], X[:, bass.ds(4 * g, 4), :]).then_inc(stored, 16)
            sp.wait_ge(stored, 16 * 8)

        @block.gpsimd
        def _(pool):
            nc.gpsimd.memset(ones_f[:, :], 1.0).then_inc(ones_set, 1)
            pool.wait_ge(ones_set, 1)
            nc.gpsimd.iota(numbers[:, :, :], pattern=[[0, TILES], [1, EXPERTS]], base=0, channel_multiplier=0,
                           allow_small_or_imprecise_dtypes=True).then_inc(consts_set, 1)
            nc.gpsimd.affine_select(out=before[:, :], in_=ones_f[:, :], compare_op=ALU.is_gt, fill=0.0, base=0,
                                    pattern=[[1, P]], channel_multiplier=-1).then_inc(consts_set, 1)
            nc.gpsimd.affine_select(out=onesb[:, :], in_=ones_f[:, :], compare_op=ALU.is_ge, fill=1.0, base=0,
                                    pattern=[[1, P]], channel_multiplier=0).then_inc(consts_set, 1)

            def scatter(g, slot):
                pool.wait_ge(in_set, g + 1)
                if not isinstance(g, int):
                    pool.sem_inc(waited, 1)
                for t in range(4):
                    for k in range(2):
                        nc.gpsimd.indirect_dma_start(
                            out=rows_in, out_offset=bass.IndirectOffsetOnAxis(in_index[:, slot, t, k:k + 1], 0),
                            in_=in_rows[:, slot, t, :], in_offset=None, bounds_check=EXPERTS * CAP - 1,
                            oob_is_err=False).then_inc(scattered[slot], 16)

            def gather(g, slot):
                pool.wait_ge(out_index_set, g + 1)
                if not isinstance(g, int):
                    pool.sem_inc(waited, 1)
                for t in range(4):
                    for k in range(2):
                        nc.gpsimd.indirect_dma_start(
                            out=out_rows[:, slot, t, k, :], out_offset=None, in_=rows_out,
                            in_offset=bass.IndirectOffsetOnAxis(out_index[:, slot, t, k:k + 1], 0),
                            bounds_check=EXPERTS * CAP - 1, oob_is_err=False).then_inc(gathered[slot], 16)

            with pool.Fori(0, 7, 2) as g:
                for u in range(2):
                    scatter(g + u, u)
            for i in range(2):
                pool.wait_ge(y_stored[i], 16 * (EXPERTS // 2))
            with pool.Fori(0, 7, 2) as g:
                for u in range(2):
                    gather(g + u, u)

        @block.scalar
        def _(act):
            act.preload_act_table(ACT.Exp)
            act.wait_ge(gap_set, 1)
            nc.scalar.activation(grown[:, :], gap[:, :], ACT.Exp).then_inc(grown_set, 1)
            act.preload_act_table(ACT.Gelu_apprx_tanh)

            def body(e, slot):
                for c in range(CHUNKS):
                    m, s2 = CHUNKS * e + c, (slot + c) % 2
                    act.wait_ge(h_full, m + 1)
                    wait(act, y_full, m - 1)
                    act.wait_ge(b1_set, e + 2)
                    for f in range(NF):
                        last = nc.scalar.activation(HT[:, s2, f, :], ps_h[s2][:, f, :], ACT.Gelu_apprx_tanh,
                                                    bias=b1c[:, slot, f:f + 1])
                    last.then_inc(ht_set, 1)

            body(0, 0)
            body(1, 1)
            with act.Fori(2, EXPERTS - 1, 2) as e:
                for u in range(2):
                    body(e + u, u)

        @block.tensor
        def _(pe):
            pe.wait_ge(ld_b, 16)
            nc.tensor.transpose(ps_y[0][:, 0:EXPERTS * NF], b1r[:, :], ident[0:EXPERTS * NF, 0:EXPERTS * NF]).then_inc(b1_full, 1)
            pe.wait_ge(consts_set, 3)
            pe.wait_ge(mask_set, 1)
            nc.tensor.matmul(ps_t[0][:, 0:T], before[:, :], mask[:, :], start=True, stop=True)
            nc.tensor.matmul(ps_t[1][:, 0:T], onesb[:, :], mask[:, :], start=True, stop=True).then_inc(counted, 1)
            pe.wait_ge(in_set, 1)
            pe.wait_ge(b1_set, 1)

            def transpose_rows(m, e, c, slot, s2):
                if c == 0:
                    pe.wait_ge(ld_x[slot], 8 * (e - slot) + 16)
                wait(pe, xgt_set, m - 1)
                for t in range(2):
                    last = nc.tensor.transpose(ps_t[s2][:, P * t:P * t + P], XG[:, slot, 2 * c + t, :], ident[:, :])
                last.then_inc(t_full, 1)

            def hidden(m, e, c, slot, s2):
                pe.wait_ge(xgt_set, m + 1)
                if c == 0:
                    pe.wait_ge(ld_w[slot], 32 * (e - slot) + 64)
                wait(pe, ht_set, m - 1)
                for f in range(NF):
                    last = nc.tensor.matmul(ps_h[s2][:, f, :], w1[:, slot, P * f:P * f + P], XGT[:, slot, T * c:T * c + T],
                                            start=True, stop=True)
                last.then_inc(h_full, 1)

            def outputs(m, slot, s2):
                pe.wait_ge(ht_set, m + 1)
                wait(pe, y_set, m - 1)
                for t in range(2):
                    for f in range(NF):
                        last = nc.tensor.matmul(ps_y[s2][:, P * t:P * t + P], HT[:, s2, f, P * t:P * t + P], w2[:, slot, f, :],
                                                start=(f == 0), stop=(f == NF - 1))
                last.then_inc(y_full, 1)

            def body(e, slot, first=False, final=False):
                for c in range(CHUNKS):
                    m, s2 = CHUNKS * e + c, (slot + c) % 2
                    hidden(m, e, c, slot, s2)
                    if not final:
                        transpose_rows(m + CHUNKS, e + 1, c, 1 - slot, 1 - s2)
                    if not (first and c == 0):
                        outputs(m - 1, slot if c else 1 - slot, 1 - s2)

            for c in range(CHUNKS):
                transpose_rows(c, 0, c, 0, c % 2)
            body(0, 0, first=True)
            with pe.Fori(1, EXPERTS - 2, 2) as e:
                body(e, 1)
                body(e + 1, 0)
            body(EXPERTS - 1, 1, final=True)
            outputs(ALL - 1, 1, (ALL - 1) % 2)

        @block.vector
        def _(dve):
            count = [0]

            def then(ins):
                count[0] += 1
                ins.then_inc(chain, 1)
                dve.wait_ge(chain, count[0])

            for t in range(TILES):
                last = nc.vector.max(top[:, t, :], LG[:, t, :])
            last.then_inc(top_set, 1)
            dve.wait_ge(top_set, 1)
            nc.vector.tensor_tensor(gap[:, :], top[:, :, 1], top[:, :, 0], ALU.subtract).then_inc(gap_set, 1)
            for t in range(TILES):
                last = nc.vector.max_index(picked[:, t, :], top[:, t, :], LG[:, t, :])
            last.then_inc(picked_set, 1)
            dve.wait_ge(picked_set, 1)
            then(nc.vector.tensor_copy(expert[:, :, :].rearrange("p k t -> p t k"), picked[:, :, 0:2]))
            dve.wait_ge(consts_set, 3)
            for k in range(2):
                last = nc.vector.tensor_tensor(own[:, k, :, :], numbers[:, :, :],
                                               expert[:, k, :].unsqueeze(2).to_broadcast([P, TILES, EXPERTS]), ALU.is_equal)
            then(last)
            nc.vector.tensor_tensor(mask[:, :].rearrange("p (t e) -> p t e", e=EXPERTS), own[:, 0, :, :], own[:, 1, :, :],
                                    ALU.add).then_inc(mask_set, 1)
            then(nc.vector.tensor_scalar(base[:, :, :], expert[:, :, :], float(CAP), 0.0, ALU.mult, ALU.add))
            dve.wait_ge(counted, 1)
            then(nc.vector.tensor_copy(counts[:, 0, :, :].rearrange("p t e -> p (t e)"), ps_t[1][:, 0:T]))
            a = 0
            for d in (1, 2, 4, 8, 16):
                nc.vector.tensor_copy(counts[:, 1 - a, 0:d, :], counts[:, a, 0:d, :])
                then(nc.vector.tensor_tensor(counts[:, 1 - a, d:, :], counts[:, a, d:, :], counts[:, a, :TILES - d, :], ALU.add))
                a = 1 - a
            within = ps_t[0][:, 0:T].rearrange("p (t e) -> p t e", e=EXPERTS)
            nc.vector.tensor_copy(position[:, 0, :], within[:, 0, :])
            then(nc.vector.tensor_tensor(position[:, 1:, :], within[:, 1:, :], counts[:, a, :TILES - 1, :], ALU.add))
            for k in range(2):
                last = nc.vector.tensor_tensor(own[:, k, :, :], own[:, k, :, :], position[:, :, :], ALU.mult)
            then(last)
            then(nc.vector.tensor_reduce(place_of[:, :, :], own[:, :, :, :], AX.X, ALU.add))
            nc.vector.tensor_scalar(late[:, :, :], place_of[:, :, :], float(CAP) - 0.5, 0.0, ALU.is_gt, ALU.add)
            then(nc.vector.tensor_tensor(to_f[:, :, :], base[:, :, :], place_of[:, :, :], ALU.add))
            nc.vector.scalar_tensor_tensor(from_f[:, :, :], place_of[:, :, :], float(CAP - 1), base[:, :, :], ALU.min, ALU.add)
            then(nc.vector.scalar_tensor_tensor(to_f[:, :, :], late[:, :, :], float(DROPPED), to_f[:, :, :], ALU.mult, ALU.add))
            nc.vector.tensor_copy(to[:, :, :], to_f[:, :, :])
            then(nc.vector.tensor_copy(frm[:, :, :], from_f[:, :, :]))

            def scatter_in(g, slot):
                wait(dve, scattered[slot], 64 * (g - slot))
                nc.vector.tensor_copy(in_index[:, slot, :, :], to[:, :, bass.ds(4 * g, 4)].rearrange("p k t -> p t k"))
                nc.vector.tensor_copy(in_rows[:, slot, :, :], X4[:, bass.ds(4 * g, 4), :]).then_inc(in_set, 1)

            scatter_in(0, 0)
            scatter_in(1, 1)
            dve.wait_ge(grown_set, 1)
            then(nc.vector.tensor_scalar(denominator[:, :], grown[:, :], 1.0, 0.0, ALU.add, ALU.add))
            then(nc.vector.reciprocal(denominator[:, :], denominator[:, :]))
            nc.vector.tensor_copy(gate[:, 0, :], denominator[:, :])
            nc.vector.tensor_tensor(gate[:, 1, :], grown[:, :], denominator[:, :], ALU.mult)
            then(nc.vector.tensor_scalar(late[:, :, :], late[:, :, :], -1.0, 1.0, ALU.mult, ALU.add))
            then(nc.vector.tensor_tensor(gate[:, :, :], gate[:, :, :], late[:, :, :], ALU.mult))
            dve.wait_ge(b1_full, 1)
            nc.vector.tensor_copy(b1T[:, :], ps_y[0][:, 0:EXPERTS * NF]).then_inc(b1_set, 1)
            with dve.Fori(2, 7, 2) as g:
                for u in range(2):
                    scatter_in(g + u, u)

            def drain_rows(m, c, slot, s2):
                dve.wait_ge(t_full, m + 1)
                nc.vector.tensor_copy(XGT[:, slot, T * c:T * c + T], ps_t[s2][:, 0:T]).then_inc(xgt_set, 1)

            def drain_outputs(m, e, c, slot, s2):
                dve.wait_ge(y_full, m + 1)
                if c == 0:
                    wait(dve, y_stored[slot], 8 * (e - slot))
                nc.vector.tensor_tensor(Y[:, slot, 2 * c:2 * c + 2, :].rearrange("p t c -> p (t c)"), ps_y[s2][:, 0:T],
                                        b2b[:, slot, :, :].rearrange("p t c -> p (t c)"), ALU.add).then_inc(y_set, 1)

            def bias(e, slot):
                nc.vector.tensor_copy(b1c[:, slot, :], b1T[:, bass.ds(NF * e, NF)]).then_inc(b1_set, 1)

            def body(e, slot, final=False):
                for c in range(CHUNKS):
                    m, s2 = CHUNKS * e + c, (slot + c) % 2
                    if not final:
                        drain_rows(m + CHUNKS, c, 1 - slot, 1 - s2)
                    drain_outputs(m, e, c, slot, s2)
                if not final:
                    bias(e + 2, slot) if not (isinstance(e, int) and e + 2 >= EXPERTS) else None

            dve.wait_ge(b1_set, 1)
            bias(0, 0)
            bias(1, 1)
            for c in range(CHUNKS):
                drain_rows(c, c, 0, c % 2)
            body(0, 0)
            body(1, 1)
            with dve.Fori(2, EXPERTS - 3, 2) as e:
                for u in range(2):
                    body(e + u, u)
            body(EXPERTS - 2, 0)
            body(EXPERTS - 1, 1, final=True)

            def indices(g, slot):
                wait(dve, gathered[slot], 64 * (g - slot))
                nc.vector.tensor_copy(out_index[:, slot, :, :],
                                      frm[:, :, bass.ds(4 * g, 4)].rearrange("p k t -> p t k")).then_inc(out_index_set, 1)

            def combine(g, slot):
                dve.wait_ge(gathered[slot], 64 * (g - slot) + 128)
                for k in range(2):
                    for t in range(4):
                        at = X[:, bass.ds(4 * g + t, 1), :].rearrange("p a c -> p (a c)")
                        last = nc.vector.scalar_tensor_tensor(at, out_rows[:, slot, t, k, :], gate[:, k, bass.ds(4 * g + t, 1)],
                                                              at, ALU.mult, ALU.add)
                    last.then_inc(half_added if k == 0 else added, 1)
                    if k == 0:
                        dve.wait_ge(half_added, g + 1)

            indices(0, 0)
            indices(1, 1)
            combine(0, 0)
            indices(2, 0)
            combine(1, 1)
            indices(3, 1)
            with dve.Fori(2, 5, 2) as g:
                for u in range(2):
                    combine(g + u, u)
                    indices(g + u + 2, u)
            combine(6, 0)
            combine(7, 1)


def program(nc, io, out):
    with ExitStack() as ctx:
        X = ctx.enter_context(nc.sbuf_tensor("X", [P, 2 * NB, P], F32))
        ident = ctx.enter_context(nc.sbuf_tensor("ident", [P, P], F32))
        identb = ctx.enter_context(nc.sbuf_tensor("identb", [P, P], BF16))
        rows_in = nc.dram_tensor("expert_rows_in", (EXPERTS * CAP, P), F32).ap()
        rows_out = nc.dram_tensor("expert_rows_out", (EXPERTS * CAP, P), F32).ap()
        attention0(nc, io, X, ident, identb)
        X4 = ctx.enter_context(nc.sbuf_tensor("X4", [P, 2 * NB, P], F32))
        LG = ctx.enter_context(nc.sbuf_tensor("LG", [P, 2 * NB, 8], F32))
        with nc.sbuf_tensor("XT", [P, NB, T], F32) as XT:
            ffn0(nc, io, X, XT, ident, rows_in)
            attention1(nc, io, X, XT, X4, LG, ident)
        moe(nc, io, out, X, X4, LG, ident, rows_in, rows_out)


NAMES = ["x", "ctx_512"] + ["L0_xattn_" + n for n in ("Wk", "bk", "Wq", "bq", "Wv", "bv", "Wck", "bck", "Wcq", "bcq",
                                                     "Wcv", "bcv", "Wp", "bp")] + [
    "L0_ffn_" + n for n in ("Wr", "br", "W1", "b1", "W2", "b2")] + [
    "L1_xattn_" + n for n in ("Wq", "bq", "Wk", "bk", "Wv", "bv")] + ["L1_ffn_" + n for n in ("wr", "w1", "b1", "w2", "b2")]


def kernel(**inputs):
    import concourse.bacc as bacc
    from concourse.bass_utils import run_bass_kernel_spmd

    nc = bacc.Bacc("TRN2", target_bir_lowering=False, num_devices=1)
    arrays, io = {}, {}
    for name in NAMES:
        a = np.ascontiguousarray(inputs[name])
        arrays[name + "_dram"] = a
        io[name] = nc.dram_tensor(name + "_dram", a.shape, mybir.dt.from_np(a.dtype), kind="ExternalInput").ap()
    out = nc.dram_tensor("out_dram", (NB, T, P), F32, kind="ExternalOutput").ap()
    program(nc, io, out)
    return run_bass_kernel_spmd(nc, [arrays], core_ids=[0]).results[0]["out_dram"]
```

```python
from contextlib import ExitStack

import numpy as np
import concourse.bass as bass
from concourse import mybir

ALU = mybir.AluOpType
ACT = mybir.ActivationFunctionType
AX = mybir.AxisListType
F32 = mybir.dt.float32
F32R = mybir.dt.float32r
BF16 = mybir.dt.bfloat16
U32 = mybir.dt.uint32

P = 128
NB = 16
T = 256
TC = 64
CC = 64
H0 = 16
HD = 8
NG = 4
HG = 4
GC = HG * HD
NSTACK = 3 * GC
NROW = NSTACK + HG
SCALE = float(np.float32(1.0 / np.sqrt(HD)))
EPS = 1e-5
NEG = -1e30
RING = 3



def steps(g, prev, nxt, nxt2):
    ahead = g < 2 or nxt
    u = []
    if ahead:
        u += ["S0", "S1"]
    if g == 3 and prev:
        u += ["O"]
    if nxt:
        u += ["K"]
    if g < 3 or nxt:
        u += ["M"]
    if ahead:
        u += ["S2"]
    if nxt:
        u += ["Q"]
    if ahead:
        u += ["S3"]
    if nxt:
        u += ["C"]
    if g == 0 and nxt:
        u += ["V0"]
    if g == 1:
        u += (["T1"] if prev else []) + (["V1"] if nxt else [])
    if g == 2:
        u += (["YT"] if prev else []) + (["X"] if nxt2 else [])
    if g == 3:
        u += ["T0"]
    return u


START = ([("CT", 0), ("CT", 1), ("X", 0), ("V0", 0), ("V1", 0)] + [("KC", i) for i in range(8)]
         + [(k, g) for g in range(NG) for k in "KQC"] + [("VC", i) for i in range(4)] + [("X", 1)]
         + [(f"S{j}", n) for n in range(2) for j in range(4)] + [("M", 0)])
LOOPED = NB - 3


def ring_plan():
    parts = [("start", START)]
    for part, prev, nxt, nxt2 in (("first", 0, 1, 1), ("loop", 1, 1, 1), ("before last", 1, 1, 0), ("last", 1, 0, 0)):
        parts.append((part, [(u, g) for g in range(NG) for u in steps(g, prev, nxt, nxt2)]))
    parts.append(("end", [("T1", 0), ("YT", 0), ("O", 0)]))
    where, at = {}, 0
    for part, uses in parts:
        where[part] = {u: at + i for i, u in enumerate(uses)}
        at += len(uses) * (LOOPED if part == "loop" else 1)
    return where


WHERE = ring_plan()
PER_SEQ = len(WHERE["loop"])
assert PER_SEQ % RING == 0
BEFORE = {"first": "start", "loop": "loop", "before last": "loop", "last": "before last"}


class Seq:

    def __init__(self, b, part, prev=True, nxt=True, nxt2=True, slot=0):
        self.b, self.part, self.slot = b, part, slot
        self.prev, self.nxt, self.nxt2 = prev, nxt, nxt2

    def at(self, position):
        before = position // RING
        if self.part == "loop":
            before = before + (self.b - 1) * (PER_SEQ // RING)
        return position % RING, before

    def ring(self, name, g):
        return self.at(WHERE[self.part][(name, g)])

    def maxima(self, g):
        if g:
            return self.ring("M", g - 1)
        last = WHERE[BEFORE[self.part]]
        back = len(last) - list(last).index(("M", 0 if self.part == "first" else 3))
        return self.at(min(WHERE[self.part].values()) - back)


def sequences(eng, body):
    body(Seq(0, "first", prev=False, slot=0))
    with eng.Fori(1, NB - 3, 2) as i:
        body(Seq(i, "loop", slot=1))
        body(Seq(i + 1, "loop", slot=0))
    body(Seq(NB - 3, "loop", slot=1))
    body(Seq(NB - 2, "before last", nxt2=False, slot=0))
    body(Seq(NB - 1, "last", nxt=False, nxt2=False, slot=1))


def attention0(nc, io, X, CT, ident, identb):
    st = ExitStack()

    def sb(name, shape, dt=F32):
        return st.enter_context(nc.sbuf_tensor(name, shape, dt))

    def sem(name):
        return st.enter_context(nc.semaphore(name))

    with st:
        ones = sb("ones", [P, P])
        causal = sb("causal", [P, HG, P], BF16)
        stats = sb("stats", [P, 2 * NB, 6])
        mv = sb("mv", [P, 2 * NB, 2])
        rstd = sb("rstd", [P, 2 * NB])
        power = sb("power", [P, 2 * NB])
        half = sb("half", [P, 2 * NB])
        shift = sb("shift", [P, 2 * NB])
        XN = sb("XN", [P, 2, 2, P])
        W = {k: sb("w" + k, [P, P]) for k in ("K", "Q", "C", "V", "P")}
        WC = {k: sb("wc" + k, [CC, P]) for k in ("K", "V")}
        WS = {k: sb("ws" + k, [P, 2, NG, 3, GC], F32R) for k in ("K", "Q", "C")}
        WCS = sb("wcs", [CC, 2, NG, 3, GC], F32R)
        WV = sb("wv", [P, 2, P], F32R)
        BS = {k: sb("bs" + k, [NSTACK, NG]) for k in ("K", "Q", "C", "KC")}
        BL = {k: sb("bl" + k, [NSTACK, NG]) for k in ("K", "Q", "C", "KC")}
        lowk = sb("lowk", [NSTACK, 1])
        lowq = sb("lowq", [NSTACK, 1])
        headrow = sb("headrow", [P, HG])
        bvb = sb("bvb", [P, P])
        bcvb = sb("bcvb", [P, P])
        bpb = sb("bpb", [P, 2, P])
        ctxs = sb("ctxs", [P, 8, CC])
        CTR = sb("CTR", [CC, 2, NB * TC], F32R)
        KC = sb("KC", [NSTACK, NG, NB * TC], F32R)
        VCA = sb("VCA", [P, NB, P])
        XR = sb("XR", [P, 2, 2, T], F32R)
        LO = sb("LO", [NSTACK, 4, T], F32R)
        KS = sb("KS", [NSTACK, 2, T], F32R)
        KM = sb("KM", [NROW, 2 * NG, HG, T], F32R)
        KCM = sb("KCM", [NROW, 2, NG, HG, TC], F32R)
        QC = sb("QC", [NROW, 2 * NG, 2, T], F32R)
        VS = sb("VS", [P, 2, 2, H0, 4 * HD])
        VC = sb("VC", [P, 2, H0 // 2, 8 * HD])
        MG = sb("MG", [P, 2, 4, NROW])
        PT = sb("PT", [P, 2, 2048])
        NV = sb("NV", [P, 2, 512])
        RD = sb("RD", [P, 4, HG, 2])
        YN = sb("YN", [P, 4, 2, HG, HD])
        Y = sb("Y", [P, 2, P])
        YT = sb("YT", [P, T])

        ps_ring = [st.enter_context(nc.psum_tensor(f"ring{i}", [P, 512], F32)) for i in range(RING)]
        ps_pv = st.enter_context(nc.psum_tensor("ps_pv", [P, 512], F32))
        ps_st = st.enter_context(nc.psum_tensor("ps_st", [P, 2048], F32))

        ld_x = [sem(f"ld_x{i}") for i in range(4)]
        ld_w, ld_b, ld_s, ld_c = sem("ld_w"), sem("ld_b"), sem("ld_s"), sem("ld_c")
        ring_full = [sem(f"ring_full{i}") for i in range(RING)]
        ring_free = [sem(f"ring_free{i}") for i in range(RING)]
        zeros_set, consts_set = sem("zeros_set"), sem("consts_set")
        low_masks_set, weights_set = sem("low_masks_set"), sem("weights_set")
        waited = sem("waited")
        stats_set, var_set, rstd_set, shift_set = sem("stats_set"), sem("var_set"), sem("rstd_set"), sem("shift_set")
        chain = sem("chain")
        xn_set, xb_set, xhigh_set, ctxt_set = sem("xn_set"), sem("xb_set"), sem("xhigh_set"), sem("ctxt_set")
        low_set, km_set, kcm_set, vc_set = sem("low_set"), sem("km_set"), sem("kcm_set"), sem("vc_set")
        max_set, rd_set, y_set = sem("max_set"), sem("rd_set"), sem("y_set")
        st_full, exp_done, sel_done, pv_done, nv_set = (
            sem("st_full"), sem("exp_done"), sem("sel_done"), sem("pv_done"), sem("nv_set"))

        block = st.enter_context(nc.Block())
        start = Seq(0, "start")
        end = Seq(NB, "end")

        def wait_full(eng, s, name, g):
            bank, before = s.ring(name, g)
            eng.wait_ge(ring_full[bank], before + 1)
            return ps_ring[bank], ring_free[bank]

        def wait_drained(eng, s, name, g):
            bank, before = s.ring(name, g)
            eng.wait_ge(ring_free[bank], before + 1)

        def pair(b):
            return X[:, bass.ds(2 * b, 2), :]

        @block.sync
        def _(sp):
            xv = io["x"].rearrange("b (t p) c -> p (b t) c", p=P)
            for q in range(4):
                sp.dma_start(X[:, 8 * q:8 * q + 8, :], xv[:, 8 * q:8 * q + 8, :]).then_inc(ld_x[q], 16)
            sp.dma_start(W["P"][:, :], io["L0_xattn_Wp"]).then_inc(ld_w, 16)

            def row(name):
                return io[name].rearrange("(a c) -> a c", a=1).to_broadcast([P, P])

            sp.dma_start(bvb[:, :], row("L0_xattn_bv")).then_inc(ld_b, 16)
            sp.dma_start(bcvb[:, :], row("L0_xattn_bcv")).then_inc(ld_b, 16)
            for t in range(2):
                sp.dma_start(bpb[:, t, :], row("L0_xattn_bp")).then_inc(ld_b, 16)

        @block.scalar
        def _(act):
            act.dma_start(ctxs[:, :, :], io["ctx_512"].rearrange("(o u) s c -> (u s) o c", u=2)).then_inc(ld_c, 16)
            for k, name in (("K", "Wk"), ("Q", "Wq"), ("C", "Wcq"), ("V", "Wv")):
                act.dma_start(W[k][:, :], io["L0_xattn_" + name]).then_inc(ld_w, 16)
            for k, name in (("K", "Wck"), ("V", "Wcv")):
                act.dma_start(WC[k][:, :], io["L0_xattn_" + name]).then_inc(ld_w, 16)
            act.preload_act_table(ACT.Exp)

            def low(s, kind, g):
                bank, _ = wait_full(act, s, kind, g)
                mask = lowk if kind == "K" else lowq
                nc.scalar.activation(LO[:, "KQC".index(kind), :], bank[0:NSTACK, 0:T], ACT.Identity,
                                     bias=BL[kind][:, g:g + 1], scale=mask[:, 0:1]).then_inc(low_set, 1)

            def x_high(s, g, slot):
                bank, _ = wait_full(act, s, "X", g)
                nc.scalar.copy(XR[:, slot, 0, :], bank[:, 0:T]).then_inc(xhigh_set, 1)

            def maxima(s, g, at):
                bank, free = wait_full(act, s, "M", g)
                nc.scalar.copy(QC[NSTACK:NROW, at, :, :].rearrange("p a t -> p (a t)"),
                               bank[NSTACK:NROW, :]).then_inc(free, 1)

            for i in range(2):
                bank, _ = wait_full(act, start, "CT", i)
                nc.scalar.copy(CT[0:CC, 512 * i:512 * i + 512], bank[0:CC, :]).then_inc(ctxt_set, 1)
                nc.scalar.copy(CTR[:, 0, 512 * i:512 * i + 512], bank[0:CC, :]).then_inc(ctxt_set, 1)
            x_high(start, 0, 0)
            act.wait_ge(low_masks_set, 1)
            for i in range(8):
                bank, _ = wait_full(act, start, "KC", i)
                if i >= 2:
                    wait_drained(act, start, "KC", i - 2)
                at = 2 * (i % 2)
                nc.scalar.activation(LO[:, at:at + 2, :].rearrange("p a t -> p (a t)"), bank[0:NSTACK, :], ACT.Identity,
                                     bias=BL["KC"][:, i // 2:i // 2 + 1], scale=lowk[:, 0:1]).then_inc(low_set, 1)
            wait_drained(act, start, "KC", 7)
            for g in range(NG):
                for kind in "KQC":
                    if g:
                        wait_drained(act, start, kind, g - 1)
                    low(start, kind, g)
            x_high(start, 1, 1)
            maxima(start, 0, 0)

            def body(s):
                for g in range(NG):
                    n = 4 * s.b + g
                    for h in range(2):
                        act.wait_ge(st_full, 2 * n + h + 1)
                        nc.scalar.activation(PT[:, g % 2, 1024 * h:1024 * h + 1024], ps_st[:, 1024 * h:1024 * h + 1024],
                                             ACT.Exp, scale=SCALE).then_inc(exp_done, 1)
                    if s.nxt:
                        low(s, "K", g)
                    if g == 2 or (g == 0 and s.prev):
                        act.wait_ge(pv_done, n)
                        nc.scalar.copy(NV[:, 1 - g // 2, :], ps_pv[:, :]).then_inc(nv_set, 1)
                    if g < 3 or s.nxt:
                        maxima(s, g, (4 * s.slot + g + 1) % 8)
                    if s.nxt:
                        for kind in "QC":
                            low(s, kind, g)
                    if g == 2 and s.prev:
                        bank, free = wait_full(act, s, "YT", g)
                        nc.scalar.copy(YT[:, :], bank[:, 0:T]).then_inc(free, 1)
                    if g == 2 and s.nxt2:
                        x_high(s, g, s.slot)

            sequences(act, body)
            act.wait_ge(pv_done, 4 * NB)
            nc.scalar.copy(NV[:, 1, :], ps_pv[:, :]).then_inc(nv_set, 1)
            bank, free = wait_full(act, end, "YT", 0)
            nc.scalar.copy(YT[:, :], bank[:, 0:T]).then_inc(free, 1)

        @block.gpsimd
        def _(pool):
            with nc.allow_non_contiguous_dma(reason="biases onto the stacks' rows"):
                for k, name in (("K", "bk"), ("Q", "bq"), ("C", "bcq"), ("KC", "bck")):
                    for j in range(3):
                        pool.dma_start(BS[k][GC * j:GC * j + GC, :],
                                       io["L0_xattn_" + name].rearrange("(g c) -> c g", g=NG)).then_inc(ld_s, 16)
            nc.gpsimd.memset(ones[:, :], 1.0).then_inc(zeros_set, 1)
            nc.gpsimd.memset(causal[:, :, :], 0.0).then_inc(zeros_set, 1)
            pool.wait_ge(zeros_set, 2)
            nc.gpsimd.affine_select(out=ident[:, :], in_=ones[:, :], compare_op=ALU.is_equal, fill=0.0, base=0,
                                    pattern=[[-1, P]], channel_multiplier=1).then_inc(consts_set, 1)
            nc.gpsimd.affine_select(out=causal[:, :, :], in_=causal[:, :, :], compare_op=ALU.is_ge, fill=NEG, base=0,
                                    pattern=[[0, HG], [-1, P]], channel_multiplier=1).then_inc(consts_set, 1)
            nc.gpsimd.memset(power[:, :], -0.5)
            nc.gpsimd.memset(MG[:, :, :, :], 0.0).then_inc(zeros_set, 1)
            nc.gpsimd.memset(VS[:, :, :, :, :], 0.0).then_inc(zeros_set, 1)
            nc.gpsimd.memset(VC[:, :, :, :], 0.0).then_inc(zeros_set, 1)
            pool.wait_ge(zeros_set, 5)
            pool.wait_ge(stats_set, 1)
            nc.gpsimd.tensor_scalar(rstd[:, :], mv[:, :, 1], EPS, 1.0, ALU.add, ALU.mult).then_inc(var_set, 1)
            pool.wait_ge(var_set, 1)
            nc.gpsimd.tensor_tensor(rstd[:, :], rstd[:, :], power[:, :], ALU.pow).then_inc(rstd_set, 1)
            def wait(semaphore, value):
                pool.wait_ge(semaphore, value)
                if not isinstance(value, int):
                    pool.sem_inc(waited, 1)

            def normalise(b, slot):
                at = bass.ds(2 * b, 2)
                nc.gpsimd.tensor_tensor(XN[:, slot, :, :], pair(b), rstd[:, at].unsqueeze(2).to_broadcast([P, 2, P]),
                                        ALU.mult).then_inc(xn_set, 1)
                wait(xn_set, 2 * b + 1)
                nc.gpsimd.tensor_tensor(XN[:, slot, :, :], XN[:, slot, :, :],
                                        shift[:, at].unsqueeze(2).to_broadcast([P, 2, P]), ALU.add).then_inc(xn_set, 1)
                nc.gpsimd.tensor_tensor(pair(b), pair(b), bpb[:, :, :], ALU.add).then_inc(xb_set, 1)

            def keys_by_head(s, g, n, at):
                bank, before = s.ring("K", g)
                wait(ring_free[bank], before + 1)
                for r in range(HG):
                    nc.gpsimd.tensor_scalar(KM[0:NSTACK, at, r, :], KS[:, g % 2, :], headrow[0:NSTACK, r:r + 1], 1.0,
                                            ALU.mult, ALU.mult).then_inc(km_set, 1)

            def context_keys(b, slot):
                for r in range(HG):
                    own = headrow[0:NSTACK, r:r + 1].unsqueeze(2).to_broadcast([NSTACK, NG, TC])
                    nc.gpsimd.tensor_tensor(KCM[0:NSTACK, slot, :, r, :], KC[:, :, bass.ds(TC * b, TC)], own,
                                            ALU.mult).then_inc(kcm_set, 1)

            pool.wait_ge(shift_set, 1)
            for q in range(4):
                pool.wait_ge(ld_x[q], 16)
            pool.wait_ge(ld_b, 16 * 4)
            normalise(0, 0)
            normalise(1, 1)
            pool.wait_ge(low_masks_set, 2)
            for g in range(NG):
                keys_by_head(start, g, g, g)
            wait_drained(pool, start, "KC", 7)
            context_keys(0, 0)

            def body(s):
                for g in range(NG):
                    n = 4 * s.b + g
                    for h in range(2):
                        wait(exp_done, 2 * n + h + 1)
                        if h == 0:
                            diagonal = PT[:, g % 2, 0:1024].rearrange("p (r q) -> p r q", r=HG)[:, :, 0:P]
                        else:
                            diagonal = PT[:, g % 2, 1024:1536].rearrange("p (r q) -> p r q", r=HG)
                        nc.gpsimd.affine_select(out=diagonal, in_=diagonal, compare_op=ALU.is_ge, fill=0.0, base=0,
                                                pattern=[[0, HG], [1, P]], channel_multiplier=-1).then_inc(sel_done, 1)
                    if s.nxt:
                        keys_by_head(s, g, n + 4, (4 * s.slot + g + 4) % 8)
                    if g == 0 and s.nxt:
                        context_keys(s.b + 1, 1 - s.slot)
                    if g == 0 and s.nxt2:
                        normalise(s.b + 2, s.slot)

            sequences(pool, body)

        @block.vector
        def _(dve):
            count = [0]

            def then(ins):
                count[0] += 1
                ins.then_inc(chain, 1)
                dve.wait_ge(chain, count[0])

            for q in range(4):
                dve.wait_ge(ld_x[q], 16)
                for t in range(8 * q, 8 * q + 8):
                    last = nc.vector.bn_stats(stats[:, t, :], X[:, t, :])
            then(last)
            for t in range(2 * NB):
                last = nc.vector.bn_aggr(mv[:, t, :], stats[:, t, :])
            last.then_inc(stats_set, 1)
            nc.vector.memset(lowk[:, :], 0.0)
            then(nc.vector.memset(lowq[:, :], 0.0))
            nc.vector.memset(lowk[GC:2 * GC, :], 1.0)
            then(nc.vector.memset(lowq[2 * GC:3 * GC, :], 1.0))
            dve.wait_ge(ld_b, 16 * 4)
            dve.wait_ge(ld_s, 16 * 12)
            for k in ("K", "Q", "C", "KC"):
                mask = lowk if k in ("K", "KC") else lowq
                last = nc.vector.tensor_scalar(BL[k][:, :], BS[k][:, :], mask[:, 0:1], None, ALU.mult)
            last.then_inc(low_masks_set, 1)
            dve.wait_ge(rstd_set, 1)
            nc.vector.scalar_tensor_tensor(out=shift[:, :], in0=mv[:, :, 0], scalar=-1.0, in1=rstd[:, :],
                                           op0=ALU.mult, op1=ALU.mult).then_inc(shift_set, 1)
            dve.wait_ge(consts_set, 2)
            dve.wait_ge(zeros_set, 5)
            for gp in range(2):
                v = VS[:, :, :, :, :].rearrange("p s k (a e r) c -> p (s k) a e r c", a=2, e=2)
                w = VC[:, :, :, :].rearrange("p s (a e u) c -> p s a e u c", a=2, e=2)
                for a in range(2):
                    nc.vector.memset(v[:, :, a, gp, :, 2 * HD + gp], 1.0)
                    nc.vector.memset(w[0:TC, :, a, gp, :, 2 * HD + gp], 1.0)
                    nc.vector.memset(w[TC:P, :, a, gp, :, 6 * HD + gp], 1.0)
            nc.vector.tensor_copy(identb[:, :], ident[:, :])
            nc.vector.tensor_reduce(headrow[:, :], ident[:, :].rearrange("p (j r d) -> p r j d", j=4, r=HG),
                                    AX.XY, ALU.add).then_inc(low_masks_set, 1)
            for r in range(HG):
                one = ident[NSTACK:NROW, NSTACK + r:NSTACK + r + 1].unsqueeze(2)
                nc.vector.tensor_copy(KM[NSTACK:NROW, :, r, :], one.to_broadcast([HG, 2 * NG, T]))
                nc.vector.tensor_copy(KCM[NSTACK:NROW, :, :, r, :].rearrange("p s g t -> p (s g) t"),
                                      one.to_broadcast([HG, 2 * NG, TC]))
            dve.wait_ge(ld_w, 16 * 7)
            stacks = [(WS[k], W[k], P) for k in ("K", "Q", "C")] + [(WCS, WC["K"], CC)]

            def copies(w, g, rows):
                return w[:, GC * g:GC * g + GC].unsqueeze(1).to_broadcast([rows, 3, GC])

            for ws, w, rows in stacks:
                for g in range(NG):
                    nc.vector.tensor_copy(ws[:, 0, g, :, :], copies(w, g, rows))
            then(nc.vector.tensor_copy(WV[:, 0, :], W["V"][:, :]))
            for ws, w, rows in stacks:
                for g in range(NG):
                    nc.vector.tensor_tensor(ws[:, 1, g, :, :], copies(w, g, rows), ws[:, 0, g, :, :], ALU.subtract)
            nc.vector.tensor_tensor(WV[:, 1, :], W["V"][:, :], WV[:, 0, :], ALU.subtract).then_inc(weights_set, 1)

            def x_low(s, g, b, slot):
                bank, free = wait_full(dve, s, "X", g)
                dve.wait_ge(xhigh_set, b + 1)
                nc.vector.tensor_tensor(XR[:, slot, 1, :], bank[:, 0:T], XR[:, slot, 0, :], ALU.subtract).then_inc(free, 1)

            def stack(s, kind, g, n, at):
                bank, free = wait_full(dve, s, kind, g)
                j = "KQC".index(kind)
                dve.wait_ge(low_set, 8 + 3 * n + j + 1)
                if kind == "K":
                    if not (isinstance(n, int) and n < 2):
                        dve.wait_ge(km_set, HG * (n - 1))
                    to = KS[:, g % 2, :]
                else:
                    to = QC[0:NSTACK, at, j - 1, :]
                nc.vector.scalar_tensor_tensor(out=to, in0=bank[0:NSTACK, 0:T], scalar=BS[kind][:, g:g + 1],
                                               in1=LO[:, j, :], op0=ALU.add, op1=ALU.subtract).then_inc(free, 1)

            def values(s, t, g, slot):
                bank, free = wait_full(dve, s, f"V{t}", g)
                v = bank[:, 0:P].rearrange("p (a e r d) -> p a e r d", a=2, e=2, r=HG)
                bias = bvb[:, :].rearrange("p (a e r d) -> p a e r d", a=2, e=2, r=HG)
                to = VS[:, slot, t, :, :].rearrange("p (a e r) c -> p a e r c", a=2, e=2)
                for gp in range(2):
                    last = nc.vector.tensor_tensor(to[:, :, gp, :, HD * gp:HD * gp + HD], v[:, :, gp], bias[:, :, gp], ALU.add)
                last.then_inc(free, 1)

            def context_values(b, slot):
                src = VCA[:, bass.ds(b, 1), :].rearrange("p s (a e u w d) -> p (s a) e u w d", a=2, e=2, u=2, w=2)
                to = VC[:, slot, :, :].rearrange("p (a e u) c -> p a e u c", a=2, e=2)
                for gp in range(2):
                    for w in range(2):
                        rows = slice(TC * w, TC * w + TC)
                        col = 4 * HD * w + HD * gp
                        last = nc.vector.tensor_copy(to[rows, :, gp, :, col:col + HD], src[rows, :, gp, :, w, :])
                last.then_inc(vc_set, 1)

            def maximum(s, j, g, at2):
                bank, free = wait_full(dve, s, f"S{j}", g)
                if j == 0:
                    src, to = bank[:, :].rearrange("p (r k) -> p r k", r=HG), MG[:, at2, 0, NSTACK:NROW]
                elif j < 3:
                    at = NSTACK + 2 * (j - 1)
                    src, to = bank[:, :].rearrange("p (r k) -> p r k", r=2), MG[:, at2, 1, at:at + 2]
                else:
                    src, to = (bank[:, :].rearrange("p (t r k) -> p t r k", t=2, r=HG), MG[:, at2, 2:4, NSTACK:NROW])
                nc.vector.tensor_reduce(to, src, AX.X, ALU.max, negate=True).then_inc(free, 1)

            def divide(s, a, g, b):
                bank, free = wait_full(dve, s, f"T{a}", g)
                v = bank[:, :].rearrange("p (k r w) -> p k r w", k=4, r=HG)
                nc.vector.reciprocal(RD[:, :, :, :], v[:, :, :, 2 * HD:2 * HD + 2]).then_inc(rd_set, 1)
                dve.wait_ge(rd_set, 2 * b + a + 1)
                for gp in range(2):
                    last = nc.vector.tensor_tensor(YN[:, :, gp, :, :], v[:, :, :, HD * gp:HD * gp + HD],
                                                   RD[:, :, :, gp:gp + 1].to_broadcast([P, 4, HG, HD]), ALU.mult)
                last.then_inc(free, 1)
                wait_drained(dve, s, f"T{a}", g)
                yn = YN[:, :, :, :, :].rearrange("p k e r d -> p k (e r d)")
                nc.vector.tensor_tensor(Y[:, :, 2 * GC * a:2 * GC * a + 2 * GC], yn[:, 0:2, :], yn[:, 2:4, :],
                                        ALU.add).then_inc(y_set, 1)

            def add_to_x(s, g, b):
                bank, free = wait_full(dve, s, "O", g)
                dve.wait_ge(xb_set, b + 1)
                nc.vector.tensor_tensor(pair(b), pair(b), bank[:, 0:T].rearrange("p (t c) -> p t c", t=2),
                                        ALU.add).then_inc(free, 1)

            dve.wait_ge(ctxt_set, 4)
            for i in range(2):
                bank, free = wait_full(dve, start, "CT", i)
                nc.vector.tensor_tensor(CTR[:, 1, 512 * i:512 * i + 512], bank[0:CC, :], CTR[:, 0, 512 * i:512 * i + 512],
                                        ALU.subtract).then_inc(free, 1)
            x_low(start, 0, 0, 0)
            values(start, 0, 0, 0)
            values(start, 1, 0, 0)
            for i in range(8):
                g, h = i // 2, i % 2
                bank, free = wait_full(dve, start, "KC", i)
                dve.wait_ge(low_set, i + 1)
                at = 2 * h
                nc.vector.scalar_tensor_tensor(out=KC[:, g, 512 * h:512 * h + 512], in0=bank[0:NSTACK, :],
                                               scalar=BS["KC"][:, g:g + 1],
                                               in1=LO[:, at:at + 2, :].rearrange("p a t -> p (a t)"),
                                               op0=ALU.add, op1=ALU.subtract).then_inc(free, 1)
            for g in range(NG):
                for kind in "KQC":
                    stack(start, kind, g, g, g)
            for i in range(4):
                bank, free = wait_full(dve, start, "VC", i)
                nc.vector.tensor_tensor(VCA[:, 4 * i:4 * i + 4, :], bank[:, :].rearrange("p (b c) -> p b c", b=4),
                                        bcvb[:, :].unsqueeze(1).to_broadcast([P, 4, P]), ALU.add).then_inc(free, 1)
            wait_drained(dve, start, "VC", 3)
            context_values(0, 0)
            x_low(start, 1, 1, 1)
            for n in range(2):
                for j in range(4):
                    maximum(start, j, n, n % 2)

            def body(s):
                for g in range(NG):
                    n = 4 * s.b + g
                    ahead = g < 2 or s.nxt
                    if ahead:
                        maximum(s, 0, g, g % 2)
                        maximum(s, 1, g, g % 2)
                    if g == 3 and s.prev:
                        add_to_x(s, g, s.b - 1)
                    at = (4 * s.slot + g + 4) % 8
                    if s.nxt:
                        stack(s, "K", g, n + 4, at)
                    if ahead:
                        maximum(s, 2, g, g % 2)
                    if s.nxt:
                        stack(s, "Q", g, n + 4, at)
                    if ahead:
                        maximum(s, 3, g, g % 2)
                    if s.nxt:
                        stack(s, "C", g, n + 4, at)
                    if g == 0 and s.nxt:
                        values(s, 0, g, 1 - s.slot)
                    if g == 1 and s.prev:
                        divide(s, 1, g, s.b - 1)
                    if g == 1 and s.nxt:
                        values(s, 1, g, 1 - s.slot)
                        context_values(s.b + 1, 1 - s.slot)
                    if g == 2 and s.nxt2:
                        x_low(s, g, s.b + 2, s.slot)
                    if g == 3:
                        divide(s, 0, g, s.b)

            sequences(dve, body)
            divide(end, 1, 0, NB - 1)
            add_to_x(end, 0, NB - 1)

        @block.tensor
        def _(pe):
            def take(s, name, g):
                bank, before = s.ring(name, g)
                if not (isinstance(before, int) and before == 0):
                    pe.wait_ge(ring_free[bank], before)
                return ps_ring[bank], ring_full[bank]

            def split(to, stationary, moving):
                for i, (a, b) in enumerate(((0, 0), (1, 0), (0, 1))):
                    last = nc.tensor.matmul(to, stationary(a), moving(b), start=(i == 0), stop=(i == 2))
                return last

            def transpose_x(s, g, b, slot):
                bank, full = take(s, "X", g)
                pe.wait_ge(xn_set, 2 * b + 2)
                for t in range(2):
                    last = nc.tensor.transpose(bank[:, P * t:P * t + P], XN[:, slot, t, :], ident[:, :])
                last.then_inc(full, 1)

            def project(s, kind, g, slot):
                bank, full = take(s, kind, g)
                split(bank[0:NSTACK, 0:T], lambda a: WS[kind][:, a, g, :, :].rearrange("p j c -> p (j c)"),
                      lambda b: XR[:, slot, b, :]).then_inc(full, 1)

            def project_values(s, t, g, slot):
                bank, full = take(s, f"V{t}", g)
                split(bank[:, 0:P], lambda a: XR[:, slot, a, P * t:P * t + P], lambda b: WV[:, b, :]).then_inc(full, 1)

            def scores_for_max(s, j, g, gn, n, slot, b):
                bank, full = take(s, f"S{j}", g)
                at = 4 * slot + gn
                if j == 0:
                    pe.wait_ge(km_set, HG * (n + 1))
                    nc.tensor.matmul(bank[:, :], QC[0:NSTACK, at, 0, 0:P], KM[0:NSTACK, at, :, 0:P], start=True, stop=False)
                    last = nc.tensor.matmul(bank[:, :], identb[:, :], causal[:, :, :], start=False, stop=True)
                elif j < 3:
                    r = 2 * (j - 1)
                    v = bank[:, :].rearrange("p (r k) -> p r k", r=2)
                    nc.tensor.matmul(v[:, :, P:T], identb[:, :], causal[:, 0:2, :], start=True, stop=False,
                                     skip_group_check=True)
                    last = nc.tensor.matmul(bank[:, :], QC[0:NSTACK, at, 0, P:T], KM[0:NSTACK, at, r:r + 2, :],
                                            start=False, stop=True, skip_group_check=True)
                else:
                    if gn == 0:
                        pe.wait_ge(kcm_set, HG * (b + 1))
                    for t in range(2):
                        last = nc.tensor.matmul(bank[:, T * t:T * t + T], QC[0:NSTACK, at, 1, P * t:P * t + P],
                                                KCM[0:NSTACK, slot, gn, :, :], start=True, stop=True)
                last.then_inc(full, 1)

            def transpose_max(s, g, n, at2):
                bank, full = take(s, "M", g)
                for k in range(4):
                    last = nc.tensor.transpose(bank[0:NROW, P * k:P * k + P], MG[:, at2, k, :], ident[:, :])
                last.then_inc(full, 1)

            def scores(s, g, h, n):
                at = 4 * s.slot + g
                if h == 0:
                    bank, before = s.maxima(g)
                    pe.wait_ge(ring_free[bank], before + 1)
                if not (isinstance(n, int) and n == 0):
                    pe.wait_ge(exp_done, 2 * n - 1 + h)
                if h == 0:
                    for r in range(HG):
                        last = nc.tensor.matmul(ps_st[:, T * r:T * r + T], KM[:, at, r, 0:P], QC[:, at, 0, :],
                                                start=True, stop=True)
                else:
                    for r in range(HG):
                        nc.tensor.matmul(ps_st[:, 1024 + P * r:1024 + P * r + P], KM[:, at, r, P:T], QC[:, at, 0, P:T],
                                         start=True, stop=True)
                    for u in range(2):
                        last = nc.tensor.matmul(ps_st[:, 1536 + T * u:1536 + T * u + T],
                                                KCM[:, s.slot, g, 2 * u:2 * u + 2, :].rearrange("p r t -> p (r t)"),
                                                QC[:, at, 1, :], start=True, stop=True)
                last.then_inc(st_full, 1)

            def sums(h, g, n, slot, pairs, b):
                pe.wait_ge(sel_done, 2 * n + h + 1)
                if h == 0:
                    if g % 2 == 0 and not (isinstance(pairs, int) and pairs == 0):
                        pe.wait_ge(nv_set, pairs)
                    for r in range(HG):
                        nc.tensor.matmul(ps_pv[GC * r:GC * r + GC, 0:T], VS[:, slot, 0, HG * g + r, :],
                                         PT[:, g % 2, T * r:T * r + T], start=(g % 2 == 0), stop=False,
                                         tile_position=(0, GC * r), skip_group_check=True)
                    return
                if g == 0:
                    pe.wait_ge(vc_set, b + 1)
                for r in range(HG):
                    nc.tensor.matmul(ps_pv[GC * r:GC * r + GC, P:T], VS[:, slot, 1, HG * g + r, :],
                                     PT[:, g % 2, 1024 + P * r:1024 + P * r + P], start=False, stop=(g % 2 == 1),
                                     tile_position=(0, GC * r), skip_group_check=True)
                for u in range(2):
                    last = nc.tensor.matmul(ps_pv[2 * GC * u:2 * GC * u + 2 * GC, T:2 * T], VC[:, slot, 2 * g + u, :],
                                            PT[:, g % 2, 1536 + T * u:1536 + T * u + T], start=False, stop=(g % 2 == 1),
                                            tile_position=(0, 2 * GC * u), skip_group_check=True)
                last.then_inc(pv_done, 1)

            def transpose_sums(s, a, g, b):
                bank, full = take(s, f"T{a}", g)
                pe.wait_ge(nv_set, 2 * b + a + 1)
                for k in range(4):
                    last = nc.tensor.transpose(bank[:, P * k:P * k + P], NV[:, a, P * k:P * k + P], ident[:, :])
                last.then_inc(full, 1)

            def transpose_y(s, g, b):
                bank, full = take(s, "YT", g)
                pe.wait_ge(y_set, 2 * b + 2)
                for t in range(2):
                    last = nc.tensor.transpose(bank[:, P * t:P * t + P], Y[:, t, :], ident[:, :])
                last.then_inc(full, 1)

            def project_out(s, g, gy):
                bank, full = take(s, "O", g)
                wait_drained(pe, s, "YT", gy)
                for t in range(2):
                    last = nc.tensor.matmul(bank[:, P * t:P * t + P], YT[:, P * t:P * t + P], W["P"][:, :],
                                            start=True, stop=True)
                last.then_inc(full, 1)

            pe.wait_ge(consts_set, 2)
            pe.wait_ge(ld_c, 16)
            for i in range(2):
                bank, full = take(start, "CT", i)
                for o in range(4):
                    last = nc.tensor.transpose(bank[0:CC, P * o:P * o + P], ctxs[:, 4 * i + o, :], ident[:, :])
                last.then_inc(full, 1)
            transpose_x(start, 0, 0, 0)
            pe.wait_ge(weights_set, 1)
            wait_drained(pe, start, "X", 0)
            project_values(start, 0, 0, 0)
            project_values(start, 1, 0, 0)
            for i in range(8):
                g, h = i // 2, i % 2
                bank, full = take(start, "KC", i)
                split(bank[0:NSTACK, :], lambda a: WCS[:, a, g, :, :].rearrange("p j c -> p (j c)"),
                      lambda b: CTR[:, b, 512 * h:512 * h + 512]).then_inc(full, 1)
            for g in range(NG):
                for kind in "KQC":
                    project(start, kind, g, 0)
            for i in range(4):
                bank, full = take(start, "VC", i)
                for o in range(4):
                    b = 4 * i + o
                    for w in range(2):
                        last = nc.tensor.matmul(bank[TC * w:TC * w + TC, P * o:P * o + P], CT[0:CC, TC * b:TC * b + TC],
                                                WC["V"][:, :], start=True, stop=True)
                last.then_inc(full, 1)
            transpose_x(start, 1, 1, 1)
            for n in range(2):
                for j in range(4):
                    scores_for_max(start, j, n, n, n, 0, 0)
            wait_drained(pe, start, "S3", 0)
            transpose_max(start, 0, 0, 0)

            def body(s):
                for g in range(NG):
                    n = 4 * s.b + g
                    ahead = g < 2 or s.nxt
                    gn, sn, bn = (g + 2, s.slot, s.b) if g < 2 else (g - 2, 1 - s.slot, s.b + 1)
                    gp, sp_, bp = (g - 1, s.slot, s.b) if g else (3, 1 - s.slot, s.b - 1)
                    pairs = 2 * s.b + g // 2 if g else 2 * s.b
                    before = g or s.prev

                    def ahead_scores(j):
                        if ahead:
                            scores_for_max(s, j, g, gn, n + 2, sn, bn)

                    scores(s, g, 0, n)
                    ahead_scores(0)
                    if before:
                        sums(0, gp, n - 1, sp_, pairs, bp)
                    scores(s, g, 1, n)
                    ahead_scores(1)
                    if g == 3 and s.prev:
                        project_out(s, g, 2)
                    if s.nxt:
                        project(s, "K", g, 1 - s.slot)
                    if before:
                        sums(1, gp, n - 1, sp_, pairs, bp)
                    if g < 3 or s.nxt:
                        pe.wait_ge(*max_wait(s, g))
                        transpose_max(s, g, n + 1, (g + 1) % 2)
                    ahead_scores(2)
                    if s.nxt:
                        project(s, "Q", g, 1 - s.slot)
                    ahead_scores(3)
                    if s.nxt:
                        project(s, "C", g, 1 - s.slot)
                    if g == 0 and s.nxt:
                        project_values(s, 0, g, 1 - s.slot)
                    if g == 1 and s.prev:
                        transpose_sums(s, 1, g, s.b - 1)
                    if g == 1 and s.nxt:
                        project_values(s, 1, g, 1 - s.slot)
                    if g == 2 and s.prev:
                        transpose_y(s, g, s.b - 1)
                    if g == 2 and s.nxt2:
                        transpose_x(s, g, s.b + 2, s.slot)
                    if g == 3:
                        transpose_sums(s, 0, g, s.b)

            def max_wait(s, g):
                last = WHERE[BEFORE[s.part]] if g == 0 else WHERE[s.part]
                if g == 0:
                    back = len(last) - list(last).index(("S3", 1 if s.part == "first" else 3))
                    bank, before = s.at(min(WHERE[s.part].values()) - back)
                else:
                    bank, before = s.ring("S3", g - 1)
                return ring_free[bank], before + 1

            sequences(pe, body)
            sums(0, 3, 4 * NB - 1, 1, 2 * NB - 1, NB - 1)
            sums(1, 3, 4 * NB - 1, 1, 2 * NB - 1, NB - 1)
            transpose_sums(end, 1, 0, NB - 1)
            transpose_y(end, 0, NB - 1)
            project_out(end, 0, 0)


EXPERTS = 8
CAP = max(8, int(max(1, NB * T * 2 // EXPERTS) * 1.25))
FF = 512
NF = FF // P
TILES = 2 * NB
CT_ = CAP // P
CHUNKS = CT_ // 2
ROW = P + 1
NOWHERE = 1 << 20


def wait(eng, semaphore, value):
    if not (isinstance(value, int) and value <= 0):
        eng.wait_ge(semaphore, value)


def pipeline(eng, count, depth, unroll, body):
    lo = (depth // unroll + 1) * unroll
    hi = lo + (count - lo) // unroll * unroll
    for j in range(lo):
        body(j, j % unroll, lambda s, j=j: 0 <= j - s < count)
    with eng.Fori(lo, hi - unroll + 1, unroll) as i:
        for u in range(unroll):
            body(i + u, u, lambda s: True)
    for j in range(hi, count + depth):
        body(j, j % unroll, lambda s, j=j: 0 <= j - s < count)


class Norm:

    def __init__(self, nc, st, name):
        def sb(what, shape):
            return st.enter_context(nc.sbuf_tensor(f"{name}_{what}", shape, F32))

        def sem(what):
            return st.enter_context(nc.semaphore(f"{name}_{what}"))

        self.nc = nc
        self.stats, self.mv = sb("stats", [P, 2, 2, 6]), sb("mv", [P, 2, 2, 2])
        self.rstd, self.shift = sb("rstd", [P, 2, 2]), sb("shift", [P, 2, 2])
        self.var, self.power = sb("var", [P, 2, 2]), sb("power", [P, 2])
        self.stats_set, self.mv_set, self.var_set = sem("stats_set"), sem("mv_set"), sem("var_set")
        self.rstd_set, self.shift_set, self.xn_set = sem("rstd_set"), sem("shift_set"), sem("xn_set")
        self.power_set = sem("power_set")
        self.waited = sem("waited")

    def wait(self, eng, semaphore, value):
        eng.wait_ge(semaphore, value)
        if not isinstance(value, int):
            eng.sem_inc(self.waited, 1)

    def statistics(self, x, b, slot):
        for t in range(2):
            last = self.nc.vector.bn_stats(self.stats[:, slot, t, :], x(t))
        last.then_inc(self.stats_set, 1)

    def aggregate(self, dve, b, slot):
        if not isinstance(b, int) or b > 1:
            self.wait(dve, self.shift_set, b - 1)
        self.wait(dve, self.stats_set, b + 1)
        for t in range(2):
            last = self.nc.vector.bn_aggr(self.mv[:, slot, t, :], self.stats[:, slot, t, :])
        last.then_inc(self.mv_set, 1)

    def variance(self, dve, b, slot):
        wait(dve, self.rstd_set, b - 1)
        dve.wait_ge(self.mv_set, b + 1)
        self.nc.vector.tensor_scalar(self.var[:, slot, :], self.mv[:, slot, :, 1], EPS, 1.0,
                                     ALU.add, ALU.mult).then_inc(self.var_set, 1)

    def prepare(self, pool):
        self.nc.gpsimd.memset(self.power[:, :], -0.5).then_inc(self.power_set, 1)
        pool.wait_ge(self.power_set, 1)

    def root(self, pool, b, slot):
        if not isinstance(b, int) or b > 1:
            self.wait(pool, self.xn_set, b - 1)
        self.wait(pool, self.var_set, b + 1)
        self.nc.gpsimd.tensor_tensor(self.rstd[:, slot, :], self.var[:, slot, :], self.power[:, :],
                                     ALU.pow).then_inc(self.rstd_set, 1)

    def shifts(self, dve, b, slot):
        dve.wait_ge(self.rstd_set, b + 1)
        self.nc.vector.scalar_tensor_tensor(self.shift[:, slot, :], self.mv[:, slot, :, 0], -1.0, self.rstd[:, slot, :],
                                            ALU.mult, ALU.mult).then_inc(self.shift_set, 1)

    def normalise(self, dve, x, xn, b, slot, free):
        wait(dve, *free)
        self.wait(dve, self.shift_set, b + 1)
        for t in range(2):
            last = self.nc.vector.tensor_scalar(xn(t), x(t), self.rstd[:, slot, t:t + 1], self.shift[:, slot, t:t + 1],
                                                ALU.mult, ALU.add)
        last.then_inc(self.xn_set, 1)


def ffn0(nc, io, X, CT, XT, KT, V, wrT, ident, rows_in, rows_out):
    st = ExitStack()

    def sb(name, shape, dt=F32):
        return st.enter_context(nc.sbuf_tensor(name, shape, dt))

    def sem(name):
        return st.enter_context(nc.semaphore(name))

    with st:
        X2T = sb("X2T", [P, NB, T])
        XN = sb("f_xn", [P, 2, 2, P])
        Wr, brb = sb("f_wr", [P, EXPERTS]), sb("f_brb", [NB, EXPERTS])
        sc, top = sb("f_scores", [NB, EXPERTS]), sb("f_top", [NB, 8])
        chosen = sb("f_chosen", [NB, 8], U32)
        row = sb("f_row", [1, 2 * NB], U32)
        chosen_f, numbers = sb("f_chosen_f", [NB, 2]), sb("f_numbers", [NB, 2, EXPERTS])
        picks = sb("f_picks", [NB, 2, EXPERTS])
        both = sb("f_both", [NB, EXPERTS])
        bothT = sb("f_both_t", [EXPERTS, NB])
        both_now = sb("f_both_now", [EXPERTS, 2, P])
        blank = sb("f_blank", [P, CT_, ROW])
        W1, W2 = sb("f_w1", [P, EXPERTS, P]), sb("f_w2", [P, EXPERTS, P])
        W1_now = sb("f_w1_now", [P, 2, 2, P])
        b1, b1T, b2 = sb("f_b1", [EXPERTS, P]), sb("f_b1t", [P, EXPERTS]), sb("f_b2", [EXPERTS, P])
        HT = sb("f_ht", [P, 2, 2, T])
        Wk, Wv, wr = sb("c_wk", [CC, P]), sb("c_wv", [CC + 1, P]), sb("c_wr", [EXPERTS, P])
        bk = sb("c_bk", [P, 1])
        ps_tr = [st.enter_context(nc.psum_tensor(f"f_tr{i}", [P, 512], F32)) for i in range(2)]
        ps_h = [st.enter_context(nc.psum_tensor(f"f_h{i}", [P, 512], F32)) for i in range(2)]
        ps_o = [st.enter_context(nc.psum_tensor(f"f_o{i}", [P, 512], F32)) for i in range(2)]
        ps_r = st.enter_context(nc.psum_tensor("f_r", [P, 512], F32))

        ln2, ln3 = Norm(nc, st, "ln2"), Norm(nc, st, "ln3")
        ld_r, ld_w, ld_c, ld_b, ones_set = sem("f_ld_r"), sem("f_ld_w"), sem("f_ld_c"), sem("f_ld_b"), sem("f_ones_set")
        zeros_set, zeros_out, consts_set = sem("f_zeros_set"), sem("f_zeros_out"), sem("f_consts_set")
        tr2_full, x2t_set, tr3_full, xt_set = sem("f_tr2_full"), sem("f_x2t_set"), sem("f_tr3_full"), sem("f_xt_set")
        r_full, sc_set, top_set, chosen_set, row_set = (
            sem("f_r_full"), sem("f_sc_set"), sem("f_top_set"), sem("f_chosen_set"), sem("f_row_set"))
        chosen_f_set, picks_set, both_set, both_full, both_t_set = (
            sem("f_chosen_f_set"), sem("f_picks_set"), sem("f_both_set"), sem("f_both_full"), sem("f_both_t_set"))
        w_now_set, both_now_set = sem("f_w_now_set"), sem("f_both_now_set")
        h_full, ht_set, o_full, added = sem("f_h_full"), sem("f_ht_set"), sem("f_o_full"), sem("f_added")
        c_full, c_set = sem("c_full"), sem("c_set")
        block = st.enter_context(nc.Block())
        DEPTH = 4

        @block.sync
        def _(sp):
            sp.dma_start(wr[:, :], io["L1_ffn_wr"]).then_inc(ld_c, 16)
            sp.dma_start(b1[:, :], io["L0_ffn_b1"]).then_inc(ld_c, 16)
            sp.dma_start(Wk[:, :], io["L1_xattn_Wk"]).then_inc(ld_c, 16)
            sp.dma_start(Wv[0:CC, :], io["L1_xattn_Wv"]).then_inc(ld_c, 16)
            sp.dma_start(Wv[CC:CC + 1, :], io["L1_xattn_bv"].rearrange("(a c) -> a c", a=1)).then_inc(ld_c, 16)
            with nc.allow_non_contiguous_dma(reason="a bias onto the partitions"):
                sp.dma_start(bk[:, :], io["L1_xattn_bk"].rearrange("(c a) -> c a", a=1)).then_inc(ld_b, 16)
            sp.dma_start(Wr[:, :], io["L0_ffn_Wr"]).then_inc(ld_r, 16)
            sp.dma_start(brb[:, :], io["L0_ffn_br"].rearrange("(a c) -> a c", a=1).to_broadcast([NB, EXPERTS])).then_inc(ld_r, 16)
            sp.dma_start(W1[:, :, :], io["L0_ffn_W1"].rearrange("e c d -> c e d")).then_inc(ld_w, 16)
            sp.dma_start(W2[:, :, :], io["L0_ffn_W2"].rearrange("e c d -> c e d")).then_inc(ld_w, 16)
            sp.dma_start(b2[:, :], io["L0_ffn_b2"]).then_inc(ld_w, 16)
            sp.wait_ge(chosen_set, 1)
            with nc.allow_non_contiguous_dma(reason="two of eight"):
                sp.dma_start(row[:, :], chosen[:, 0:2]).then_inc(row_set, 16)
            sp.wait_ge(zeros_set, 2)
            with sp.Fori(0, EXPERTS, 1) as e:
                sp.dma_start(rows_in[bass.ds(CAP * e, CAP), :].rearrange("(p t) c -> p t c", p=P),
                             blank[:, :, :]).then_inc(zeros_out, 16)
            with sp.Fori(0, 8, 1) as g:
                sp.dma_start(rows_out[bass.ds(8 * P * g, 8 * P), :].rearrange("(p t) c -> p t c", p=P),
                             blank[:, 0:8, 0:P]).then_inc(zeros_out, 16)
            sp.wait_ge(zeros_out, 16 * 16)

        @block.gpsimd
        def _(pool):
            nc.gpsimd.iota(numbers[:, :, :], pattern=[[0, 2], [1, EXPERTS]], base=0, channel_multiplier=0,
                           allow_small_or_imprecise_dtypes=True).then_inc(consts_set, 1)
            nc.gpsimd.memset(V[:, :, :, :], 0.0).then_inc(consts_set, 1)
            ln2.prepare(pool)
            ln3.prepare(pool)
            pipeline(pool, NB, 0, 2, lambda b, place, on: ln2.root(pool, b, place))
            nc.gpsimd.memset(blank[:, :, 0:P], 0.0).then_inc(zeros_set, 1)
            nc.gpsimd.memset(blank[:, :, P:ROW], float(NOWHERE)).then_inc(zeros_set, 1)
            pipeline(pool, NB, 0, 2, lambda b, place, on: ln3.root(pool, b, place))

        @block.scalar
        def _(act):
            act.preload_act_table(ACT.Gelu)
            act.wait_ge(c_full, 1)
            nc.scalar.copy(wrT[:, :], ps_r[:, 0:EXPERTS])
            nc.scalar.copy(b1T[:, :], ps_r[:, EXPERTS:2 * EXPERTS]).then_inc(c_set, 1)

            def normed(j, place, on):
                if on(1):
                    b, other = j - 1, 1 - place
                    act.wait_ge(ln2.shift_set, b + 1)
                    wait(act, tr2_full, b - 1)
                    for t in range(2):
                        last = nc.scalar.activation(XN[:, other, t, :], X[:, bass.ds(2 * b + t, 1), :].rearrange("p a c -> p (a c)"),
                                                    ACT.Identity, bias=ln2.shift[:, other, t:t + 1], scale=ln2.rstd[:, other, t:t + 1])
                    last.then_inc(ln2.xn_set, 1)
                if not on(2):
                    return
                j = j - 2
                act.wait_ge(tr2_full, j + 1)
                nc.scalar.copy(X2T[:, bass.ds(j, 1), :].rearrange("p a t -> p (a t)"),
                               ps_tr[place][:, 0:T]).then_inc(x2t_set, 1)

            pipeline(act, NB, 2, 2, normed)

            act.wait_ge(ld_b, 16)
            for i in range(2):
                act.wait_ge(c_full, 2 + i)
                nc.scalar.activation(KT[:, 8 * i:8 * i + 8, :].rearrange("p b t -> p (b t)"), ps_o[i][:, :], ACT.Identity,
                                     bias=bk[:, 0:1]).then_inc(c_set, 1)

            act.wait_ge(consts_set, 2)

            def values(i):
                act.wait_ge(c_full, 4 + i)
                for t in range(2):
                    half = slice(TC * t, TC * t + TC)
                    last = nc.scalar.copy(V[half, 4 * i:4 * i + 4, t, :],
                                          [*ps_h, *ps_tr][i][half, :].rearrange("p (b c) -> p b c", b=4))
                last.then_inc(c_set, 1)

            for i in range(4):
                values(i)
            act.wait_ge(both_full, 1)
            nc.scalar.copy(bothT[:, :], ps_r[0:EXPERTS, 0:NB]).then_inc(both_t_set, 1)
            act.wait_ge(ld_w, 16 * 3)
            act.wait_ge(row_set, 16)

            def expert(b, k):
                return act.value_load(row[0:1, bass.ds(2 * b + k, 1)], min_val=0, max_val=EXPERTS - 1)

            def body(j, place, on):
                other = 1 - place
                if on(0):
                    e = [expert(j, k) for k in range(2)]
                    wait(act, h_full, j - 1)
                    for k in range(2):
                        last = nc.scalar.copy(W1_now[:, place, k, :], W1[:, bass.ds(e[k], 1), :].rearrange("p a d -> p (a d)"))
                    last.then_inc(w_now_set, 1)
                if on(1):
                    b = j - 1
                    e = [expert(b, k) for k in range(2)]
                    act.wait_ge(h_full, b + 1)
                    wait(act, o_full, b - 1)
                    for k in range(2):
                        last = nc.scalar.activation(HT[:, other, k, :], ps_h[other][:, T * k:T * k + T], ACT.Gelu,
                                                    bias=b1T[:, bass.ds(e[k], 1)])
                    last.then_inc(ht_set, 1)
                if on(4):
                    b = j - 4
                    act.wait_ge(tr3_full, b + 1)
                    nc.scalar.copy(XT[:, bass.ds(b, 1), :].rearrange("p a t -> p (a t)"),
                                   ps_tr[place][:, 0:T]).then_inc(xt_set, 1)

            pipeline(act, NB, DEPTH, 2, body)

        @block.tensor
        def _(pe):
            pe.wait_ge(ld_c, 16 * 5)
            nc.tensor.transpose(ps_r[:, 0:EXPERTS], wr[:, :], ident[0:EXPERTS, 0:EXPERTS])
            nc.tensor.transpose(ps_r[:, EXPERTS:2 * EXPERTS], b1[:, :], ident[0:EXPERTS, 0:EXPERTS]).then_inc(c_full, 1)
            for i in range(2):
                nc.tensor.matmul(ps_o[i][:, :], Wk[:, :], CT[0:CC, 512 * i:512 * i + 512], start=True, stop=True).then_inc(c_full, 1)
            pe.wait_ge(ones_set, 1)

            def values(i):
                bank = [*ps_h, *ps_tr][i]
                for o in range(4):
                    b = 4 * i + o
                    for w in range(2):
                        last = nc.tensor.matmul(bank[TC * w:TC * w + TC, P * o:P * o + P], CT[:, TC * b:TC * b + TC], Wv[:, :],
                                                start=True, stop=True)
                last.then_inc(c_full, 1)

            for i in range(2):
                values(i)

            def normed(j, place, on):
                if not on(0):
                    return
                pe.wait_ge(ln2.xn_set, j + 1)
                wait(pe, x2t_set, j - 1)
                for t in range(2):
                    last = nc.tensor.transpose(ps_tr[place][:, P * t:P * t + P], XN[:, place, t, :], ident[:, :])
                last.then_inc(tr2_full, 1)

            pipeline(pe, NB, 2, 2, normed)
            pe.wait_ge(x2t_set, NB)
            pe.wait_ge(c_set, 1)
            pe.wait_ge(ld_r, 32)
            nc.tensor.matmul(ps_r[0:NB, 0:EXPERTS], X2T[:, :, 0], Wr[:, :], start=True, stop=True).then_inc(r_full, 1)
            for i in range(2, 4):
                values(i)
            pe.wait_ge(both_set, 1)
            nc.tensor.transpose(ps_r[0:EXPERTS, 0:NB], both[:, :], ident[0:NB, 0:NB]).then_inc(both_full, 1)
            pe.wait_ge(ld_w, 16 * 3)
            pe.wait_ge(row_set, 16)
            pe.wait_ge(c_set, 7)

            def body(j, place, on):
                other = 1 - place
                if on(1):
                    b = j - 1
                    pe.wait_ge(w_now_set, b + 1)
                    wait(pe, ht_set, b - 1)
                    for k in range(2):
                        last = nc.tensor.matmul(ps_h[other][:, T * k:T * k + T], W1_now[:, other, k, :],
                                                X2T[:, bass.ds(b, 1), :].rearrange("p a t -> p (a t)"), start=True, stop=True)
                    last.then_inc(h_full, 1)
                if on(2):
                    b = j - 2
                    e = [pe.value_load(row[0:1, bass.ds(2 * b + k, 1)], min_val=0, max_val=EXPERTS - 1) for k in range(2)]
                    pe.wait_ge(both_now_set, b + 1)
                    wait(pe, added, b - 1)
                    pe.wait_ge(ht_set, b + 1)
                    nc.tensor.matmul(ps_o[place][:, 0:T], both_now[:, place, :],
                                     b2[:, :].unsqueeze(1).to_broadcast([EXPERTS, 2, P]), start=True, stop=False,
                                     skip_group_check=True)
                    for k in range(2):
                        w2 = W2[:, bass.ds(e[k], 1), :].rearrange("p a d -> p (a d)")
                        for t in range(2):
                            last = nc.tensor.matmul(ps_o[place][:, P * t:P * t + P], HT[:, place, k, P * t:P * t + P], w2,
                                                    start=False, stop=(k == 1), skip_group_check=True)
                    last.then_inc(o_full, 1)
                if on(4):
                    b = j - 4
                    pe.wait_ge(ln3.xn_set, b + 1)
                    wait(pe, xt_set, b - 1)
                    for t in range(2):
                        last = nc.tensor.transpose(ps_tr[place][:, P * t:P * t + P], XN[:, place, t, :], ident[:, :])
                    last.then_inc(tr3_full, 1)

            pipeline(pe, NB, DEPTH, 2, body)

        @block.vector
        def _(dve):
            def x(b):
                return lambda t: X[:, bass.ds(2 * b + t, 1), :].rearrange("p a c -> p (a c)")

            def normed(j, place, on):
                if on(0):
                    ln2.statistics(x(j), j, place)
                if on(2):
                    ln2.shifts(dve, j - 2, place)
                if on(0):
                    ln2.aggregate(dve, j, place)
                if on(0):
                    ln2.variance(dve, j, place)

            nc.vector.memset(CT[CC:CC + 1, :], 1.0).then_inc(ones_set, 1)
            pipeline(dve, NB, 4, 2, normed)
            dve.wait_ge(r_full, 1)
            nc.vector.tensor_tensor(sc[:, :], ps_r[0:NB, 0:EXPERTS], brb[:, :], ALU.add).then_inc(sc_set, 1)
            dve.wait_ge(sc_set, 1)
            nc.vector.max(top[:, :], sc[:, :]).then_inc(top_set, 1)
            dve.wait_ge(top_set, 1)
            nc.vector.max_index(chosen[:, :], top[:, :], sc[:, :]).then_inc(chosen_set, 1)
            dve.wait_ge(chosen_set, 1)
            nc.vector.tensor_copy(chosen_f[:, :], chosen[:, 0:2]).then_inc(chosen_f_set, 1)
            dve.wait_ge(chosen_f_set, 1)
            dve.wait_ge(consts_set, 2)
            nc.vector.tensor_tensor(picks[:, :, :], numbers[:, :, :], chosen_f[:, :].unsqueeze(2).to_broadcast([NB, 2, EXPERTS]),
                                    ALU.is_equal).then_inc(picks_set, 1)
            dve.wait_ge(picks_set, 1)
            nc.vector.tensor_tensor(both[:, :], picks[:, 0, :], picks[:, 1, :], ALU.add).then_inc(both_set, 1)
            dve.wait_ge(both_t_set, 1)

            def body(j, place, on):
                other = 1 - place
                if on(1):
                    b = j - 1
                    wait(dve, o_full, b - 1)
                    nc.vector.tensor_copy(both_now[:, other, :],
                                          bothT[:, bass.ds(b, 1)].to_broadcast([EXPERTS, P])).then_inc(both_now_set, 1)
                if on(2):
                    b = j - 2
                    dve.wait_ge(o_full, b + 1)
                    at = X[:, bass.ds(2 * b, 2), :].rearrange("p a c -> p (a c)")
                    nc.vector.scalar_tensor_tensor(at, ps_o[place][:, 0:T], 0.5, at, ALU.mult, ALU.add).then_inc(added, 1)
                if on(3):
                    ln3.shifts(dve, j - 3, other)
                if on(2):
                    ln3.wait(dve, added, j - 1)
                    ln3.statistics(x(j - 2), j - 2, place)
                if on(3):
                    b = j - 3
                    ln3.normalise(dve, x(b), lambda t: XN[:, other, t, :], b, other, (tr3_full, b - 1))
                if on(2):
                    ln3.aggregate(dve, j - 2, place)
                    ln3.variance(dve, j - 2, place)

            pipeline(dve, NB, DEPTH, 2, body)


def attention1(nc, io, X, XT, KT, V, wrT, TOPS, LATE, ident, rows_in):
    st = ExitStack()

    def sb(name, shape, dt=F32):
        return st.enter_context(nc.sbuf_tensor(name, shape, dt))

    def sem(name):
        return st.enter_context(nc.semaphore(name))

    with st:
        X4 = sb("X4", [P, TILES, P])
        logits = sb("a_logits", [P, 2, 2, EXPERTS])
        top, picked = sb("a_top", [P, 2, 2, 8]), sb("a_picked", [P, 2, 2, 8], U32)
        expert = sb("a_expert", [P, 2, 2, 2])
        numbers = sb("a_numbers", [P, 2, 2, EXPERTS])
        own = sb("a_own", [P, 2, 2, 2, EXPERTS])
        mask = sb("a_mask", [P, 2, 2, EXPERTS], BF16)
        ones_f, onesb = sb("a_ones", [P, P]), sb("a_onesb", [P, P], BF16)
        before = sb("a_before", [P, P], BF16)
        carried = sb("a_carried", [P, 2, EXPERTS])
        position = sb("a_position", [P, 2, 2, EXPERTS])
        place_of, late, to_f = (sb("a_" + n, [P, 2, 2, 2]) for n in ("place_of", "late", "to_f"))
        to = sb("a_to", [P, 2, 2, 2], U32)
        home = sb("a_home", [P, 2, TILES])
        rows = sb("a_rows", [P, 2, 2, 2, ROW])
        Wq, bq = sb("a_wq", [P, P]), sb("a_bq", [P, 1])
        QT = sb("a_qt", [P, 2, T])
        negmax, total, inverse = sb("a_negmax", [P, 2, 2]), sb("a_total", [P, 2, 2]), sb("a_inverse", [P, 2, 2])
        E, ET = sb("a_e", [P, 2, 2 * TC]), sb("a_et", [P, 2, P])
        XN4S = sb("a_xn4", [P, 2, 2, P])
        XN4T = sb("a_x4t", [P, 2, T])
        ps_q, ps_e, ps_x, ps_l = (st.enter_context(nc.psum_tensor(f"a_ps_{k}", [P, 512], F32)) for k in "qexl")
        ps_s = [st.enter_context(nc.psum_tensor(f"a_ps_s{i}", [P, 512], F32)) for i in range(2)]
        ps_o, ps_p = (st.enter_context(nc.psum_tensor(f"a_ps_{k}", [P, 512], F32)) for k in "op")
        ln4 = Norm(nc, st, "ln4")
        ld_a, q_full, qt_set = sem("a_ld"), sem("a_q_full"), sem("a_qt_set")
        s_full, max_set, exp_set, e_full, et_set = sem("a_s_full"), sem("a_max_set"), sem("a_exp_set"), sem("a_e_full"), sem("a_et_set")
        inverse_set, o_full, added = sem("a_inverse_set"), sem("a_o_full"), sem("a_added")
        x_full, xt_set, l_full, l_set = sem("a_x_full"), sem("a_xt_set"), sem("a_l_full"), sem("a_l_set")
        ones_set, consts_set, top_set, picked_set, expert_set = (
            sem("a_ones_set"), sem("a_consts_set"), sem("a_top_set"), sem("a_picked_set"), sem("a_expert_set"))
        own_set, mask_set, p_full, p_read, share_set = (
            sem("a_own_set"), sem("a_mask_set"), sem("a_p_full"), sem("a_p_read"), sem("a_share_set"))
        place_set, to_f_set, to_set, rows_set = sem("a_place_set"), sem("a_to_f_set"), sem("a_to_set"), sem("a_rows_set")
        scattered = [sem(f"a_scattered{i}") for i in range(2)]
        block = st.enter_context(nc.Block())
        DEPTH = 8

        def scatters(b, slot):
            return 32 * (b - slot) + 64

        @block.sync
        def _(sp):
            sp.dma_start(Wq[:, :], io["L1_xattn_Wq"]).then_inc(ld_a, 16)
            with nc.allow_non_contiguous_dma(reason="a bias onto the partitions"):
                sp.dma_start(bq[:, :], io["L1_xattn_bq"].rearrange("(c a) -> c a", a=1)).then_inc(ld_a, 16)

        @block.gpsimd
        def _(pool):
            nc.gpsimd.memset(ones_f[:, :], 1.0).then_inc(ones_set, 1)
            nc.gpsimd.memset(carried[:, :, :], 0.0).then_inc(consts_set, 1)
            nc.gpsimd.iota(numbers[:, :, :, :], pattern=[[0, 4], [1, EXPERTS]], base=0, channel_multiplier=0,
                           allow_small_or_imprecise_dtypes=True).then_inc(consts_set, 1)
            nc.gpsimd.iota(home[:, :, :], pattern=[[NB * T, 2], [P, TILES]], base=0, channel_multiplier=1,
                           allow_small_or_imprecise_dtypes=True).then_inc(consts_set, 1)
            pool.wait_ge(ones_set, 1)
            nc.gpsimd.affine_select(out=before[:, :], in_=ones_f[:, :], compare_op=ALU.is_gt, fill=0.0, base=0,
                                    pattern=[[1, P]], channel_multiplier=-1).then_inc(consts_set, 1)
            nc.gpsimd.affine_select(out=onesb[:, :], in_=ones_f[:, :], compare_op=ALU.is_ge, fill=1.0, base=0,
                                    pattern=[[1, P]], channel_multiplier=0).then_inc(consts_set, 1)
            ln4.prepare(pool)

            def body(j, place, on):
                if on(0):
                    ln4.root(pool, j, place)
                if on(5):
                    b, slot = j - 5, 1 - place
                    ln4.wait(pool, rows_set, b + 1)
                    ln4.wait(pool, to_set, b + 1)
                    for k in range(2):
                        for t in range(2):
                            nc.gpsimd.indirect_dma_start(
                                out=rows_in, out_offset=bass.IndirectOffsetOnAxis(to[:, slot, k, t:t + 1], 0),
                                in_=rows[:, slot, k, t, :], in_offset=None, bounds_check=EXPERTS * CAP - 1,
                                oob_is_err=False).then_inc(scattered[slot], 16)

            pipeline(pool, NB, 5, 2, body)
            for i in range(2):
                pool.wait_ge(scattered[i], scatters(NB - 2 + i, i))

        @block.scalar
        def _(act):
            act.preload_act_table(ACT.Exp)
            act.wait_ge(consts_set, 5)
            act.wait_ge(ld_a, 32)

            def body(j, place, on):
                other = 1 - place
                if on(0):
                    act.wait_ge(q_full, j + 1)
                    wait(act, s_full, j - 1)
                    nc.scalar.activation(QT[:, place, :], ps_q[:, 0:T], ACT.Identity,
                                         bias=bq[:, 0:1]).then_inc(qt_set, 1)
                if on(1):
                    b = j - 1
                    act.wait_ge(max_set, b + 1)
                    wait(act, e_full, b - 1)
                    wait(act, inverse_set, b - 1)
                    for t in range(2):
                        last = nc.scalar.activation(E[:, other, TC * t:TC * t + TC], ps_s[other][:, TC * t:TC * t + TC], ACT.Exp,
                                                    bias=negmax[:, other, t:t + 1], accum_out=total[:, other, t:t + 1])
                    last.then_inc(exp_set, 1)
                if on(2):
                    b = j - 2
                    act.wait_ge(e_full, b + 1)
                    wait(act, o_full, b - 1)
                    nc.scalar.copy(ET[:, place, :], ps_e[:, 0:P]).then_inc(et_set, 1)
                if on(5):
                    b = j - 5
                    act.wait_ge(x_full, b + 1)
                    nc.scalar.copy(X4[:, bass.ds(2 * b, 2), :], XN4S[:, other, :, :])
                    wait(act, l_full, b - 1)
                    nc.scalar.copy(XN4T[:, other, :], ps_x[:, 0:T]).then_inc(xt_set, 1)
                if on(7):
                    b = j - 7
                    wait(act, scattered[other], scatters(b - 2, other) if not isinstance(b, int) or b > 1 else 0)
                    nc.scalar.copy(rows[:, other, :, :, 0:P], X4[:, bass.ds(2 * b, 2), :].unsqueeze(1).to_broadcast([P, 2, 2, P]))
                    nc.scalar.copy(rows[:, other, :, :, P], home[:, :, bass.ds(2 * b, 2)]).then_inc(rows_set, 1)

            pipeline(act, NB, DEPTH, 2, body)

        @block.tensor
        def _(pe):
            pe.wait_ge(ld_a, 32)
            pe.wait_ge(consts_set, 5)

            def body(j, place, on):
                other = 1 - place
                if on(0):
                    wait(pe, qt_set, j)
                    nc.tensor.matmul(ps_q[:, 0:T], Wq[:, :], XT[:, bass.ds(j, 1), :].rearrange("p a t -> p (a t)"),
                                     start=True, stop=True).then_inc(q_full, 1)
                if on(1):
                    b = j - 1
                    pe.wait_ge(qt_set, b + 1)
                    wait(pe, exp_set, b - 1)
                    for t in range(2):
                        last = nc.tensor.matmul(ps_s[other][:, TC * t:TC * t + TC], QT[:, other, P * t:P * t + P],
                                                KT[:, bass.ds(b, 1), :].rearrange("p a t -> p (a t)"), start=True, stop=True)
                    last.then_inc(s_full, 1)
                if on(2):
                    b = j - 2
                    pe.wait_ge(exp_set, b + 1)
                    wait(pe, et_set, b)
                    nc.tensor.transpose(ps_e[:, 0:P], E[:, place, :], ident[:, :]).then_inc(e_full, 1)
                if on(3):
                    b = j - 3
                    pe.wait_ge(et_set, b + 1)
                    wait(pe, added, b)
                    nc.tensor.matmul(ps_o[:, 0:T], ET[:, other, :], V[:, bass.ds(b, 1), :, :].rearrange("p a t c -> p (a t c)"),
                                     start=True, stop=True).then_inc(o_full, 1)
                if on(5):
                    b = j - 5
                    pe.wait_ge(ln4.xn_set, b + 1)
                    wait(pe, xt_set, b)
                    for t in range(2):
                        last = nc.tensor.transpose(ps_x[:, P * t:P * t + P], XN4S[:, other, t, :], ident[:, :])
                    last.then_inc(x_full, 1)
                if on(6):
                    b = j - 6
                    pe.wait_ge(xt_set, b + 1)
                    wait(pe, l_set, b)
                    for t in range(2):
                        last = nc.tensor.matmul(ps_l[:, 8 * t:8 * t + 8], XN4T[:, place, P * t:P * t + P], wrT[:, :],
                                                start=True, stop=True)
                    last.then_inc(l_full, 1)
                if on(8):
                    b = j - 8
                    pe.wait_ge(mask_set, b + 1)
                    wait(pe, p_read, b)
                    first, second = mask[:, place, 0, :], mask[:, place, 1, :]
                    nc.tensor.matmul(ps_p[:, 0:8], before[:, :], first, start=True, stop=True)
                    nc.tensor.matmul(ps_p[:, 8:16], before[:, :], second, start=True, stop=False)
                    nc.tensor.matmul(ps_p[:, 8:16], onesb[:, :], first, start=False, stop=True)
                    nc.tensor.matmul(ps_p[:, 16:24], onesb[:, :], first, start=True, stop=False)
                    nc.tensor.matmul(ps_p[:, 16:24], onesb[:, :], second, start=False, stop=True).then_inc(p_full, 1)

            pipeline(pe, NB, DEPTH, 2, body)

        @block.vector
        def _(dve):
            dve.wait_ge(consts_set, 5)

            def x(b):
                return lambda t: X[:, bass.ds(2 * b + t, 1), :].rearrange("p a c -> p (a c)")

            def body(j, place, on):
                other = 1 - place
                if on(1):
                    b = j - 1
                    dve.wait_ge(s_full, b + 1)
                    wait(dve, exp_set, b - 1)
                    nc.vector.tensor_reduce(negmax[:, other, :], ps_s[other][:, 0:P].rearrange("p (t k) -> p t k", t=2), AX.X, ALU.max,
                                            negate=True).then_inc(max_set, 1)
                if on(3):
                    b = j - 3
                    dve.wait_ge(exp_set, b + 1)
                    nc.vector.reciprocal(inverse[:, other, :], total[:, other, :]).then_inc(inverse_set, 1)
                    dve.wait_ge(inverse_set, b + 1)
                    dve.wait_ge(o_full, b + 1)
                    for t in range(2):
                        at = X[:, bass.ds(2 * b + t, 1), :].rearrange("p a c -> p (a c)")
                        last = nc.vector.scalar_tensor_tensor(at, ps_o[:, P * t:P * t + P], inverse[:, other, t:t + 1], at,
                                                              ALU.mult, ALU.add)
                    last.then_inc(added, 1)
                    ln4.wait(dve, added, b + 1)
                    ln4.statistics(x(b), b, other)
                if on(4):
                    ln4.shifts(dve, j - 4, place)
                if on(3):
                    ln4.aggregate(dve, j - 3, other)
                if on(4):
                    b = j - 4
                    ln4.normalise(dve, x(b), lambda t: XN4S[:, place, t, :], b, place, (xt_set, b - 1))
                if on(3):
                    ln4.variance(dve, j - 3, other)
                if on(6):
                    b = j - 6
                    dve.wait_ge(l_full, b + 1)
                    nc.vector.tensor_copy(logits[:, place, :, :], ps_l[:, 0:16].rearrange("p (t e) -> p t e", t=2)).then_inc(l_set, 1)
                if on(8):
                    b = j - 8
                    dve.wait_ge(p_full, b + 1)
                    nc.vector.tensor_tensor(carried[:, other, :], carried[:, place, :], ps_p[:, 16:24], ALU.add)
                    nc.vector.tensor_tensor(position[:, place, :, :], ps_p[:, 0:16].rearrange("p (t e) -> p t e", t=2),
                                            carried[:, place, :].unsqueeze(1).to_broadcast([P, 2, EXPERTS]),
                                            ALU.add).then_inc(p_read, 1)
                if on(7):
                    b = j - 7
                    ln4.wait(dve, l_set, b + 1)
                    for t in range(2):
                        last = nc.vector.max(top[:, other, t, :], logits[:, other, t, :])
                    last.then_inc(top_set, 1)
                if on(8):
                    b = j - 8
                    dve.wait_ge(p_read, b + 1)
                    nc.vector.tensor_tensor(own[:, place, :, :, :], own[:, place, :, :, :],
                                            position[:, place, :, :].unsqueeze(1).to_broadcast([P, 2, 2, EXPERTS]),
                                            ALU.mult).then_inc(share_set, 1)
                if on(7):
                    b = j - 7
                    ln4.wait(dve, top_set, b + 1)
                    for t in range(2):
                        last = nc.vector.max_index(picked[:, other, t, :], top[:, other, t, :], logits[:, other, t, :])
                    last.then_inc(picked_set, 1)
                if on(8):
                    b = j - 8
                    dve.wait_ge(share_set, b + 1)
                    nc.vector.tensor_reduce(place_of[:, place, :, :], own[:, place, :, :, :], AX.X, ALU.add).then_inc(place_set, 1)
                if on(7):
                    b = j - 7
                    nc.vector.tensor_copy(TOPS[:, bass.ds(2 * b, 2), :], top[:, other, :, 0:2])
                    dve.wait_ge(picked_set, b + 1)
                    nc.vector.tensor_copy(expert[:, other, :, :].rearrange("p k t -> p t k"),
                                          picked[:, other, :, 0:2]).then_inc(expert_set, 1)
                if on(8):
                    b = j - 8
                    dve.wait_ge(place_set, b + 1)
                    nc.vector.tensor_scalar(late[:, place, :, :], place_of[:, place, :, :], float(CAP) - 0.5, 0.0, ALU.is_gt, ALU.add)
                    nc.vector.scalar_tensor_tensor(to_f[:, place, :, :], expert[:, place, :, :], float(CAP),
                                                   place_of[:, place, :, :], ALU.mult, ALU.add).then_inc(to_f_set, 1)
                if on(7):
                    b = j - 7
                    dve.wait_ge(expert_set, b + 1)
                    nc.vector.tensor_tensor(own[:, other, :, :, :], numbers[:, :, :, :],
                                            expert[:, other, :, :].unsqueeze(3).to_broadcast([P, 2, 2, EXPERTS]),
                                            ALU.is_equal).then_inc(own_set, 1)
                if on(8):
                    b = j - 8
                    dve.wait_ge(to_f_set, b + 1)
                    nc.vector.tensor_copy(LATE[:, :, bass.ds(2 * b, 2)], late[:, place, :, :])
                    wait(dve, scattered[place], scatters(b - 2, place) if not isinstance(b, int) or b > 1 else 0)
                    nc.vector.scalar_tensor_tensor(to[:, place, :, :], late[:, place, :, :], float(NOWHERE), to_f[:, place, :, :],
                                                   ALU.mult, ALU.add).then_inc(to_set, 1)
                if on(7):
                    b = j - 7
                    wait(dve, p_full, b - 1)
                    dve.wait_ge(own_set, b + 1)
                    nc.vector.tensor_tensor(mask[:, other, :, :], own[:, other, 0, :, :], own[:, other, 1, :, :],
                                            ALU.add).then_inc(mask_set, 1)

            pipeline(dve, NB, DEPTH, 2, body)


def moe(nc, io, out, X, TOPS, LATE, ident, rows_in, rows_out):
    st = ExitStack()

    def sb(name, shape, dt=F32):
        return st.enter_context(nc.sbuf_tensor(name, shape, dt))

    def sem(name):
        return st.enter_context(nc.semaphore(name))

    with st:
        gate = sb("m_gate", [P, 2, TILES])
        gap, grown, denominator = sb("m_gap", [P, TILES]), sb("m_grown", [P, TILES]), sb("m_denominator", [P, TILES])
        home = sb("m_home", [P, 2, CT_], U32)
        back = sb("m_back", [P, 4, 2, 4, P])
        b1r, b1T = sb("m_b1r", [EXPERTS * NF, P]), sb("m_b1t", [P, EXPERTS * NF])
        w1, w2 = sb("m_w1", [P, 2, FF]), sb("m_w2", [P, 2, NF, P])
        b2b = sb("m_b2b", [P, 2, 2, P])
        b1c = sb("m_b1c", [P, 2, NF])
        XG = sb("m_xg", [P, 2, CT_, ROW])
        XGT = sb("m_xgt", [P, 2, CAP])
        HT = sb("m_ht", [P, 2, NF, T])
        Y = sb("m_y", [P, 2, CT_, P])
        ps_h = [st.enter_context(nc.psum_tensor(f"m_h{i}", [P, NF, T], F32)) for i in range(2)]
        ps_y = [st.enter_context(nc.psum_tensor(f"m_y{i}", [P, 512], F32)) for i in range(2)]
        ps_t = [st.enter_context(nc.psum_tensor(f"m_t{i}", [P, 512], F32)) for i in range(2)]

        chain = sem("m_chain")
        gap_set, grown_set, home_set = sem("m_gap_set"), sem("m_grown_set"), sem("m_home_set")
        ld_b, b1_full, b1_set = sem("m_ld_b"), sem("m_b1_full"), sem("m_b1_set")
        ld_w, ld_x = [sem(f"m_ld_w{i}") for i in range(2)], [sem(f"m_ld_x{i}") for i in range(2)]
        t_full, xgt_set, h_full, ht_set = sem("m_t_full"), sem("m_xgt_set"), sem("m_h_full"), sem("m_ht_set")
        y_full, y_set, y_sent = sem("m_y_full"), sem("m_y_set"), [sem(f"m_y_sent{i}") for i in range(2)]
        ld_back, half_added, added = [sem(f"m_ld_back{i}") for i in range(4)], sem("m_half_added"), sem("m_added")
        all_sent = sem("m_all_sent")
        stored = sem("m_stored")
        waited = sem("m_waited")
        block = st.enter_context(nc.Block())
        ALL = EXPERTS * CHUNKS

        def rows(x, e):
            return x[bass.ds(CAP * e, CAP), :].rearrange("(t p) c -> p t c", p=P)

        @block.sync
        def _(sp):
            sp.dma_start(b1r[:, :], io["L1_ffn_b1"].rearrange("e (f c) -> (e f) c", c=P)).then_inc(ld_b, 16)

            def load_weights(e, slot):
                wait(sp, y_full, CHUNKS * (e - 1))
                sp.dma_start(w1[:, slot, :], io["L1_ffn_w1"][bass.ds(e, 1), :, :].rearrange("a c f -> (a c) f")).then_inc(ld_w[slot], 16)
                sp.dma_start(w2[:, slot, :, :], io["L1_ffn_w2"][bass.ds(e, 1), :, :].rearrange("a (f p) c -> p (a f) c", p=P)).then_inc(ld_w[slot], 16)
                wait(sp, y_set, CHUNKS * (e - 1))
                for t in range(2):
                    sp.dma_start(b2b[:, slot, t, :], io["L1_ffn_b2"][bass.ds(e, 1), :].to_broadcast([P, P])).then_inc(ld_w[slot], 16)

            def load_tokens(e, slot):
                wait(sp, xgt_set, CHUNKS * (e - 1))
                wait(sp, home_set, e - 1)
                sp.dma_start(XG[:, slot, :, :], rows(rows_in, e)).then_inc(ld_x[slot], 16)

            load_weights(0, 0)
            load_weights(1, 1)
            load_tokens(0, 0)
            load_tokens(1, 1)
            with sp.Fori(2, EXPERTS - 1, 2) as e:
                for u in range(2):
                    load_tokens(e + u, u)
                    load_weights(e + u, u)
            ov = out.rearrange("b (t p) c -> p (b t) c", p=P)

            def load_back(g, slot):
                for k in range(2):
                    sp.dma_start(back[:, slot, k, :, :],
                                 rows_out[bass.ds(NB * T * k + 4 * P * g, 4 * P), :].rearrange("(t p) c -> p t c", p=P)).then_inc(ld_back[slot], 16)

            sp.wait_ge(all_sent, 1)
            for g in range(4):
                load_back(g, g)
            for g in range(8):
                sp.wait_ge(added, g + 1)
                if g < 4:
                    load_back(g + 4, g)
                sp.dma_start(ov[:, 4 * g:4 * g + 4, :], X[:, 4 * g:4 * g + 4, :]).then_inc(stored, 16)
            sp.wait_ge(stored, 16 * 8)

        @block.gpsimd
        def _(pool):
            def send(e, slot):
                for c in range(CHUNKS):
                    pool.wait_ge(y_set, CHUNKS * e + c + 1)
                    if not isinstance(e, int):
                        pool.sem_inc(waited, 1)
                    for t in range(2 * c, 2 * c + 2):
                        nc.gpsimd.indirect_dma_start(
                            out=rows_out, out_offset=bass.IndirectOffsetOnAxis(home[:, slot, t:t + 1], 0),
                            in_=Y[:, slot, t, :], in_offset=None, bounds_check=2 * NB * T - 1,
                            oob_is_err=False).then_inc(y_sent[slot], 16)

            with pool.Fori(0, EXPERTS - 1, 2) as e:
                for u in range(2):
                    send(e + u, u)
            for i in range(2):
                pool.wait_ge(y_sent[i], 16 * CT_ * (EXPERTS // 2))
            pool.sem_inc(all_sent, 1)

        @block.scalar
        def _(act):
            act.preload_act_table(ACT.Exp)
            act.wait_ge(gap_set, 1)
            nc.scalar.activation(grown[:, :], gap[:, :], ACT.Exp).then_inc(grown_set, 1)
            act.preload_act_table(ACT.Gelu_apprx_tanh)

            def body(e, slot):
                for c in range(CHUNKS):
                    m, s2 = CHUNKS * e + c, (slot + c) % 2
                    act.wait_ge(h_full, m + 1)
                    wait(act, y_full, m - 1)
                    act.wait_ge(b1_set, e + 2)
                    for f in range(NF):
                        last = nc.scalar.activation(HT[:, s2, f, :], ps_h[s2][:, f, :], ACT.Gelu_apprx_tanh,
                                                    bias=b1c[:, slot, f:f + 1])
                    last.then_inc(ht_set, 1)

            body(0, 0)
            body(1, 1)
            with act.Fori(2, EXPERTS - 1, 2) as e:
                for u in range(2):
                    body(e + u, u)

        @block.tensor
        def _(pe):
            pe.wait_ge(ld_b, 16)
            nc.tensor.transpose(ps_y[0][:, 0:EXPERTS * NF], b1r[:, :], ident[0:EXPERTS * NF, 0:EXPERTS * NF]).then_inc(b1_full, 1)
            pe.wait_ge(b1_set, 1)

            def transpose_rows(m, e, c, slot, s2):
                if c == 0:
                    pe.wait_ge(ld_x[slot], 8 * (e - slot) + 16)
                wait(pe, xgt_set, m - 1)
                for t in range(2):
                    last = nc.tensor.transpose(ps_t[s2][:, P * t:P * t + P], XG[:, slot, 2 * c + t, 0:P], ident[:, :])
                last.then_inc(t_full, 1)

            def hidden(m, e, c, slot, s2):
                pe.wait_ge(xgt_set, m + 1)
                if c == 0:
                    pe.wait_ge(ld_w[slot], 32 * (e - slot) + 64)
                wait(pe, ht_set, m - 1)
                for f in range(NF):
                    last = nc.tensor.matmul(ps_h[s2][:, f, :], w1[:, slot, P * f:P * f + P], XGT[:, slot, T * c:T * c + T],
                                            start=True, stop=True)
                last.then_inc(h_full, 1)

            def outputs(m, slot, s2):
                pe.wait_ge(ht_set, m + 1)
                wait(pe, y_set, m - 1)
                for t in range(2):
                    for f in range(NF):
                        last = nc.tensor.matmul(ps_y[s2][:, P * t:P * t + P], HT[:, s2, f, P * t:P * t + P], w2[:, slot, f, :],
                                                start=(f == 0), stop=(f == NF - 1))
                last.then_inc(y_full, 1)

            def body(e, slot, first=False, final=False):
                for c in range(CHUNKS):
                    m, s2 = CHUNKS * e + c, (slot + c) % 2
                    hidden(m, e, c, slot, s2)
                    if not final:
                        transpose_rows(m + CHUNKS, e + 1, c, 1 - slot, 1 - s2)
                    if not (first and c == 0):
                        outputs(m - 1, slot if c else 1 - slot, 1 - s2)

            for c in range(CHUNKS):
                transpose_rows(c, 0, c, 0, c % 2)
            body(0, 0, first=True)
            with pe.Fori(1, EXPERTS - 2, 2) as e:
                body(e, 1)
                body(e + 1, 0)
            body(EXPERTS - 1, 1, final=True)
            outputs(ALL - 1, 1, (ALL - 1) % 2)

        @block.vector
        def _(dve):
            count = [0]

            def then(ins):
                count[0] += 1
                ins.then_inc(chain, 1)
                dve.wait_ge(chain, count[0])

            nc.vector.tensor_tensor(gap[:, :], TOPS[:, :, 1], TOPS[:, :, 0], ALU.subtract).then_inc(gap_set, 1)
            dve.wait_ge(b1_full, 1)
            nc.vector.tensor_copy(b1T[:, :], ps_y[0][:, 0:EXPERTS * NF]).then_inc(b1_set, 1)
            dve.wait_ge(grown_set, 1)
            then(nc.vector.tensor_scalar(denominator[:, :], grown[:, :], 1.0, 0.0, ALU.add, ALU.add))
            then(nc.vector.reciprocal(denominator[:, :], denominator[:, :]))
            nc.vector.tensor_copy(gate[:, 0, :], denominator[:, :])
            nc.vector.tensor_tensor(gate[:, 1, :], grown[:, :], denominator[:, :], ALU.mult)
            then(nc.vector.tensor_scalar(LATE[:, :, :], LATE[:, :, :], -1.0, 1.0, ALU.mult, ALU.add))
            then(nc.vector.tensor_tensor(gate[:, :, :], gate[:, :, :], LATE[:, :, :], ALU.mult))
            def drain_rows(m, c, slot, s2):
                dve.wait_ge(t_full, m + 1)
                nc.vector.tensor_copy(XGT[:, slot, T * c:T * c + T], ps_t[s2][:, 0:T]).then_inc(xgt_set, 1)

            def drain_outputs(m, e, c, slot, s2):
                dve.wait_ge(y_full, m + 1)
                if c == 0:
                    wait(dve, y_sent[slot], 8 * CT_ * (e - slot))
                    nc.vector.tensor_copy(home[:, slot, :], XG[:, slot, :, P]).then_inc(home_set, 1)
                nc.vector.tensor_tensor(Y[:, slot, 2 * c:2 * c + 2, :].rearrange("p t c -> p (t c)"), ps_y[s2][:, 0:T],
                                        b2b[:, slot, :, :].rearrange("p t c -> p (t c)"), ALU.add).then_inc(y_set, 1)

            def bias(e, slot):
                nc.vector.tensor_copy(b1c[:, slot, :], b1T[:, bass.ds(NF * e, NF)]).then_inc(b1_set, 1)

            def body(e, slot, final=False):
                for c in range(CHUNKS):
                    m, s2 = CHUNKS * e + c, (slot + c) % 2
                    if not final:
                        drain_rows(m + CHUNKS, c, 1 - slot, 1 - s2)
                    drain_outputs(m, e, c, slot, s2)
                if not final:
                    bias(e + 2, slot) if not (isinstance(e, int) and e + 2 >= EXPERTS) else None

            dve.wait_ge(b1_set, 1)
            bias(0, 0)
            bias(1, 1)
            for c in range(CHUNKS):
                drain_rows(c, c, 0, c % 2)
            body(0, 0)
            body(1, 1)
            with dve.Fori(2, EXPERTS - 3, 2) as e:
                for u in range(2):
                    body(e + u, u)
            body(EXPERTS - 2, 0)
            body(EXPERTS - 1, 1, final=True)

            def combine(g, slot):
                dve.wait_ge(ld_back[slot], 8 * (g - slot) + 32)
                for k in range(2):
                    for t in range(4):
                        at = X[:, bass.ds(4 * g + t, 1), :].rearrange("p a c -> p (a c)")
                        last = nc.vector.scalar_tensor_tensor(at, back[:, slot, k, t, :], gate[:, k, bass.ds(4 * g + t, 1)],
                                                              at, ALU.mult, ALU.add)
                    last.then_inc(half_added if k == 0 else added, 1)
                    if k == 0:
                        dve.wait_ge(half_added, g + 1)

            with dve.Fori(0, 5, 4) as g:
                for u in range(4):
                    combine(g + u, u)


def program(nc, io, out):
    with ExitStack() as ctx:
        X = ctx.enter_context(nc.sbuf_tensor("X", [P, 2 * NB, P], F32))
        ident = ctx.enter_context(nc.sbuf_tensor("ident", [P, P], F32))
        CT = ctx.enter_context(nc.sbuf_tensor("CT", [CC + 1, NB * TC], F32))
        identb = ctx.enter_context(nc.sbuf_tensor("identb", [P, P], BF16))
        rows_in = nc.dram_tensor("expert_rows", (EXPERTS * CAP, ROW), F32).ap()
        rows_out = nc.dram_tensor("expert_outputs", (2 * NB * T, P), F32).ap()
        attention0(nc, io, X, CT, ident, identb)
        TOPS = ctx.enter_context(nc.sbuf_tensor("TOPS", [P, TILES, 2], F32))
        LATE = ctx.enter_context(nc.sbuf_tensor("LATE", [P, 2, TILES], F32))
        with ExitStack() as st:
            XT = st.enter_context(nc.sbuf_tensor("XT", [P, NB, T], F32))
            KT = st.enter_context(nc.sbuf_tensor("KT", [P, NB, TC], F32))
            V = st.enter_context(nc.sbuf_tensor("V", [P, NB, 2, P], F32))
            wrT = st.enter_context(nc.sbuf_tensor("wrT", [P, EXPERTS], F32))
            ffn0(nc, io, X, CT, XT, KT, V, wrT, ident, rows_in, rows_out)
            attention1(nc, io, X, XT, KT, V, wrT, TOPS, LATE, ident, rows_in)
        moe(nc, io, out, X, TOPS, LATE, ident, rows_in, rows_out)


NAMES = ["x", "ctx_512"] + ["L0_xattn_" + n for n in ("Wk", "bk", "Wq", "bq", "Wv", "bv", "Wck", "bck", "Wcq", "bcq",
                                                     "Wcv", "bcv", "Wp", "bp")] + [
    "L0_ffn_" + n for n in ("Wr", "br", "W1", "b1", "W2", "b2")] + [
    "L1_xattn_" + n for n in ("Wq", "bq", "Wk", "bk", "Wv", "bv")] + ["L1_ffn_" + n for n in ("wr", "w1", "b1", "w2", "b2")]


def kernel(**inputs):
    import concourse.bacc as bacc
    from concourse.bass_utils import run_bass_kernel_spmd

    nc = bacc.Bacc("TRN2", target_bir_lowering=False, num_devices=1)
    arrays, io = {}, {}
    for name in NAMES:
        a = np.ascontiguousarray(inputs[name])
        arrays[name + "_dram"] = a
        io[name] = nc.dram_tensor(name + "_dram", a.shape, mybir.dt.from_np(a.dtype), kind="ExternalInput").ap()
    out = nc.dram_tensor("out_dram", (NB, T, P), F32, kind="ExternalOutput").ap()
    program(nc, io, out)
    return run_bass_kernel_spmd(nc, [arrays], core_ids=[0]).results[0]["out_dram"]
```

```python
from contextlib import ExitStack

import numpy as np
import concourse.bass as bass
from concourse import mybir

ALU = mybir.AluOpType
ACT = mybir.ActivationFunctionType
AX = mybir.AxisListType
F32 = mybir.dt.float32
F32R = mybir.dt.float32r
BF16 = mybir.dt.bfloat16
U32 = mybir.dt.uint32

P = 128
NB = 16
T = 256
TC = 64
CC = 64
H0 = 16
HD = 8
NG = 4
HG = 4
GC = HG * HD
NSTACK = 3 * GC
NROW = NSTACK + HG
SCALE = float(np.float32(1.0 / np.sqrt(HD)))
EPS = 1e-5
NEG = -1e30
FIRST = 8
RING = 3



def steps(g, prev, nxt, nxt2):
    ahead = g < 2 or nxt
    u = []
    if ahead:
        u += ["S0", "S1"]
    if g == 3 and prev:
        u += ["O"]
    if nxt:
        u += ["K"]
    if nxt:
        u += ["Q"]
    if nxt:
        u += ["C"]
    if g < 3 or nxt:
        u += ["M"]
    if ahead:
        u += ["S2"]
    if ahead:
        u += ["S3"]
    if g == 0 and nxt:
        u += ["V0"]
    if g == 1:
        u += (["T1"] if prev else []) + (["V1"] if nxt else [])
    if g == 2:
        u += (["YT"] if prev else []) + (["X"] if nxt2 else [])
    if g == 3:
        u += ["T0"]
    return u


START = ([("CT", 0), ("CT", 1), ("X", 0)] + [("VC", i) for i in range(4)] + [("V0", 0), ("V1", 0)]
         + [("KC", i) for i in range(8)] + [(k, g) for g in range(NG) for k in "KQC"] + [("X", 1)]
         + [(f"S{j}", n) for n in range(2) for j in range(4)] + [("M", 0)])
LOOPED = NB - 3


def ring_plan():
    parts = [("start", START)]
    for part, prev, nxt, nxt2 in (("first", 0, 1, 1), ("loop", 1, 1, 1), ("before last", 1, 1, 0), ("last", 1, 0, 0)):
        parts.append((part, [(u, g) for g in range(NG) for u in steps(g, prev, nxt, nxt2)]))
    parts.append(("end", [("T1", 0), ("YT", 0), ("O", 0)]))
    where, at = {}, 0
    for part, uses in parts:
        where[part] = {u: at + i for i, u in enumerate(uses)}
        at += len(uses) * (LOOPED if part == "loop" else 1)
    return where


WHERE = ring_plan()
PER_SEQ = len(WHERE["loop"])
assert PER_SEQ % RING == 0
BEFORE = {"first": "start", "loop": "loop", "before last": "loop", "last": "before last"}


class Seq:

    def __init__(self, b, part, prev=True, nxt=True, nxt2=True, slot=0):
        self.b, self.part, self.slot = b, part, slot
        self.prev, self.nxt, self.nxt2 = prev, nxt, nxt2

    def at(self, position):
        before = position // RING
        if self.part == "loop":
            before = before + (self.b - 1) * (PER_SEQ // RING)
        return position % RING, before

    def ring(self, name, g):
        return self.at(WHERE[self.part][(name, g)])

    def maxima(self, g):
        if g:
            return self.ring("M", g - 1)
        last = WHERE[BEFORE[self.part]]
        back = len(last) - list(last).index(("M", 0 if self.part == "first" else 3))
        return self.at(min(WHERE[self.part].values()) - back)


def sequences(eng, body):
    body(Seq(0, "first", prev=False, slot=0))
    with eng.Fori(1, NB - 3, 2) as i:
        body(Seq(i, "loop", slot=1))
        body(Seq(i + 1, "loop", slot=0))
    body(Seq(NB - 3, "loop", slot=1))
    body(Seq(NB - 2, "before last", nxt2=False, slot=0))
    body(Seq(NB - 1, "last", nxt=False, nxt2=False, slot=1))


def attention0(nc, io, X, CT, ident, identb):
    st = ExitStack()

    def sb(name, shape, dt=F32):
        return st.enter_context(nc.sbuf_tensor(name, shape, dt))

    def sem(name):
        return st.enter_context(nc.semaphore(name))

    with st:
        ones = sb("ones", [P, P])
        causal = sb("causal", [P, HG, P], BF16)
        stats = sb("stats", [P, 2 * NB, 6])
        mv = sb("mv", [P, 2 * NB, 2])
        rstd = sb("rstd", [P, 2 * NB])
        power = sb("power", [P, 2 * NB])
        half = sb("half", [P, 2 * NB])
        shift = sb("shift", [P, 2 * NB])
        XN = sb("XN", [P, 2, 2, P])
        W = {k: sb("w" + k, [P, P]) for k in ("K", "Q", "C", "V", "P")}
        WC = {k: sb("wc" + k, [CC, P]) for k in ("K", "V")}
        WS = {k: sb("ws" + k, [P, 2, NG, 3, GC], F32R) for k in ("K", "Q", "C")}
        WCS = sb("wcs", [CC, 2, NG, 3, GC], F32R)
        WV = sb("wv", [P, 2, P], F32R)
        BS = {k: sb("bs" + k, [NSTACK, NG]) for k in ("K", "Q", "C", "KC")}
        BL = {k: sb("bl" + k, [NSTACK, NG]) for k in ("K", "Q", "C", "KC")}
        lowk = sb("lowk", [NSTACK, 1])
        lowq = sb("lowq", [NSTACK, 1])
        headrow = sb("headrow", [P, HG])
        bvb = sb("bvb", [P, P])
        bcvb = sb("bcvb", [P, P])
        bpb = sb("bpb", [P, 2, P])
        ctxs = sb("ctxs", [P, 8, CC])
        CTR = sb("CTR", [CC, 2, NB * TC], F32R)
        KC = sb("KC", [NSTACK, NG, NB * TC], F32R)
        VCA = sb("VCA", [P, NB, P])
        XR = sb("XR", [P, 2, 2, T], F32R)
        LO = sb("LO", [NSTACK, 4, T], F32R)
        KS = sb("KS", [NSTACK, 2, T], F32R)
        KM = sb("KM", [NROW, 2 * NG, HG, T], F32R)
        KCM = sb("KCM", [NROW, 2, NG, HG, TC], F32R)
        QC = sb("QC", [NROW, 2 * NG, 2, T], F32R)
        VS = sb("VS", [P, 2, 2, H0, 4 * HD])
        VC = sb("VC", [P, 2, H0 // 2, 8 * HD])
        MG = sb("MG", [P, 2, 4, NROW])
        PT = sb("PT", [P, 2, 2048])
        NV = sb("NV", [P, 2, 512])
        RD = sb("RD", [P, 4, HG, 2])
        YN = sb("YN", [P, 4, 2, HG, HD])
        Y = sb("Y", [P, 2, P])
        YT = sb("YT", [P, T])

        ps_ring = [st.enter_context(nc.psum_tensor(f"ring{i}", [P, 512], F32)) for i in range(RING)]
        ps_pv = st.enter_context(nc.psum_tensor("ps_pv", [P, 512], F32))
        ps_st = st.enter_context(nc.psum_tensor("ps_st", [P, 2048], F32))

        ld_x = [sem(f"ld_x{i}") for i in range(4)]
        ld_w, ld_b, ld_s, ld_c = sem("ld_w"), sem("ld_b"), sem("ld_s"), sem("ld_c")
        ring_full = [sem(f"ring_full{i}") for i in range(RING)]
        ring_free = [sem(f"ring_free{i}") for i in range(RING)]
        zeros_set, consts_set = sem("zeros_set"), sem("consts_set")
        low_masks_set, weights_set = sem("low_masks_set"), sem("weights_set")
        waited = sem("waited")
        stats_set, var_set, rstd_set, shift_set = sem("stats_set"), sem("var_set"), sem("rstd_set"), sem("shift_set")
        chain = sem("chain")
        xn_set, xb_set, xhigh_set, ctxt_set = sem("xn_set"), sem("xb_set"), sem("xhigh_set"), sem("ctxt_set")
        low_set, km_set, kcm_set, vc_set = sem("low_set"), sem("km_set"), sem("kcm_set"), sem("vc_set")
        max_set, rd_set, y_set = sem("max_set"), sem("rd_set"), sem("y_set")
        st_full, exp_done, sel_done, pv_done, nv_set = (
            sem("st_full"), sem("exp_done"), sem("sel_done"), sem("pv_done"), sem("nv_set"))

        block = st.enter_context(nc.Block())
        start = Seq(0, "start")
        end = Seq(NB, "end")

        def wait_full(eng, s, name, g):
            bank, before = s.ring(name, g)
            eng.wait_ge(ring_full[bank], before + 1)
            return ps_ring[bank], ring_free[bank]

        def wait_drained(eng, s, name, g):
            bank, before = s.ring(name, g)
            eng.wait_ge(ring_free[bank], before + 1)

        def pair(b):
            return X[:, bass.ds(2 * b, 2), :]

        @block.sync
        def _(sp):
            xv = io["x"].rearrange("b (t p) c -> p (b t) c", p=P)
            for q in range(4):
                sp.dma_start(X[:, 8 * q:8 * q + 8, :], xv[:, 8 * q:8 * q + 8, :]).then_inc(ld_x[q], 16)
            sp.dma_start(W["P"][:, :], io["L0_xattn_Wp"]).then_inc(ld_w, 16)

            def row(name):
                return io[name].rearrange("(a c) -> a c", a=1).to_broadcast([P, P])

            sp.dma_start(bvb[:, :], row("L0_xattn_bv")).then_inc(ld_b, 16)
            sp.dma_start(bcvb[:, :], row("L0_xattn_bcv")).then_inc(ld_b, 16)
            for t in range(2):
                sp.dma_start(bpb[:, t, :], row("L0_xattn_bp")).then_inc(ld_b, 16)
            with nc.allow_non_contiguous_dma(reason="biases onto the stacks' rows"):
                for k, name in (("K", "bk"), ("Q", "bq"), ("C", "bcq"), ("KC", "bck")):
                    for j in range(3):
                        sp.dma_start(BS[k][GC * j:GC * j + GC, :],
                                     io["L0_xattn_" + name].rearrange("(g c) -> c g", g=NG)).then_inc(ld_s, 16)

        @block.scalar
        def _(act):
            act.dma_start(ctxs[:, :, :], io["ctx_512"].rearrange("(o u) s c -> (u s) o c", u=2)).then_inc(ld_c, 16)
            for k, name in (("K", "Wk"), ("Q", "Wq"), ("C", "Wcq"), ("V", "Wv")):
                act.dma_start(W[k][:, :], io["L0_xattn_" + name]).then_inc(ld_w, 16)
            for k, name in (("K", "Wck"), ("V", "Wcv")):
                act.dma_start(WC[k][:, :], io["L0_xattn_" + name]).then_inc(ld_w, 16)
            act.preload_act_table(ACT.Exp)

            def low(s, kind, g):
                bank, _ = wait_full(act, s, kind, g)
                mask = lowk if kind == "K" else lowq
                nc.scalar.activation(LO[:, "KQC".index(kind), :], bank[0:NSTACK, 0:T], ACT.Identity,
                                     bias=BL[kind][:, g:g + 1], scale=mask[:, 0:1]).then_inc(low_set, 1)

            def x_high(s, g, slot):
                bank, _ = wait_full(act, s, "X", g)
                nc.scalar.copy(XR[:, slot, 0, :], bank[:, 0:T]).then_inc(xhigh_set, 1)

            def maxima(s, g, at):
                bank, free = wait_full(act, s, "M", g)
                nc.scalar.copy(QC[NSTACK:NROW, at, :, :].rearrange("p a t -> p (a t)"),
                               bank[NSTACK:NROW, :]).then_inc(free, 1)

            for i in range(2):
                bank, _ = wait_full(act, start, "CT", i)
                nc.scalar.copy(CT[0:CC, 512 * i:512 * i + 512], bank[0:CC, :]).then_inc(ctxt_set, 1)
                nc.scalar.copy(CTR[:, 0, 512 * i:512 * i + 512], bank[0:CC, :]).then_inc(ctxt_set, 1)
            x_high(start, 0, 0)
            act.wait_ge(low_masks_set, 1)
            for i in range(8):
                bank, _ = wait_full(act, start, "KC", i)
                if i >= 2:
                    wait_drained(act, start, "KC", i - 2)
                at = 2 * (i % 2)
                nc.scalar.activation(LO[:, at:at + 2, :].rearrange("p a t -> p (a t)"), bank[0:NSTACK, :], ACT.Identity,
                                     bias=BL["KC"][:, i // 2:i // 2 + 1], scale=lowk[:, 0:1]).then_inc(low_set, 1)
            wait_drained(act, start, "KC", 7)
            for g in range(NG):
                for kind in "KQC":
                    if g:
                        wait_drained(act, start, kind, g - 1)
                    low(start, kind, g)
            x_high(start, 1, 1)
            maxima(start, 0, 0)

            def body(s):
                for g in range(NG):
                    n = 4 * s.b + g
                    for h in range(2):
                        act.wait_ge(st_full, 2 * n + h + 1)
                        nc.scalar.activation(PT[:, g % 2, 1024 * h:1024 * h + 1024], ps_st[:, 1024 * h:1024 * h + 1024],
                                             ACT.Exp, scale=SCALE).then_inc(exp_done, 1)
                    if s.nxt:
                        low(s, "K", g)
                    if s.nxt:
                        low(s, "Q", g)
                    if s.nxt:
                        low(s, "C", g)
                    if g < 3 or s.nxt:
                        maxima(s, g, (4 * s.slot + g + 1) % 8)
                    if g == 2 or (g == 0 and s.prev):
                        act.wait_ge(pv_done, n)
                        nc.scalar.copy(NV[:, 1 - g // 2, :], ps_pv[:, :]).then_inc(nv_set, 1)
                    if g == 2 and s.prev:
                        bank, free = wait_full(act, s, "YT", g)
                        nc.scalar.copy(YT[:, :], bank[:, 0:T]).then_inc(free, 1)
                    if g == 2 and s.nxt2:
                        x_high(s, g, s.slot)

            sequences(act, body)
            act.wait_ge(pv_done, 4 * NB)
            nc.scalar.copy(NV[:, 1, :], ps_pv[:, :]).then_inc(nv_set, 1)
            bank, free = wait_full(act, end, "YT", 0)
            nc.scalar.copy(YT[:, :], bank[:, 0:T]).then_inc(free, 1)

        @block.gpsimd
        def _(pool):
            nc.gpsimd.memset(ones[:, :], 1.0).then_inc(zeros_set, 1)
            nc.gpsimd.memset(causal[:, :, :], 0.0).then_inc(zeros_set, 1)
            pool.wait_ge(zeros_set, 2)
            nc.gpsimd.affine_select(out=ident[:, :], in_=ones[:, :], compare_op=ALU.is_equal, fill=0.0, base=0,
                                    pattern=[[-1, P]], channel_multiplier=1).then_inc(consts_set, 1)
            nc.gpsimd.affine_select(out=causal[:, :, :], in_=causal[:, :, :], compare_op=ALU.is_ge, fill=NEG, base=0,
                                    pattern=[[0, HG], [-1, P]], channel_multiplier=1).then_inc(consts_set, 1)
            nc.gpsimd.memset(power[:, :], -0.5).then_inc(consts_set, 1)
            nc.gpsimd.memset(MG[:, :, :, :], 0.0).then_inc(zeros_set, 1)
            nc.gpsimd.memset(VS[:, :, :, :, :], 0.0).then_inc(zeros_set, 1)
            nc.gpsimd.memset(VC[:, :, :, :], 0.0).then_inc(zeros_set, 1)
            pool.wait_ge(consts_set, 3)

            def roots(part, count):
                pool.wait_ge(stats_set, count)
                nc.gpsimd.tensor_scalar(rstd[:, part], mv[:, part, 1], EPS, 1.0, ALU.add, ALU.mult).then_inc(var_set, 1)
                pool.wait_ge(var_set, count)
                nc.gpsimd.tensor_tensor(rstd[:, part], rstd[:, part], power[:, part], ALU.pow)
                nc.gpsimd.tensor_scalar(shift[:, part], mv[:, part, 0], -1.0, 1.0, ALU.mult, ALU.mult).then_inc(rstd_set, 1)
                pool.wait_ge(rstd_set, count)
                nc.gpsimd.tensor_tensor(shift[:, part], shift[:, part], rstd[:, part], ALU.mult).then_inc(shift_set, 1)

            def wait(semaphore, value):
                pool.wait_ge(semaphore, value)
                if not isinstance(value, int):
                    pool.sem_inc(waited, 1)

            def normalise(b, slot):
                at = bass.ds(2 * b, 2)
                nc.gpsimd.tensor_tensor(XN[:, slot, :, :], pair(b), rstd[:, at].unsqueeze(2).to_broadcast([P, 2, P]),
                                        ALU.mult).then_inc(xn_set, 1)
                wait(xn_set, 2 * b + 1)
                nc.gpsimd.tensor_tensor(XN[:, slot, :, :], XN[:, slot, :, :],
                                        shift[:, at].unsqueeze(2).to_broadcast([P, 2, P]), ALU.add).then_inc(xn_set, 1)
                nc.gpsimd.tensor_tensor(pair(b), pair(b), bpb[:, :, :], ALU.add).then_inc(xb_set, 1)

            def keys_by_head(s, g, n, at):
                bank, before = s.ring("K", g)
                wait(ring_free[bank], before + 1)
                for r in range(HG):
                    nc.gpsimd.tensor_scalar(KM[0:NSTACK, at, r, :], KS[:, g % 2, :], headrow[0:NSTACK, r:r + 1], 1.0,
                                            ALU.mult, ALU.mult).then_inc(km_set, 1)

            def context_keys(b, slot):
                for r in range(HG):
                    own = headrow[0:NSTACK, r:r + 1].unsqueeze(2).to_broadcast([NSTACK, NG, TC])
                    nc.gpsimd.tensor_tensor(KCM[0:NSTACK, slot, :, r, :], KC[:, :, bass.ds(TC * b, TC)], own,
                                            ALU.mult).then_inc(kcm_set, 1)

            roots(slice(0, FIRST), 1)
            pool.wait_ge(shift_set, 1)
            pool.wait_ge(ld_x[0], 16)
            pool.wait_ge(ld_b, 16 * 4)
            normalise(0, 0)
            normalise(1, 1)
            pool.wait_ge(low_masks_set, 2)
            roots(slice(FIRST, 2 * NB), 2)
            for g in range(NG):
                keys_by_head(start, g, g, g)
            wait_drained(pool, start, "KC", 7)
            context_keys(0, 0)
            pool.wait_ge(shift_set, 2)
            for q in range(4):
                pool.wait_ge(ld_x[q], 16)

            def body(s):
                for g in range(NG):
                    n = 4 * s.b + g
                    for h in range(2):
                        wait(exp_done, 2 * n + h + 1)
                        if h == 0:
                            diagonal = PT[:, g % 2, 0:1024].rearrange("p (r q) -> p r q", r=HG)[:, :, 0:P]
                        else:
                            diagonal = PT[:, g % 2, 1024:1536].rearrange("p (r q) -> p r q", r=HG)
                        nc.gpsimd.affine_select(out=diagonal, in_=diagonal, compare_op=ALU.is_ge, fill=0.0, base=0,
                                                pattern=[[0, HG], [1, P]], channel_multiplier=-1).then_inc(sel_done, 1)
                    if s.nxt:
                        keys_by_head(s, g, n + 4, (4 * s.slot + g + 4) % 8)
                    if g == 0 and s.nxt:
                        context_keys(s.b + 1, 1 - s.slot)
                    if g == 0 and s.nxt2:
                        normalise(s.b + 2, s.slot)

            sequences(pool, body)

        @block.vector
        def _(dve):
            count = [0]

            def then(ins):
                count[0] += 1
                ins.then_inc(chain, 1)
                dve.wait_ge(chain, count[0])

            dve.wait_ge(ld_x[0], 16)
            for t in range(FIRST):
                last = nc.vector.bn_stats(stats[:, t, :], X[:, t, :])
            then(last)
            for t in range(FIRST):
                last = nc.vector.bn_aggr(mv[:, t, :], stats[:, t, :])
            last.then_inc(stats_set, 1)
            nc.vector.memset(lowk[:, :], 0.0)
            then(nc.vector.memset(lowq[:, :], 0.0))
            nc.vector.memset(lowk[GC:2 * GC, :], 1.0)
            then(nc.vector.memset(lowq[2 * GC:3 * GC, :], 1.0))
            def x_low(s, g, b, slot):
                bank, free = wait_full(dve, s, "X", g)
                dve.wait_ge(xhigh_set, b + 1)
                nc.vector.tensor_tensor(XR[:, slot, 1, :], bank[:, 0:T], XR[:, slot, 0, :], ALU.subtract).then_inc(free, 1)

            def all_context_values(i):
                bank, free = wait_full(dve, start, "VC", i)
                nc.vector.tensor_tensor(VCA[:, 4 * i:4 * i + 4, :], bank[:, :].rearrange("p (b c) -> p b c", b=4),
                                        bcvb[:, :].unsqueeze(1).to_broadcast([P, 4, P]), ALU.add).then_inc(free, 1)

            dve.wait_ge(ctxt_set, 4)
            for i in range(2):
                bank, free = wait_full(dve, start, "CT", i)
                nc.vector.tensor_tensor(CTR[:, 1, 512 * i:512 * i + 512], bank[0:CC, :], CTR[:, 0, 512 * i:512 * i + 512],
                                        ALU.subtract).then_inc(free, 1)
            dve.wait_ge(ld_w, 16 * 7)
            stacks = [(WS[k], W[k], P) for k in ("K", "Q", "C")] + [(WCS, WC["K"], CC)]

            def copies(w, g, rows):
                return w[:, GC * g:GC * g + GC].unsqueeze(1).to_broadcast([rows, 3, GC])

            for ws, w, rows in stacks:
                for g in range(NG):
                    nc.vector.tensor_copy(ws[:, 0, g, :, :], copies(w, g, rows))
            then(nc.vector.tensor_copy(WV[:, 0, :], W["V"][:, :]))
            dve.wait_ge(ld_b, 16 * 4)
            all_context_values(0)
            x_low(start, 0, 0, 0)
            all_context_values(1)
            for ws, w, rows in stacks:
                for g in range(NG):
                    nc.vector.tensor_tensor(ws[:, 1, g, :, :], copies(w, g, rows), ws[:, 0, g, :, :], ALU.subtract)
            nc.vector.tensor_tensor(WV[:, 1, :], W["V"][:, :], WV[:, 0, :], ALU.subtract).then_inc(weights_set, 1)
            all_context_values(2)
            dve.wait_ge(ld_s, 16 * 12)
            for k in ("K", "Q", "C", "KC"):
                mask = lowk if k in ("K", "KC") else lowq
                last = nc.vector.tensor_scalar(BL[k][:, :], BS[k][:, :], mask[:, 0:1], None, ALU.mult)
            last.then_inc(low_masks_set, 1)
            dve.wait_ge(consts_set, 2)
            dve.wait_ge(zeros_set, 5)
            for gp in range(2):
                v = VS[:, :, :, :, :].rearrange("p s k (a e r) c -> p (s k) a e r c", a=2, e=2)
                w = VC[:, :, :, :].rearrange("p s (a e u) c -> p s a e u c", a=2, e=2)
                for a in range(2):
                    nc.vector.memset(v[:, :, a, gp, :, 2 * HD + gp], 1.0)
                    nc.vector.memset(w[0:TC, :, a, gp, :, 2 * HD + gp], 1.0)
                    nc.vector.memset(w[TC:P, :, a, gp, :, 6 * HD + gp], 1.0)
            nc.vector.tensor_copy(identb[:, :], ident[:, :])
            nc.vector.tensor_reduce(headrow[:, :], ident[:, :].rearrange("p (j r d) -> p r j d", j=4, r=HG),
                                    AX.XY, ALU.add).then_inc(low_masks_set, 1)

            def maximum_rows(r):
                one = ident[NSTACK:NROW, NSTACK + r:NSTACK + r + 1].unsqueeze(2)
                nc.vector.tensor_copy(KM[NSTACK:NROW, :, r, :], one.to_broadcast([HG, 2 * NG, T]))
                nc.vector.tensor_copy(KCM[NSTACK:NROW, :, :, r, :].rearrange("p s g t -> p (s g) t"),
                                      one.to_broadcast([HG, 2 * NG, TC]))

            def stack(s, kind, g, n, at):
                bank, free = wait_full(dve, s, kind, g)
                j = "KQC".index(kind)
                dve.wait_ge(low_set, 8 + 3 * n + j + 1)
                if kind == "K":
                    if not (isinstance(n, int) and n < 2):
                        dve.wait_ge(km_set, HG * (n - 1))
                    to = KS[:, g % 2, :]
                else:
                    to = QC[0:NSTACK, at, j - 1, :]
                nc.vector.scalar_tensor_tensor(out=to, in0=bank[0:NSTACK, 0:T], scalar=BS[kind][:, g:g + 1],
                                               in1=LO[:, j, :], op0=ALU.add, op1=ALU.subtract).then_inc(free, 1)

            def values(s, t, g, slot):
                bank, free = wait_full(dve, s, f"V{t}", g)
                v = bank[:, 0:P].rearrange("p (a e r d) -> p a e r d", a=2, e=2, r=HG)
                bias = bvb[:, :].rearrange("p (a e r d) -> p a e r d", a=2, e=2, r=HG)
                to = VS[:, slot, t, :, :].rearrange("p (a e r) c -> p a e r c", a=2, e=2)
                for gp in range(2):
                    last = nc.vector.tensor_tensor(to[:, :, gp, :, HD * gp:HD * gp + HD], v[:, :, gp], bias[:, :, gp], ALU.add)
                last.then_inc(free, 1)

            def context_values(b, slot):
                src = VCA[:, bass.ds(b, 1), :].rearrange("p s (a e u w d) -> p (s a) e u w d", a=2, e=2, u=2, w=2)
                to = VC[:, slot, :, :].rearrange("p (a e u) c -> p a e u c", a=2, e=2)
                for gp in range(2):
                    for w in range(2):
                        rows = slice(TC * w, TC * w + TC)
                        col = 4 * HD * w + HD * gp
                        last = nc.vector.tensor_copy(to[rows, :, gp, :, col:col + HD], src[rows, :, gp, :, w, :])
                last.then_inc(vc_set, 1)

            def maximum(s, j, g, at2):
                bank, free = wait_full(dve, s, f"S{j}", g)
                if j == 0:
                    src, to = bank[:, :].rearrange("p (r k) -> p r k", r=HG), MG[:, at2, 0, NSTACK:NROW]
                elif j < 3:
                    at = NSTACK + 2 * (j - 1)
                    src, to = bank[:, :].rearrange("p (r k) -> p r k", r=2), MG[:, at2, 1, at:at + 2]
                else:
                    src, to = (bank[:, :].rearrange("p (t r k) -> p t r k", t=2, r=HG), MG[:, at2, 2:4, NSTACK:NROW])
                nc.vector.tensor_reduce(to, src, AX.X, ALU.max, negate=True).then_inc(free, 1)

            def divide(s, a, g, b):
                bank, free = wait_full(dve, s, f"T{a}", g)
                v = bank[:, :].rearrange("p (k r w) -> p k r w", k=4, r=HG)
                nc.vector.reciprocal(RD[:, :, :, :], v[:, :, :, 2 * HD:2 * HD + 2]).then_inc(rd_set, 1)
                dve.wait_ge(rd_set, 2 * b + a + 1)
                for gp in range(2):
                    last = nc.vector.tensor_tensor(YN[:, :, gp, :, :], v[:, :, :, HD * gp:HD * gp + HD],
                                                   RD[:, :, :, gp:gp + 1].to_broadcast([P, 4, HG, HD]), ALU.mult)
                last.then_inc(free, 1)
                wait_drained(dve, s, f"T{a}", g)
                yn = YN[:, :, :, :, :].rearrange("p k e r d -> p k (e r d)")
                nc.vector.tensor_tensor(Y[:, :, 2 * GC * a:2 * GC * a + 2 * GC], yn[:, 0:2, :], yn[:, 2:4, :],
                                        ALU.add).then_inc(y_set, 1)

            def add_to_x(s, g, b):
                bank, free = wait_full(dve, s, "O", g)
                dve.wait_ge(xb_set, b + 1)
                nc.vector.tensor_tensor(pair(b), pair(b), bank[:, 0:T].rearrange("p (t c) -> p t c", t=2),
                                        ALU.add).then_inc(free, 1)

            all_context_values(3)
            values(start, 0, 0, 0)
            values(start, 1, 0, 0)
            for i in range(8):
                g, h = i // 2, i % 2
                bank, free = wait_full(dve, start, "KC", i)
                dve.wait_ge(low_set, i + 1)
                at = 2 * h
                nc.vector.scalar_tensor_tensor(out=KC[:, g, 512 * h:512 * h + 512], in0=bank[0:NSTACK, :],
                                               scalar=BS["KC"][:, g:g + 1],
                                               in1=LO[:, at:at + 2, :].rearrange("p a t -> p (a t)"),
                                               op0=ALU.add, op1=ALU.subtract).then_inc(free, 1)
                for t in range(FIRST + 3 * i, FIRST + 3 * i + 3):
                    dve.wait_ge(ld_x[t // 8], 16)
                    last = nc.vector.bn_stats(stats[:, t, :], X[:, t, :])
            then(last)
            for t in range(FIRST, 2 * NB):
                last = nc.vector.bn_aggr(mv[:, t, :], stats[:, t, :])
            last.then_inc(stats_set, 1)
            for g in range(NG):
                for kind in "KQC":
                    stack(start, kind, g, g, g)
                maximum_rows(g)
            wait_drained(dve, start, "VC", 3)
            context_values(0, 0)
            x_low(start, 1, 1, 1)
            for n in range(2):
                for j in range(4):
                    maximum(start, j, n, n % 2)

            def body(s):
                for g in range(NG):
                    n = 4 * s.b + g
                    ahead = g < 2 or s.nxt
                    if ahead:
                        maximum(s, 0, g, g % 2)
                        maximum(s, 1, g, g % 2)
                    if g == 3 and s.prev:
                        add_to_x(s, g, s.b - 1)
                    at = (4 * s.slot + g + 4) % 8
                    if s.nxt:
                        stack(s, "K", g, n + 4, at)
                    if s.nxt:
                        stack(s, "Q", g, n + 4, at)
                    if s.nxt:
                        stack(s, "C", g, n + 4, at)
                    if ahead:
                        maximum(s, 2, g, g % 2)
                    if ahead:
                        maximum(s, 3, g, g % 2)
                    if g == 0 and s.nxt:
                        values(s, 0, g, 1 - s.slot)
                    if g == 1 and s.prev:
                        divide(s, 1, g, s.b - 1)
                    if g == 1 and s.nxt:
                        values(s, 1, g, 1 - s.slot)
                        context_values(s.b + 1, 1 - s.slot)
                    if g == 2 and s.nxt2:
                        x_low(s, g, s.b + 2, s.slot)
                    if g == 3:
                        divide(s, 0, g, s.b)

            sequences(dve, body)
            divide(end, 1, 0, NB - 1)
            add_to_x(end, 0, NB - 1)

        @block.tensor
        def _(pe):
            def take(s, name, g):
                bank, before = s.ring(name, g)
                if not (isinstance(before, int) and before == 0):
                    pe.wait_ge(ring_free[bank], before)
                return ps_ring[bank], ring_full[bank]

            def split(to, stationary, moving):
                for i, (a, b) in enumerate(((0, 0), (1, 0), (0, 1))):
                    last = nc.tensor.matmul(to, stationary(a), moving(b), start=(i == 0), stop=(i == 2))
                return last

            def transpose_x(s, g, b, slot):
                bank, full = take(s, "X", g)
                pe.wait_ge(xn_set, 2 * b + 2)
                for t in range(2):
                    last = nc.tensor.transpose(bank[:, P * t:P * t + P], XN[:, slot, t, :], ident[:, :])
                last.then_inc(full, 1)

            def project(s, kind, g, slot):
                bank, full = take(s, kind, g)
                split(bank[0:NSTACK, 0:T], lambda a: WS[kind][:, a, g, :, :].rearrange("p j c -> p (j c)"),
                      lambda b: XR[:, slot, b, :]).then_inc(full, 1)

            def project_values(s, t, g, slot):
                bank, full = take(s, f"V{t}", g)
                split(bank[:, 0:P], lambda a: XR[:, slot, a, P * t:P * t + P], lambda b: WV[:, b, :]).then_inc(full, 1)

            def scores_for_max(s, j, g, gn, n, slot, b):
                bank, full = take(s, f"S{j}", g)
                at = 4 * slot + gn
                if j == 0:
                    pe.wait_ge(km_set, HG * (n + 1))
                    nc.tensor.matmul(bank[:, :], QC[0:NSTACK, at, 0, 0:P], KM[0:NSTACK, at, :, 0:P], start=True, stop=False)
                    last = nc.tensor.matmul(bank[:, :], identb[:, :], causal[:, :, :], start=False, stop=True)
                elif j < 3:
                    r = 2 * (j - 1)
                    v = bank[:, :].rearrange("p (r k) -> p r k", r=2)
                    nc.tensor.matmul(v[:, :, P:T], identb[:, :], causal[:, 0:2, :], start=True, stop=False,
                                     skip_group_check=True)
                    last = nc.tensor.matmul(bank[:, :], QC[0:NSTACK, at, 0, P:T], KM[0:NSTACK, at, r:r + 2, :],
                                            start=False, stop=True, skip_group_check=True)
                else:
                    if gn == 0:
                        pe.wait_ge(kcm_set, HG * (b + 1))
                    for t in range(2):
                        last = nc.tensor.matmul(bank[:, T * t:T * t + T], QC[0:NSTACK, at, 1, P * t:P * t + P],
                                                KCM[0:NSTACK, slot, gn, :, :], start=True, stop=True)
                last.then_inc(full, 1)

            def transpose_max(s, g, n, at2):
                bank, full = take(s, "M", g)
                for k in range(4):
                    last = nc.tensor.transpose(bank[0:NROW, P * k:P * k + P], MG[:, at2, k, :], ident[:, :])
                last.then_inc(full, 1)

            def scores(s, g, h, n):
                at = 4 * s.slot + g
                if h == 0:
                    bank, before = s.maxima(g)
                    pe.wait_ge(ring_free[bank], before + 1)
                if not (isinstance(n, int) and n == 0):
                    pe.wait_ge(exp_done, 2 * n - 1 + h)
                if h == 0:
                    for r in range(HG):
                        last = nc.tensor.matmul(ps_st[:, T * r:T * r + T], KM[:, at, r, 0:P], QC[:, at, 0, :],
                                                start=True, stop=True)
                else:
                    for r in range(HG):
                        nc.tensor.matmul(ps_st[:, 1024 + P * r:1024 + P * r + P], KM[:, at, r, P:T], QC[:, at, 0, P:T],
                                         start=True, stop=True)
                    for u in range(2):
                        last = nc.tensor.matmul(ps_st[:, 1536 + T * u:1536 + T * u + T],
                                                KCM[:, s.slot, g, 2 * u:2 * u + 2, :].rearrange("p r t -> p (r t)"),
                                                QC[:, at, 1, :], start=True, stop=True)
                last.then_inc(st_full, 1)

            def sums(h, g, n, slot, pairs, b):
                pe.wait_ge(sel_done, 2 * n + h + 1)
                if h == 0:
                    if g % 2 == 0 and not (isinstance(pairs, int) and pairs == 0):
                        pe.wait_ge(nv_set, pairs)
                    for r in range(HG):
                        nc.tensor.matmul(ps_pv[GC * r:GC * r + GC, 0:T], VS[:, slot, 0, HG * g + r, :],
                                         PT[:, g % 2, T * r:T * r + T], start=(g % 2 == 0), stop=False,
                                         tile_position=(0, GC * r), skip_group_check=True)
                    return
                if g == 0:
                    pe.wait_ge(vc_set, b + 1)
                for r in range(HG):
                    nc.tensor.matmul(ps_pv[GC * r:GC * r + GC, P:T], VS[:, slot, 1, HG * g + r, :],
                                     PT[:, g % 2, 1024 + P * r:1024 + P * r + P], start=False, stop=(g % 2 == 1),
                                     tile_position=(0, GC * r), skip_group_check=True)
                for u in range(2):
                    last = nc.tensor.matmul(ps_pv[2 * GC * u:2 * GC * u + 2 * GC, T:2 * T], VC[:, slot, 2 * g + u, :],
                                            PT[:, g % 2, 1536 + T * u:1536 + T * u + T], start=False, stop=(g % 2 == 1),
                                            tile_position=(0, 2 * GC * u), skip_group_check=True)
                last.then_inc(pv_done, 1)

            def transpose_sums(s, a, g, b):
                bank, full = take(s, f"T{a}", g)
                pe.wait_ge(nv_set, 2 * b + a + 1)
                for k in range(4):
                    last = nc.tensor.transpose(bank[:, P * k:P * k + P], NV[:, a, P * k:P * k + P], ident[:, :])
                last.then_inc(full, 1)

            def transpose_y(s, g, b):
                bank, full = take(s, "YT", g)
                pe.wait_ge(y_set, 2 * b + 2)
                for t in range(2):
                    last = nc.tensor.transpose(bank[:, P * t:P * t + P], Y[:, t, :], ident[:, :])
                last.then_inc(full, 1)

            def project_out(s, g, gy):
                bank, full = take(s, "O", g)
                wait_drained(pe, s, "YT", gy)
                for t in range(2):
                    last = nc.tensor.matmul(bank[:, P * t:P * t + P], YT[:, P * t:P * t + P], W["P"][:, :],
                                            start=True, stop=True)
                last.then_inc(full, 1)

            pe.wait_ge(consts_set, 2)
            pe.wait_ge(ld_c, 16)
            for i in range(2):
                bank, full = take(start, "CT", i)
                for o in range(4):
                    last = nc.tensor.transpose(bank[0:CC, P * o:P * o + P], ctxs[:, 4 * i + o, :], ident[:, :])
                last.then_inc(full, 1)
            transpose_x(start, 0, 0, 0)
            pe.wait_ge(ctxt_set, 4)
            pe.wait_ge(ld_w, 16 * 7)
            for i in range(4):
                bank, full = take(start, "VC", i)
                for o in range(4):
                    b = 4 * i + o
                    for w in range(2):
                        last = nc.tensor.matmul(bank[TC * w:TC * w + TC, P * o:P * o + P], CT[0:CC, TC * b:TC * b + TC],
                                                WC["V"][:, :], start=True, stop=True)
                last.then_inc(full, 1)
            pe.wait_ge(weights_set, 1)
            wait_drained(pe, start, "X", 0)
            project_values(start, 0, 0, 0)
            project_values(start, 1, 0, 0)
            for i in range(8):
                g, h = i // 2, i % 2
                bank, full = take(start, "KC", i)
                split(bank[0:NSTACK, :], lambda a: WCS[:, a, g, :, :].rearrange("p j c -> p (j c)"),
                      lambda b: CTR[:, b, 512 * h:512 * h + 512]).then_inc(full, 1)
            for g in range(NG):
                for kind in "KQC":
                    project(start, kind, g, 0)
            transpose_x(start, 1, 1, 1)
            for n in range(2):
                for j in range(4):
                    scores_for_max(start, j, n, n, n, 0, 0)
            wait_drained(pe, start, "S3", 0)
            transpose_max(start, 0, 0, 0)

            def body(s):
                for g in range(NG):
                    n = 4 * s.b + g
                    ahead = g < 2 or s.nxt
                    gn, sn, bn = (g + 2, s.slot, s.b) if g < 2 else (g - 2, 1 - s.slot, s.b + 1)
                    gp, sp_, bp = (g - 1, s.slot, s.b) if g else (3, 1 - s.slot, s.b - 1)
                    pairs = 2 * s.b + g // 2 if g else 2 * s.b
                    before = g or s.prev

                    def ahead_scores(j):
                        if ahead:
                            scores_for_max(s, j, g, gn, n + 2, sn, bn)

                    scores(s, g, 0, n)
                    ahead_scores(0)
                    if before:
                        sums(0, gp, n - 1, sp_, pairs, bp)
                    scores(s, g, 1, n)
                    ahead_scores(1)
                    if g == 3 and s.prev:
                        project_out(s, g, 2)
                    if s.nxt:
                        project(s, "K", g, 1 - s.slot)
                    if s.nxt:
                        project(s, "Q", g, 1 - s.slot)
                    if s.nxt:
                        project(s, "C", g, 1 - s.slot)
                    if before:
                        sums(1, gp, n - 1, sp_, pairs, bp)
                    if g < 3 or s.nxt:
                        pe.wait_ge(*max_wait(s, g))
                        transpose_max(s, g, n + 1, (g + 1) % 2)
                    ahead_scores(2)
                    ahead_scores(3)
                    if g == 0 and s.nxt:
                        project_values(s, 0, g, 1 - s.slot)
                    if g == 1 and s.prev:
                        transpose_sums(s, 1, g, s.b - 1)
                    if g == 1 and s.nxt:
                        project_values(s, 1, g, 1 - s.slot)
                    if g == 2 and s.prev:
                        transpose_y(s, g, s.b - 1)
                    if g == 2 and s.nxt2:
                        transpose_x(s, g, s.b + 2, s.slot)
                    if g == 3:
                        transpose_sums(s, 0, g, s.b)

            def max_wait(s, g):
                last = WHERE[BEFORE[s.part]] if g == 0 else WHERE[s.part]
                if g == 0:
                    back = len(last) - list(last).index(("S3", 1 if s.part == "first" else 3))
                    bank, before = s.at(min(WHERE[s.part].values()) - back)
                else:
                    bank, before = s.ring("S3", g - 1)
                return ring_free[bank], before + 1

            sequences(pe, body)
            sums(0, 3, 4 * NB - 1, 1, 2 * NB - 1, NB - 1)
            sums(1, 3, 4 * NB - 1, 1, 2 * NB - 1, NB - 1)
            transpose_sums(end, 1, 0, NB - 1)
            transpose_y(end, 0, NB - 1)
            project_out(end, 0, 0)


EXPERTS = 8
CAP = max(8, int(max(1, NB * T * 2 // EXPERTS) * 1.25))
FF = 512
NF = FF // P
TILES = 2 * NB
CT_ = CAP // P
CHUNKS = CT_ // 2
ROW = P + 1
NOWHERE = 1 << 20


def wait(eng, semaphore, value):
    if not (isinstance(value, int) and value <= 0):
        eng.wait_ge(semaphore, value)


def pipeline(eng, count, depth, unroll, body):
    lo = (depth // unroll + 1) * unroll
    hi = lo + (count - lo) // unroll * unroll
    for j in range(lo):
        body(j, j % unroll, lambda s, j=j: 0 <= j - s < count)
    with eng.Fori(lo, hi - unroll + 1, unroll) as i:
        for u in range(unroll):
            body(i + u, u, lambda s: True)
    for j in range(hi, count + depth):
        body(j, j % unroll, lambda s, j=j: 0 <= j - s < count)


class Norm:

    def __init__(self, nc, st, name, waited, slots=2):
        def sb(what, shape):
            return st.enter_context(nc.sbuf_tensor(f"{name}_{what}", shape, F32))

        def sem(what):
            return st.enter_context(nc.semaphore(f"{name}_{what}"))

        self.nc, self.slots = nc, slots
        self.stats, self.mv = sb("stats", [P, slots, 2, 6]), sb("mv", [P, slots, 2, 2])
        self.rstd, self.shift = sb("rstd", [P, slots, 2]), sb("shift", [P, slots, 2])
        self.var, self.power = sb("var", [P, slots, 2]), sb("power", [P, 2])
        self.stats_set, self.mv_set, self.var_set = sem("stats_set"), sem("mv_set"), sem("var_set")
        self.rstd_set, self.shift_set, self.xn_set = sem("rstd_set"), sem("shift_set"), sem("xn_set")
        self.power_set = sem("power_set")
        self.waited = waited

    def wait(self, eng, semaphore, value):
        eng.wait_ge(semaphore, value)
        if not isinstance(value, int):
            eng.sem_inc(self.waited, 1)

    def statistics(self, x, b, slot):
        for t in range(2):
            last = self.nc.vector.bn_stats(self.stats[:, slot, t, :], x(t))
        last.then_inc(self.stats_set, 1)

    def aggregate(self, dve, b, slot):
        if not isinstance(b, int) or b >= self.slots:
            self.wait(dve, self.shift_set, b + 1 - self.slots)
        self.wait(dve, self.stats_set, b + 1)
        for t in range(2):
            last = self.nc.vector.bn_aggr(self.mv[:, slot, t, :], self.stats[:, slot, t, :])
        last.then_inc(self.mv_set, 1)

    def variance(self, dve, b, slot):
        wait(dve, self.rstd_set, b + 1 - self.slots)
        dve.wait_ge(self.mv_set, b + 1)
        self.nc.vector.tensor_scalar(self.var[:, slot, :], self.mv[:, slot, :, 1], EPS, 1.0,
                                     ALU.add, ALU.mult).then_inc(self.var_set, 1)

    def prepare(self, pool):
        self.nc.gpsimd.memset(self.power[:, :], -0.5).then_inc(self.power_set, 1)
        pool.wait_ge(self.power_set, 1)

    def root(self, pool, b, slot):
        if not isinstance(b, int) or b >= self.slots:
            self.wait(pool, self.xn_set, b + 1 - self.slots)
        self.wait(pool, self.var_set, b + 1)
        self.nc.gpsimd.tensor_tensor(self.rstd[:, slot, :], self.var[:, slot, :], self.power[:, :],
                                     ALU.pow).then_inc(self.rstd_set, 1)

    def shifts(self, dve, b, slot):
        dve.wait_ge(self.rstd_set, b + 1)
        self.nc.vector.scalar_tensor_tensor(self.shift[:, slot, :], self.mv[:, slot, :, 0], -1.0, self.rstd[:, slot, :],
                                            ALU.mult, ALU.mult).then_inc(self.shift_set, 1)

    def normalise(self, dve, x, xn, b, slot, free):
        wait(dve, *free)
        self.wait(dve, self.shift_set, b + 1)
        for t in range(2):
            last = self.nc.vector.tensor_scalar(xn(t), x(t), self.rstd[:, slot, t:t + 1], self.shift[:, slot, t:t + 1],
                                                ALU.mult, ALU.add)
        last.then_inc(self.xn_set, 1)


def ffn0(nc, io, X, CT, XT, KT, V, wrT, ident, rows_in, rows_out):
    st = ExitStack()

    def sb(name, shape, dt=F32):
        return st.enter_context(nc.sbuf_tensor(name, shape, dt))

    def sem(name):
        return st.enter_context(nc.semaphore(name))

    with st:
        X2T = sb("X2T", [P, NB, T])
        XN = sb("f_xn", [P, 2, 2, P])
        Wr, brb = sb("f_wr", [P, EXPERTS]), sb("f_brb", [NB, EXPERTS])
        sc, top = sb("f_scores", [NB, EXPERTS]), sb("f_top", [NB, 8])
        chosen = sb("f_chosen", [NB, 8], U32)
        row = sb("f_row", [1, 2 * NB], U32)
        chosen_f, numbers = sb("f_chosen_f", [NB, 2]), sb("f_numbers", [NB, 2, EXPERTS])
        picks = sb("f_picks", [NB, 2, EXPERTS])
        picksT = sb("f_picks_t", [EXPERTS, 2, NB])
        bothT = sb("f_both_t", [EXPERTS, NB])
        both_now = sb("f_both_now", [EXPERTS, 2, P])
        blank = sb("f_blank", [P, CT_, ROW])
        W1_all, W2_all = sb("f_w1_all", [P, EXPERTS, P]), sb("f_w2_all", [P, EXPERTS, P])
        W1, W2 = sb("f_w1", [P, 2, 2, P]), sb("f_w2", [P, 4, 2, P])
        b1, b2 = sb("f_b1", [EXPERTS, P]), sb("f_b2", [EXPERTS, P])
        b1_of = sb("f_b1_of", [P, 2, NB])
        HT = sb("f_ht", [P, 2, 2, T])
        Wk, Wv, wr = sb("c_wk", [CC, P]), sb("c_wv", [CC + 1, P]), sb("c_wr", [EXPERTS, P])
        bk = sb("c_bk", [P, 1])
        ps_tr = [st.enter_context(nc.psum_tensor(f"f_tr{i}", [P, 512], F32)) for i in range(2)]
        ps_h = [st.enter_context(nc.psum_tensor(f"f_h{i}", [P, 512], F32)) for i in range(2)]
        ps_o = [st.enter_context(nc.psum_tensor(f"f_o{i}", [P, 512], F32)) for i in range(2)]
        ps_r = st.enter_context(nc.psum_tensor("f_r", [P, 512], F32))

        waited = sem("f_waited")
        ln2, ln3 = Norm(nc, st, "ln2", waited, slots=4), Norm(nc, st, "ln3", waited)
        ld_r, ld_c, ld_b, ones_set = sem("f_ld_r"), sem("f_ld_c"), sem("f_ld_b"), sem("f_ones_set")
        ld_w, weights_set = sem("f_ld_w"), sem("f_weights_set")
        zeros_set, zeros_out, consts_set = sem("f_zeros_set"), sem("f_zeros_out"), sem("f_consts_set")
        tr2_full, x2t_set, tr3_full, xt_set = sem("f_tr2_full"), sem("f_x2t_set"), sem("f_tr3_full"), sem("f_xt_set")
        r_full, chosen_set, row_set = sem("f_r_full"), sem("f_chosen_set"), sem("f_row_set")
        steps_done = sem("f_steps_done")
        picks_full, picks_t_set, b1_full, b1_set, both_now_set = (
            sem("f_picks_full"), sem("f_picks_t_set"), sem("f_b1_full"), sem("f_b1_set"), sem("f_both_now_set"))
        h_full, ht_set, o_full, added = sem("f_h_full"), sem("f_ht_set"), sem("f_o_full"), sem("f_added")
        c_full, c_set = sem("c_full"), sem("c_set")
        block = st.enter_context(nc.Block())
        DEPTH = 4

        @block.sync
        def _(sp):
            sp.dma_start(wr[:, :], io["L1_ffn_wr"]).then_inc(ld_c, 16)
            sp.dma_start(b1[:, :], io["L0_ffn_b1"]).then_inc(ld_c, 16)
            sp.dma_start(Wk[:, :], io["L1_xattn_Wk"]).then_inc(ld_c, 16)
            sp.dma_start(Wv[0:CC, :], io["L1_xattn_Wv"]).then_inc(ld_c, 16)
            sp.dma_start(Wv[CC:CC + 1, :], io["L1_xattn_bv"].rearrange("(a c) -> a c", a=1)).then_inc(ld_c, 16)
            with nc.allow_non_contiguous_dma(reason="a bias onto the partitions"):
                sp.dma_start(bk[:, :], io["L1_xattn_bk"].rearrange("(c a) -> c a", a=1)).then_inc(ld_b, 16)
            sp.dma_start(Wr[:, :], io["L0_ffn_Wr"]).then_inc(ld_r, 16)
            sp.dma_start(brb[:, :], io["L0_ffn_br"].rearrange("(a c) -> a c", a=1).to_broadcast([NB, EXPERTS])).then_inc(ld_r, 16)
            sp.dma_start(b2[:, :], io["L0_ffn_b2"]).then_inc(ld_r, 16)
            sp.dma_start(W1_all[:, :, :], io["L0_ffn_W1"].rearrange("e c d -> c e d")).then_inc(ld_w, 16)
            sp.dma_start(W2_all[:, :, :], io["L0_ffn_W2"].rearrange("e c d -> c e d")).then_inc(ld_w, 16)
            sp.wait_ge(zeros_set, 2)
            with sp.Fori(0, EXPERTS, 1) as e:
                sp.dma_start(rows_in[bass.ds(CAP * e, CAP), :].rearrange("(p t) c -> p t c", p=P),
                             blank[:, :, :]).then_inc(zeros_out, 16)
            sp.wait_ge(chosen_set, 1)
            with nc.allow_non_contiguous_dma(reason="two of eight"):
                sp.dma_start(row[:, :], chosen[:, 0:2]).then_inc(row_set, 16)
            with sp.Fori(0, 8, 1) as g:
                sp.dma_start(rows_out[bass.ds(8 * P * g, 8 * P), :].rearrange("(p t) c -> p t c", p=P),
                             blank[:, 0:8, 0:P]).then_inc(zeros_out, 16)
            sp.wait_ge(zeros_out, 16 * (EXPERTS + 8))

        @block.gpsimd
        def _(pool):
            nc.gpsimd.iota(numbers[:, :, :], pattern=[[0, 2], [1, EXPERTS]], base=0, channel_multiplier=0,
                           allow_small_or_imprecise_dtypes=True).then_inc(consts_set, 1)
            ln2.prepare(pool)
            ln3.prepare(pool)
            nc.gpsimd.memset(blank[:, :, 0:P], 0.0).then_inc(zeros_set, 1)
            nc.gpsimd.memset(blank[:, :, P:ROW], float(NOWHERE)).then_inc(zeros_set, 1)
            pipeline(pool, NB, 0, 4, lambda b, place, on: ln2.root(pool, b, place))
            nc.gpsimd.memset(V[:, :, :, :], 0.0).then_inc(consts_set, 1)
            pipeline(pool, NB, 0, 2, lambda b, place, on: ln3.root(pool, b, place))

        @block.scalar
        def _(act):
            act.preload_act_table(ACT.Gelu)
            def normed(j, place, on):
                if isinstance(j, int) and j == 3:
                    act.wait_ge(c_full, 1)
                    nc.scalar.copy(wrT[:, :], ps_r[:, 0:EXPERTS]).then_inc(c_set, 1)
                if on(1):
                    b, slot, other = j - 1, (place - 1) % 4, (place - 1) % 2
                    act.wait_ge(ln2.shift_set, b + 1)
                    wait(act, tr2_full, b - 1)
                    for t in range(2):
                        last = nc.scalar.activation(XN[:, other, t, :], X[:, bass.ds(2 * b + t, 1), :].rearrange("p a c -> p (a c)"),
                                                    ACT.Identity, bias=ln2.shift[:, slot, t:t + 1], scale=ln2.rstd[:, slot, t:t + 1])
                    last.then_inc(ln2.xn_set, 1)
                if not on(2):
                    return
                j = j - 2
                act.wait_ge(tr2_full, j + 1)
                nc.scalar.copy(X2T[:, bass.ds(j, 1), :].rearrange("p a t -> p (a t)"),
                               ps_tr[place % 2][:, 0:T]).then_inc(x2t_set, 1)

            pipeline(act, NB, 2, 4, normed)

            act.wait_ge(ld_b, 16)
            for i in range(2):
                act.wait_ge(c_full, 2 + i)
                nc.scalar.activation(KT[:, 8 * i:8 * i + 8, :].rearrange("p b t -> p (b t)"), ps_o[i][:, :], ACT.Identity,
                                     bias=bk[:, 0:1]).then_inc(c_set, 1)

            act.wait_ge(consts_set, 2)

            def values(i):
                act.wait_ge(c_full, 4 + i)
                for t in range(2):
                    half = slice(TC * t, TC * t + TC)
                    last = nc.scalar.copy(V[half, 4 * i:4 * i + 4, t, :],
                                          [*ps_h, *ps_tr][i][half, :].rearrange("p (b c) -> p b c", b=4))
                last.then_inc(c_set, 1)

            for i in range(4):
                values(i)
            act.wait_ge(picks_full, 1)
            nc.scalar.copy(picksT[:, :, :], ps_r[0:EXPERTS, 0:2 * NB].rearrange("e (k b) -> e k b", k=2)).then_inc(picks_t_set, 1)
            act.wait_ge(b1_full, 1)
            nc.scalar.copy(b1_of[:, :, :], ps_r[:, 0:2 * NB].rearrange("p (k b) -> p k b", k=2)).then_inc(b1_set, 1)
            act.wait_ge(b1_set, 1)
            act.wait_ge(ld_w, 32)
            act.wait_ge(row_set, 16)

            def body(j, place, on):
                other = 1 - place % 2
                if on(0):
                    e = [act.value_load(row[0:1, bass.ds(2 * j + k, 1)], min_val=0, max_val=EXPERTS - 1) for k in range(2)]
                    wait(act, h_full, j - 1)
                    for k in range(2):
                        nc.scalar.copy(W1[:, place % 2, k, :], W1_all[:, bass.ds(e[k], 1), :].rearrange("p a d -> p (a d)"))
                    wait(act, o_full, j - 3)
                    for k in range(2):
                        last = nc.scalar.copy(W2[:, place, k, :], W2_all[:, bass.ds(e[k], 1), :].rearrange("p a d -> p (a d)"))
                    last.then_inc(weights_set, 1)
                if on(1):
                    b = j - 1
                    act.wait_ge(h_full, b + 1)
                    wait(act, o_full, b - 1)
                    for k in range(2):
                        last = nc.scalar.activation(HT[:, other, k, :], ps_h[other][:, T * k:T * k + T], ACT.Gelu,
                                                    bias=b1_of[:, k, bass.ds(b, 1)])
                    last.then_inc(ht_set, 1)
                if on(4):
                    b = j - 4
                    act.wait_ge(tr3_full, b + 1)
                    nc.scalar.copy(XT[:, bass.ds(b, 1), :].rearrange("p a t -> p (a t)"),
                                   ps_tr[place % 2][:, 0:T]).then_inc(xt_set, 1)

            pipeline(act, NB, DEPTH, 4, body)

        @block.tensor
        def _(pe):
            def keys(i):
                nc.tensor.matmul(ps_o[i][:, :], Wk[:, :], CT[0:CC, 512 * i:512 * i + 512], start=True, stop=True).then_inc(c_full, 1)

            def values(i, of=range(4)):
                bank = [*ps_h, *ps_tr][i]
                for o in of:
                    b = 4 * i + o
                    for w in range(2):
                        last = nc.tensor.matmul(bank[TC * w:TC * w + TC, P * o:P * o + P], CT[:, TC * b:TC * b + TC], Wv[:, :],
                                                start=True, stop=True)
                if 3 in of:
                    last.then_inc(c_full, 1)

            def normed(j, place, on):
                if not on(0):
                    return
                if isinstance(j, int) and j == 2:
                    pe.wait_ge(ld_c, 16 * 5)
                    nc.tensor.transpose(ps_r[:, 0:EXPERTS], wr[:, :], ident[0:EXPERTS, 0:EXPERTS]).then_inc(c_full, 1)
                    keys(0)
                if isinstance(j, int) and j == 3:
                    keys(1)
                    pe.wait_ge(ones_set, 1)
                if isinstance(j, int) and j > 3:
                    values((j - 4) // 2, range(2 * (j % 2), 2 * (j % 2) + 2))
                pe.wait_ge(ln2.xn_set, j + 1)
                wait(pe, x2t_set, j - 1)
                for t in range(2):
                    last = nc.tensor.transpose(ps_tr[place % 2][:, P * t:P * t + P], XN[:, place % 2, t, :], ident[:, :])
                last.then_inc(tr2_full, 1)

            pipeline(pe, NB, 4, 4, normed)
            pe.wait_ge(x2t_set, NB)
            pe.wait_ge(c_set, 1)
            pe.wait_ge(ld_r, 16 * 3)
            nc.tensor.matmul(ps_r[0:NB, 0:EXPERTS], X2T[:, :, 0], Wr[:, :], start=True, stop=True).then_inc(r_full, 1)
            for i in range(2, 4):
                values(i)
            pe.wait_ge(steps_done, 4)
            for k in range(2):
                last = nc.tensor.transpose(ps_r[0:EXPERTS, NB * k:NB * k + NB], picks[:, k, :], ident[0:NB, 0:NB])
            last.then_inc(picks_full, 1)
            pe.wait_ge(picks_t_set, 1)
            nc.tensor.matmul(ps_r[:, 0:2 * NB], b1[:, :], picksT[:, :, :].rearrange("e k b -> e (k b)"),
                             start=True, stop=True).then_inc(b1_full, 1)
            pe.wait_ge(c_set, 7)

            def body(j, place, on):
                even = place % 2
                other = 1 - even
                if on(1):
                    b = j - 1
                    pe.wait_ge(weights_set, b + 1)
                    wait(pe, ht_set, b - 1)
                    for k in range(2):
                        last = nc.tensor.matmul(ps_h[other][:, T * k:T * k + T], W1[:, other, k, :],
                                                X2T[:, bass.ds(b, 1), :].rearrange("p a t -> p (a t)"), start=True, stop=True)
                    last.then_inc(h_full, 1)
                if on(2):
                    b = j - 2
                    pe.wait_ge(both_now_set, b + 1)
                    wait(pe, added, b - 1)
                    pe.wait_ge(ht_set, b + 1)
                    nc.tensor.matmul(ps_o[even][:, 0:T], both_now[:, even, :],
                                     b2[:, :].unsqueeze(1).to_broadcast([EXPERTS, 2, P]), start=True, stop=False,
                                     skip_group_check=True)
                    for k in range(2):
                        for t in range(2):
                            last = nc.tensor.matmul(ps_o[even][:, P * t:P * t + P], HT[:, even, k, P * t:P * t + P], W2[:, (place - 2) % 4, k, :],
                                                    start=False, stop=(k == 1), skip_group_check=True)
                    last.then_inc(o_full, 1)
                if on(4):
                    b = j - 4
                    pe.wait_ge(ln3.xn_set, b + 1)
                    wait(pe, xt_set, b - 1)
                    for t in range(2):
                        last = nc.tensor.transpose(ps_tr[even][:, P * t:P * t + P], XN[:, even, t, :], ident[:, :])
                    last.then_inc(tr3_full, 1)

            pipeline(pe, NB, DEPTH, 4, body)

        @block.vector
        def _(dve):
            def x(b):
                return lambda t: X[:, bass.ds(2 * b + t, 1), :].rearrange("p a c -> p (a c)")

            def normed(j, place, on):
                if on(0):
                    ln2.statistics(x(j), j, place)
                if on(2):
                    ln2.shifts(dve, j - 2, (place - 2) % 4)
                if on(0):
                    ln2.aggregate(dve, j, place)
                if on(0):
                    ln2.variance(dve, j, place)

            nc.vector.memset(CT[CC:CC + 1, :], 1.0).then_inc(ones_set, 1)
            pipeline(dve, NB, 2, 4, normed)
            dve.wait_ge(r_full, 1)
            nc.vector.tensor_tensor(sc[:, :], ps_r[0:NB, 0:EXPERTS], brb[:, :], ALU.add).then_inc(steps_done, 1)
            dve.wait_ge(steps_done, 1)
            nc.vector.max(top[:, :], sc[:, :]).then_inc(steps_done, 1)
            dve.wait_ge(steps_done, 2)
            nc.vector.max_index(chosen[:, :], top[:, :], sc[:, :]).then_inc(chosen_set, 1)
            dve.wait_ge(chosen_set, 1)
            nc.vector.tensor_copy(chosen_f[:, :], chosen[:, 0:2]).then_inc(steps_done, 1)
            dve.wait_ge(steps_done, 3)
            dve.wait_ge(consts_set, 2)
            nc.vector.tensor_tensor(picks[:, :, :], numbers[:, :, :], chosen_f[:, :].unsqueeze(2).to_broadcast([NB, 2, EXPERTS]),
                                    ALU.is_equal).then_inc(steps_done, 1)
            dve.wait_ge(picks_t_set, 1)
            nc.vector.tensor_tensor(bothT[:, :], picksT[:, 0, :], picksT[:, 1, :], ALU.add).then_inc(steps_done, 1)
            dve.wait_ge(steps_done, 5)

            def body(j, place, on):
                other = 1 - place
                if on(1):
                    b = j - 1
                    wait(dve, o_full, b - 1)
                    nc.vector.tensor_copy(both_now[:, other, :],
                                          bothT[:, bass.ds(b, 1)].to_broadcast([EXPERTS, P])).then_inc(both_now_set, 1)
                if on(2):
                    b = j - 2
                    dve.wait_ge(o_full, b + 1)
                    at = X[:, bass.ds(2 * b, 2), :].rearrange("p a c -> p (a c)")
                    nc.vector.scalar_tensor_tensor(at, ps_o[place][:, 0:T], 0.5, at, ALU.mult, ALU.add).then_inc(added, 1)
                if on(3):
                    ln3.shifts(dve, j - 3, other)
                if on(2):
                    ln3.wait(dve, added, j - 1)
                    ln3.statistics(x(j - 2), j - 2, place)
                if on(3):
                    b = j - 3
                    ln3.normalise(dve, x(b), lambda t: XN[:, other, t, :], b, other, (tr3_full, b - 1))
                if on(2):
                    ln3.aggregate(dve, j - 2, place)
                    ln3.variance(dve, j - 2, place)

            pipeline(dve, NB, DEPTH, 2, body)


def attention1(nc, io, X, XT, KT, V, wrT, TOPS, LATE, ident, rows_in, weights):
    st = ExitStack()

    def sb(name, shape, dt=F32):
        return st.enter_context(nc.sbuf_tensor(name, shape, dt))

    def sem(name):
        return st.enter_context(nc.semaphore(name))

    with st:
        X4 = sb("X4", [P, TILES, P])
        logits = sb("a_logits", [P, 2, 2, EXPERTS])
        top, picked = sb("a_top", [P, 2, 2, 8]), sb("a_picked", [P, 2, 2, 8], U32)
        expert = sb("a_expert", [P, 2, 2, 2])
        numbers = sb("a_numbers", [P, 2, 2, EXPERTS])
        own = sb("a_own", [P, 2, 2, 2, EXPERTS])
        mask = sb("a_mask", [P, 2, 2, EXPERTS], BF16)
        ones_f, onesb = sb("a_ones", [P, P]), sb("a_onesb", [P, P], BF16)
        before = sb("a_before", [P, P], BF16)
        carried = sb("a_carried", [P, 2, EXPERTS])
        position = sb("a_position", [P, 2, 2, EXPERTS])
        place_of, late, to_f = (sb("a_" + n, [P, 2, 2, 2]) for n in ("place_of", "late", "to_f"))
        to = sb("a_to", [P, 2, 2, 2], U32)
        home = sb("a_home", [P, 2, TILES])
        rows = sb("a_rows", [P, 2, 2, 2, ROW])
        Wq, bq = sb("a_wq", [P, P]), sb("a_bq", [P, 1])
        QT = sb("a_qt", [P, 2, T])
        negmax, total, inverse = sb("a_negmax", [P, 2, 2]), sb("a_total", [P, 2, 2]), sb("a_inverse", [P, 2, 2])
        E, ET = sb("a_e", [P, 2, 2 * TC]), sb("a_et", [P, 2, P])
        XN4S = sb("a_xn4", [P, 2, 2, P])
        XN4T = sb("a_x4t", [P, 2, T])
        ps_q, ps_e, ps_x, ps_l = (st.enter_context(nc.psum_tensor(f"a_ps_{k}", [P, 512], F32)) for k in "qexl")
        ps_s = [st.enter_context(nc.psum_tensor(f"a_ps_s{i}", [P, 512], F32)) for i in range(2)]
        ps_o, ps_p = (st.enter_context(nc.psum_tensor(f"a_ps_{k}", [P, 512], F32)) for k in "op")
        ln4 = Norm(nc, st, "ln4", sem("a_waited"))
        ld_a, q_full, qt_set = sem("a_ld"), sem("a_q_full"), sem("a_qt_set")
        s_full, max_set, exp_set, e_full, et_set = sem("a_s_full"), sem("a_max_set"), sem("a_exp_set"), sem("a_e_full"), sem("a_et_set")
        inverse_set, o_full, added = sem("a_inverse_set"), sem("a_o_full"), sem("a_added")
        x_full, xt_set, l_full, l_set = sem("a_x_full"), sem("a_xt_set"), sem("a_l_full"), sem("a_l_set")
        ones_set, consts_set, top_set, picked_set, expert_set = (
            sem("a_ones_set"), sem("a_consts_set"), sem("a_top_set"), sem("a_picked_set"), sem("a_expert_set"))
        own_set, mask_set, p_full, p_read, share_set = (
            sem("a_own_set"), sem("a_mask_set"), sem("a_p_full"), sem("a_p_read"), sem("a_share_set"))
        place_set, to_f_set, to_set, rows_set = sem("a_place_set"), sem("a_to_f_set"), sem("a_to_set"), sem("a_rows_set")
        scattered = [sem(f"a_scattered{i}") for i in range(2)]
        block = st.enter_context(nc.Block())
        DEPTH = 8

        def scatters(b, slot):
            return 32 * (b - slot) + 64

        @block.sync
        def _(sp):
            sp.dma_start(Wq[:, :], io["L1_xattn_Wq"]).then_inc(ld_a, 16)
            with nc.allow_non_contiguous_dma(reason="a bias onto the partitions"):
                sp.dma_start(bq[:, :], io["L1_xattn_bq"].rearrange("(c a) -> c a", a=1)).then_inc(ld_a, 16)
            sp.dma_start(weights.b1r[:, :], io["L1_ffn_b1"].rearrange("e (f c) -> (e f) c", c=P)).then_inc(weights.ld_b, 16)
            for e in range(2):
                weights.load(sp, io, e, e)
                weights.load_bias(sp, io, e, e)

        @block.gpsimd
        def _(pool):
            nc.gpsimd.memset(ones_f[:, :], 1.0).then_inc(ones_set, 1)
            nc.gpsimd.memset(carried[:, :, :], 0.0).then_inc(consts_set, 1)
            nc.gpsimd.iota(numbers[:, :, :, :], pattern=[[0, 4], [1, EXPERTS]], base=0, channel_multiplier=0,
                           allow_small_or_imprecise_dtypes=True).then_inc(consts_set, 1)
            nc.gpsimd.iota(home[:, :, :], pattern=[[NB * T, 2], [P, TILES]], base=0, channel_multiplier=1,
                           allow_small_or_imprecise_dtypes=True).then_inc(consts_set, 1)
            pool.wait_ge(ones_set, 1)
            nc.gpsimd.affine_select(out=before[:, :], in_=ones_f[:, :], compare_op=ALU.is_gt, fill=0.0, base=0,
                                    pattern=[[1, P]], channel_multiplier=-1).then_inc(consts_set, 1)
            nc.gpsimd.affine_select(out=onesb[:, :], in_=ones_f[:, :], compare_op=ALU.is_ge, fill=1.0, base=0,
                                    pattern=[[1, P]], channel_multiplier=0).then_inc(consts_set, 1)
            ln4.prepare(pool)

            def body(j, place, on):
                if on(0):
                    ln4.root(pool, j, place)
                if on(5):
                    b, slot = j - 5, 1 - place
                    ln4.wait(pool, rows_set, b + 1)
                    ln4.wait(pool, to_set, b + 1)
                    for k in range(2):
                        for t in range(2):
                            nc.gpsimd.indirect_dma_start(
                                out=rows_in, out_offset=bass.IndirectOffsetOnAxis(to[:, slot, k, t:t + 1], 0),
                                in_=rows[:, slot, k, t, :], in_offset=None, bounds_check=EXPERTS * CAP - 1,
                                oob_is_err=False).then_inc(scattered[slot], 16)

            pipeline(pool, NB, 5, 2, body)
            for i in range(2):
                pool.wait_ge(scattered[i], scatters(NB - 2 + i, i))

        @block.scalar
        def _(act):
            act.preload_act_table(ACT.Exp)
            act.wait_ge(consts_set, 5)
            act.wait_ge(ld_a, 32)

            def body(j, place, on):
                other = 1 - place
                if on(0):
                    act.wait_ge(q_full, j + 1)
                    wait(act, s_full, j - 1)
                    nc.scalar.activation(QT[:, place, :], ps_q[:, 0:T], ACT.Identity,
                                         bias=bq[:, 0:1]).then_inc(qt_set, 1)
                if on(1):
                    b = j - 1
                    act.wait_ge(max_set, b + 1)
                    wait(act, e_full, b - 1)
                    wait(act, inverse_set, b - 1)
                    for t in range(2):
                        last = nc.scalar.activation(E[:, other, TC * t:TC * t + TC], ps_s[other][:, TC * t:TC * t + TC], ACT.Exp,
                                                    bias=negmax[:, other, t:t + 1], accum_out=total[:, other, t:t + 1])
                    last.then_inc(exp_set, 1)
                if on(2):
                    b = j - 2
                    act.wait_ge(e_full, b + 1)
                    wait(act, o_full, b - 1)
                    nc.scalar.copy(ET[:, place, :], ps_e[:, 0:P]).then_inc(et_set, 1)
                if on(4):
                    b = j - 4
                    wait(act, xt_set, b - 1)
                    act.wait_ge(ln4.shift_set, b + 1)
                    for t in range(2):
                        last = nc.scalar.activation(XN4S[:, place, t, :], X[:, bass.ds(2 * b + t, 1), :].rearrange("p a c -> p (a c)"),
                                                    ACT.Identity, bias=ln4.shift[:, place, t:t + 1], scale=ln4.rstd[:, place, t:t + 1])
                    last.then_inc(ln4.xn_set, 1)
                if on(5):
                    b = j - 5
                    act.wait_ge(x_full, b + 1)
                    nc.scalar.copy(X4[:, bass.ds(2 * b, 2), :], XN4S[:, other, :, :])
                    wait(act, l_full, b - 1)
                    nc.scalar.copy(XN4T[:, other, :], ps_x[:, 0:T]).then_inc(xt_set, 1)
                if on(7):
                    b = j - 7
                    wait(act, scattered[other], scatters(b - 2, other) if not isinstance(b, int) or b > 1 else 0)
                    nc.scalar.copy(rows[:, other, :, :, 0:P], X4[:, bass.ds(2 * b, 2), :].unsqueeze(1).to_broadcast([P, 2, 2, P]))
                    nc.scalar.copy(rows[:, other, :, :, P], home[:, :, bass.ds(2 * b, 2)]).then_inc(rows_set, 1)

            pipeline(act, NB, DEPTH, 2, body)

        @block.tensor
        def _(pe):
            pe.wait_ge(ld_a, 32)
            pe.wait_ge(consts_set, 5)

            def body(j, place, on):
                other = 1 - place
                if on(0):
                    wait(pe, qt_set, j)
                    nc.tensor.matmul(ps_q[:, 0:T], Wq[:, :], XT[:, bass.ds(j, 1), :].rearrange("p a t -> p (a t)"),
                                     start=True, stop=True).then_inc(q_full, 1)
                if on(1):
                    b = j - 1
                    pe.wait_ge(qt_set, b + 1)
                    wait(pe, exp_set, b - 1)
                    for t in range(2):
                        last = nc.tensor.matmul(ps_s[other][:, TC * t:TC * t + TC], QT[:, other, P * t:P * t + P],
                                                KT[:, bass.ds(b, 1), :].rearrange("p a t -> p (a t)"), start=True, stop=True)
                    last.then_inc(s_full, 1)
                if on(2):
                    b = j - 2
                    pe.wait_ge(exp_set, b + 1)
                    wait(pe, et_set, b)
                    nc.tensor.transpose(ps_e[:, 0:P], E[:, place, :], ident[:, :]).then_inc(e_full, 1)
                if on(3):
                    b = j - 3
                    pe.wait_ge(et_set, b + 1)
                    wait(pe, added, b)
                    nc.tensor.matmul(ps_o[:, 0:T], ET[:, other, :], V[:, bass.ds(b, 1), :, :].rearrange("p a t c -> p (a t c)"),
                                     start=True, stop=True).then_inc(o_full, 1)
                if on(5):
                    b = j - 5
                    pe.wait_ge(ln4.xn_set, b + 1)
                    wait(pe, xt_set, b)
                    for t in range(2):
                        last = nc.tensor.transpose(ps_x[:, P * t:P * t + P], XN4S[:, other, t, :], ident[:, :])
                    last.then_inc(x_full, 1)
                if on(6):
                    b = j - 6
                    pe.wait_ge(xt_set, b + 1)
                    wait(pe, l_set, b)
                    for t in range(2):
                        last = nc.tensor.matmul(ps_l[:, 8 * t:8 * t + 8], XN4T[:, place, P * t:P * t + P], wrT[:, :],
                                                start=True, stop=True)
                    last.then_inc(l_full, 1)
                if on(8):
                    b = j - 8
                    pe.wait_ge(mask_set, b + 1)
                    wait(pe, p_read, b)
                    first, second = mask[:, place, 0, :], mask[:, place, 1, :]
                    nc.tensor.matmul(ps_p[:, 0:8], before[:, :], first, start=True, stop=True)
                    nc.tensor.matmul(ps_p[:, 8:16], before[:, :], second, start=True, stop=False)
                    nc.tensor.matmul(ps_p[:, 8:16], onesb[:, :], first, start=False, stop=True)
                    nc.tensor.matmul(ps_p[:, 16:24], onesb[:, :], first, start=True, stop=False)
                    nc.tensor.matmul(ps_p[:, 16:24], onesb[:, :], second, start=False, stop=True).then_inc(p_full, 1)

            pipeline(pe, NB, DEPTH, 2, body)

        @block.vector
        def _(dve):
            dve.wait_ge(consts_set, 5)

            def x(b):
                return lambda t: X[:, bass.ds(2 * b + t, 1), :].rearrange("p a c -> p (a c)")

            def body(j, place, on):
                other = 1 - place
                if on(1):
                    b = j - 1
                    dve.wait_ge(s_full, b + 1)
                    wait(dve, exp_set, b - 1)
                    nc.vector.tensor_reduce(negmax[:, other, :], ps_s[other][:, 0:P].rearrange("p (t k) -> p t k", t=2), AX.X, ALU.max,
                                            negate=True).then_inc(max_set, 1)
                if on(3):
                    b = j - 3
                    dve.wait_ge(exp_set, b + 1)
                    nc.vector.reciprocal(inverse[:, other, :], total[:, other, :]).then_inc(inverse_set, 1)
                    dve.wait_ge(inverse_set, b + 1)
                    dve.wait_ge(o_full, b + 1)
                    for t in range(2):
                        at = X[:, bass.ds(2 * b + t, 1), :].rearrange("p a c -> p (a c)")
                        last = nc.vector.scalar_tensor_tensor(at, ps_o[:, P * t:P * t + P], inverse[:, other, t:t + 1], at,
                                                              ALU.mult, ALU.add)
                    last.then_inc(added, 1)
                    ln4.wait(dve, added, b + 1)
                    ln4.statistics(x(b), b, other)
                if on(4):
                    ln4.shifts(dve, j - 4, place)
                if on(3):
                    ln4.aggregate(dve, j - 3, other)
                if on(3):
                    ln4.variance(dve, j - 3, other)
                if on(6):
                    b = j - 6
                    dve.wait_ge(l_full, b + 1)
                    nc.vector.tensor_copy(logits[:, place, :, :], ps_l[:, 0:16].rearrange("p (t e) -> p t e", t=2)).then_inc(l_set, 1)
                if on(8):
                    b = j - 8
                    dve.wait_ge(p_full, b + 1)
                    nc.vector.tensor_tensor(carried[:, other, :], carried[:, place, :], ps_p[:, 16:24], ALU.add)
                    nc.vector.tensor_tensor(position[:, place, :, :], ps_p[:, 0:16].rearrange("p (t e) -> p t e", t=2),
                                            carried[:, place, :].unsqueeze(1).to_broadcast([P, 2, EXPERTS]),
                                            ALU.add).then_inc(p_read, 1)
                if on(7):
                    b = j - 7
                    ln4.wait(dve, l_set, b + 1)
                    for t in range(2):
                        last = nc.vector.max(top[:, other, t, :], logits[:, other, t, :])
                    last.then_inc(top_set, 1)
                if on(8):
                    b = j - 8
                    dve.wait_ge(p_read, b + 1)
                    nc.vector.tensor_tensor(own[:, place, :, :, :], own[:, place, :, :, :],
                                            position[:, place, :, :].unsqueeze(1).to_broadcast([P, 2, 2, EXPERTS]),
                                            ALU.mult).then_inc(share_set, 1)
                if on(7):
                    b = j - 7
                    ln4.wait(dve, top_set, b + 1)
                    for t in range(2):
                        last = nc.vector.max_index(picked[:, other, t, :], top[:, other, t, :], logits[:, other, t, :])
                    last.then_inc(picked_set, 1)
                if on(8):
                    b = j - 8
                    dve.wait_ge(share_set, b + 1)
                    nc.vector.tensor_reduce(place_of[:, place, :, :], own[:, place, :, :, :], AX.X, ALU.add).then_inc(place_set, 1)
                if on(7):
                    b = j - 7
                    nc.vector.tensor_copy(TOPS[:, bass.ds(2 * b, 2), :], top[:, other, :, 0:2])
                    dve.wait_ge(picked_set, b + 1)
                    nc.vector.tensor_copy(expert[:, other, :, :].rearrange("p k t -> p t k"),
                                          picked[:, other, :, 0:2]).then_inc(expert_set, 1)
                if on(8):
                    b = j - 8
                    dve.wait_ge(place_set, b + 1)
                    nc.vector.tensor_scalar(late[:, place, :, :], place_of[:, place, :, :], float(CAP) - 0.5, 0.0, ALU.is_gt, ALU.add)
                    nc.vector.scalar_tensor_tensor(to_f[:, place, :, :], expert[:, place, :, :], float(CAP),
                                                   place_of[:, place, :, :], ALU.mult, ALU.add).then_inc(to_f_set, 1)
                if on(7):
                    b = j - 7
                    dve.wait_ge(expert_set, b + 1)
                    nc.vector.tensor_tensor(own[:, other, :, :, :], numbers[:, :, :, :],
                                            expert[:, other, :, :].unsqueeze(3).to_broadcast([P, 2, 2, EXPERTS]),
                                            ALU.is_equal).then_inc(own_set, 1)
                if on(8):
                    b = j - 8
                    dve.wait_ge(to_f_set, b + 1)
                    nc.vector.tensor_copy(LATE[:, :, bass.ds(2 * b, 2)], late[:, place, :, :])
                    wait(dve, scattered[place], scatters(b - 2, place) if not isinstance(b, int) or b > 1 else 0)
                    nc.vector.scalar_tensor_tensor(to[:, place, :, :], late[:, place, :, :], float(NOWHERE), to_f[:, place, :, :],
                                                   ALU.mult, ALU.add).then_inc(to_set, 1)
                if on(7):
                    b = j - 7
                    wait(dve, p_full, b - 1)
                    dve.wait_ge(own_set, b + 1)
                    nc.vector.tensor_tensor(mask[:, other, :, :], own[:, other, 0, :, :], own[:, other, 1, :, :],
                                            ALU.add).then_inc(mask_set, 1)

            pipeline(dve, NB, DEPTH, 2, body)


class Weights:

    def __init__(self, nc, st):
        def sb(name, shape):
            return st.enter_context(nc.sbuf_tensor("m_" + name, shape, F32))

        self.w1, self.w2 = sb("w1", [P, 2, FF]), sb("w2", [P, 2, NF, P])
        self.b2b, self.b1r = sb("b2b", [P, 2, 2, P]), sb("b1r", [EXPERTS * NF, P])
        self.loaded = [st.enter_context(nc.semaphore(f"m_ld_w{i}")) for i in range(2)]
        self.ld_b = st.enter_context(nc.semaphore("m_ld_b"))

    def load(self, sp, io, e, slot):
        for to, name, rest in ((self.w1[:, slot, :], "w1", "a c f -> (a c) f"),
                               (self.w2[:, slot, :, :], "w2", "a (f p) c -> p (a f) c")):
            sp.dma_start(to, io["L1_ffn_" + name][bass.ds(e, 1), :, :].rearrange(rest, **({"p": P} if name == "w2" else {}))
                         ).then_inc(self.loaded[slot], 16)

    def load_bias(self, sp, io, e, slot):
        for t in range(2):
            sp.dma_start(self.b2b[:, slot, t, :], io["L1_ffn_b2"][bass.ds(e, 1), :].to_broadcast([P, P])).then_inc(self.loaded[slot], 16)


def moe(nc, io, out, X, weights, TOPS, LATE, ident, rows_in, rows_out):
    st = ExitStack()

    def sb(name, shape, dt=F32):
        return st.enter_context(nc.sbuf_tensor(name, shape, dt))

    def sem(name):
        return st.enter_context(nc.semaphore(name))

    with st:
        gate = sb("m_gate", [P, 2, TILES])
        gap, grown, denominator = sb("m_gap", [P, TILES]), sb("m_grown", [P, TILES]), sb("m_denominator", [P, TILES])
        home = sb("m_home", [P, 2, CT_], U32)
        back = sb("m_back", [P, 4, 2, 4, P])
        w1, w2, b2b, b1r = weights.w1, weights.w2, weights.b2b, weights.b1r
        b1T, b1c = sb("m_b1t", [P, EXPERTS * NF]), sb("m_b1c", [P, 2, NF])
        W1 = sb("m_w1s", [P, 2, 2, FF], F32R)
        XG = sb("m_xg", [P, 2, CT_, ROW])
        XR = sb("m_xr", [P, 2, 2, CAP], F32R)
        HT = sb("m_ht", [P, 2, NF, T])
        Y = sb("m_y", [P, 2, CT_, P])
        ps_h = [st.enter_context(nc.psum_tensor(f"m_h{i}", [P, NF, T], F32)) for i in range(2)]
        ps_y = [st.enter_context(nc.psum_tensor(f"m_y{i}", [P, 512], F32)) for i in range(2)]
        ps_t = [st.enter_context(nc.psum_tensor(f"m_t{i}", [P, 512], F32)) for i in range(2)]

        chain = sem("m_chain")
        gap_set, grown_set, home_set = sem("m_gap_set"), sem("m_grown_set"), sem("m_home_set")
        b1_full, b1_set, bias_set = sem("m_b1_full"), sem("m_b1_set"), sem("m_bias_set")
        ld_w, ld_x = weights.loaded, [sem(f"m_ld_x{i}") for i in range(2)]
        w_high_set, w_set = sem("m_w_high_set"), sem("m_w_set")
        x_high_set = sem("m_x_high_set")
        t_full, xgt_set, h_full, ht_set = sem("m_t_full"), sem("m_xgt_set"), sem("m_h_full"), sem("m_ht_set")
        y_full, y_set, y_sent = sem("m_y_full"), sem("m_y_set"), [sem(f"m_y_sent{i}") for i in range(2)]
        ld_back, half_added, added = [sem(f"m_ld_back{i}") for i in range(4)], sem("m_half_added"), sem("m_added")
        all_sent, weighed = sem("m_all_sent"), sem("m_weighed")
        stored = sem("m_stored")
        waited = sem("m_waited")
        block = st.enter_context(nc.Block())
        ALL = EXPERTS * CHUNKS

        def rows(x, e):
            return x[bass.ds(CAP * e, CAP), :].rearrange("(t p) c -> p t c", p=P)

        @block.sync
        def _(sp):
            def load_weights(e, slot):
                sp.wait_ge(y_full, CHUNKS * (e - 1))
                weights.load(sp, io, e, slot)
                sp.wait_ge(y_set, CHUNKS * (e - 1))
                weights.load_bias(sp, io, e, slot)

            def load_tokens(e, slot):
                wait(sp, xgt_set, CHUNKS * (e - 1))
                wait(sp, home_set, e - 1)
                sp.dma_start(XG[:, slot, :, :], rows(rows_in, e)).then_inc(ld_x[slot], 16)

            load_tokens(0, 0)
            load_tokens(1, 1)
            with sp.Fori(2, EXPERTS - 1, 2) as e:
                for u in range(2):
                    load_tokens(e + u, u)
                    load_weights(e + u, u)
            ov = out.rearrange("b (t p) c -> p (b t) c", p=P)

            def load_back(g, slot):
                for k in range(2):
                    sp.dma_start(back[:, slot, k, :, :],
                                 rows_out[bass.ds(NB * T * k + 4 * P * g, 4 * P), :].rearrange("(t p) c -> p t c", p=P)).then_inc(ld_back[slot], 16)

            sp.wait_ge(all_sent, 1)
            for g in range(4):
                load_back(g, g)
            for g in range(8):
                sp.wait_ge(added, g + 1)
                if g < 4:
                    load_back(g + 4, g)
                sp.dma_start(ov[:, 4 * g:4 * g + 4, :], X[:, 4 * g:4 * g + 4, :]).then_inc(stored, 16)
            sp.wait_ge(stored, 16 * 8)

        @block.gpsimd
        def _(pool):
            def send(e, slot):
                for c in range(CHUNKS):
                    pool.wait_ge(y_set, CHUNKS * e + c + 1)
                    if not isinstance(e, int):
                        pool.sem_inc(waited, 1)
                    for t in range(2 * c, 2 * c + 2):
                        nc.gpsimd.indirect_dma_start(
                            out=rows_out, out_offset=bass.IndirectOffsetOnAxis(home[:, slot, t:t + 1], 0),
                            in_=Y[:, slot, t, :], in_offset=None, bounds_check=2 * NB * T - 1,
                            oob_is_err=False).then_inc(y_sent[slot], 16)

            with pool.Fori(0, EXPERTS - 1, 2) as e:
                for u in range(2):
                    send(e + u, u)
            for i in range(2):
                pool.wait_ge(y_sent[i], 16 * CT_ * (EXPERTS // 2))
            pool.sem_inc(all_sent, 1)

        @block.scalar
        def _(act):
            act.preload_act_table(ACT.Exp)
            act.wait_ge(gap_set, 1)
            nc.scalar.activation(grown[:, :], gap[:, :], ACT.Exp).then_inc(grown_set, 1)
            act.preload_act_table(ACT.Gelu_apprx_tanh)

            def body(e, slot):
                for c in range(CHUNKS):
                    m, s2 = CHUNKS * e + c, (slot + c) % 2
                    if c == 0:
                        act.wait_ge(bias_set, e + 1)
                    wait(act, y_full, m - 1)
                    act.wait_ge(h_full, m + 1)
                    for f in range(NF):
                        last = nc.scalar.activation(HT[:, s2, f, :], ps_h[s2][:, f, :], ACT.Gelu_apprx_tanh,
                                                    bias=b1c[:, slot, f:f + 1])
                    last.then_inc(ht_set, 1)

            body(0, 0)
            body(1, 1)
            with act.Fori(2, EXPERTS - 1, 2) as e:
                for u in range(2):
                    body(e + u, u)

            with act.Fori(0, 5, 4) as g:
                for u in range(4):
                    act.wait_ge(ld_back[u], 8 * g + 32)
                    for t in range(4):
                        at = back[:, u, 1, t, :]
                        last = nc.scalar.activation(at, at, ACT.Identity, scale=gate[:, 1, bass.ds(4 * g + 4 * u + t, 1)])
                    last.then_inc(weighed, 1)

        @block.tensor
        def _(pe):
            pe.wait_ge(weights.ld_b, 16)
            nc.tensor.transpose(ps_y[0][:, 0:EXPERTS * NF], b1r[:, :], ident[0:EXPERTS * NF, 0:EXPERTS * NF]).then_inc(b1_full, 1)
            pe.wait_ge(b1_set, 1)

            def transpose_rows(m, e, c, slot, s2):
                if c == 0:
                    pe.wait_ge(ld_x[slot], 8 * (e - slot) + 16)
                wait(pe, xgt_set, m - 1)
                for t in range(2):
                    last = nc.tensor.transpose(ps_t[s2][:, P * t:P * t + P], XG[:, slot, 2 * c + t, 0:P], ident[:, :])
                last.then_inc(t_full, 1)

            def hidden(m, e, c, slot, s2):
                pe.wait_ge(xgt_set, m + 1)
                if c == 0:
                    pe.wait_ge(w_set, e + 1)
                wait(pe, ht_set, m - 1)
                for f in range(NF):
                    for i, (a, b) in enumerate(((0, 0), (1, 0), (0, 1))):
                        last = nc.tensor.matmul(ps_h[s2][:, f, :], W1[:, slot, a, P * f:P * f + P], XR[:, slot, b, T * c:T * c + T],
                                                start=(i == 0), stop=(i == 2))
                last.then_inc(h_full, 1)

            def outputs(m, slot, s2):
                wait(pe, y_set, m - 1)
                pe.wait_ge(ht_set, m + 1)
                for t in range(2):
                    for f in range(NF):
                        last = nc.tensor.matmul(ps_y[s2][:, P * t:P * t + P], HT[:, s2, f, P * t:P * t + P], w2[:, slot, f, :],
                                                start=(f == 0), stop=(f == NF - 1))
                last.then_inc(y_full, 1)

            def body(e, slot, first=False, final=False):
                for c in range(CHUNKS):
                    m, s2 = CHUNKS * e + c, (slot + c) % 2
                    hidden(m, e, c, slot, s2)
                    if not final:
                        transpose_rows(m + CHUNKS, e + 1, c, 1 - slot, 1 - s2)
                    if not (first and c == 0):
                        outputs(m - 1, slot if c else 1 - slot, 1 - s2)

            for c in range(CHUNKS):
                transpose_rows(c, 0, c, 0, c % 2)
            body(0, 0, first=True)
            with pe.Fori(1, EXPERTS - 2, 2) as e:
                body(e, 1)
                body(e + 1, 0)
            body(EXPERTS - 1, 1, final=True)
            outputs(ALL - 1, 1, (ALL - 1) % 2)

        @block.vector
        def _(dve):
            count = [0]

            def then(ins):
                count[0] += 1
                ins.then_inc(chain, 1)
                dve.wait_ge(chain, count[0])

            nc.vector.tensor_tensor(gap[:, :], TOPS[:, :, 1], TOPS[:, :, 0], ALU.subtract).then_inc(gap_set, 1)
            dve.wait_ge(b1_full, 1)
            nc.vector.tensor_copy(b1T[:, :], ps_y[0][:, 0:EXPERTS * NF]).then_inc(b1_set, 1)
            dve.wait_ge(grown_set, 1)
            then(nc.vector.tensor_scalar(denominator[:, :], grown[:, :], 1.0, 0.0, ALU.add, ALU.add))
            then(nc.vector.reciprocal(denominator[:, :], denominator[:, :]))
            nc.vector.tensor_copy(gate[:, 0, :], denominator[:, :])
            nc.vector.tensor_tensor(gate[:, 1, :], grown[:, :], denominator[:, :], ALU.mult)
            then(nc.vector.tensor_scalar(LATE[:, :, :], LATE[:, :, :], -1.0, 1.0, ALU.mult, ALU.add))
            then(nc.vector.tensor_tensor(gate[:, :, :], gate[:, :, :], LATE[:, :, :], ALU.mult))
            def split_weights(e, slot):
                dve.wait_ge(ld_w[slot], 32 * (e - slot) + 64)
                nc.vector.tensor_copy(W1[:, slot, 0, :], w1[:, slot, :]).then_inc(w_high_set, 1)
                dve.wait_ge(w_high_set, e + 1)
                nc.vector.tensor_tensor(W1[:, slot, 1, :], w1[:, slot, :], W1[:, slot, 0, :], ALU.subtract).then_inc(w_set, 1)

            def drain_rows(m, c, slot, s2):
                dve.wait_ge(t_full, m + 1)
                high, low = (XR[:, slot, i, T * c:T * c + T] for i in range(2))
                nc.vector.tensor_copy(high, ps_t[s2][:, 0:T]).then_inc(x_high_set, 1)
                dve.wait_ge(x_high_set, m + 1)
                nc.vector.tensor_tensor(low, ps_t[s2][:, 0:T], high, ALU.subtract).then_inc(xgt_set, 1)

            def drain_outputs(m, e, c, slot, s2):
                if c == 0:
                    wait(dve, y_sent[slot], 8 * CT_ * (e - slot))
                    nc.vector.tensor_copy(home[:, slot, :], XG[:, slot, :, P]).then_inc(home_set, 1)
                dve.wait_ge(y_full, m + 1)
                nc.vector.tensor_tensor(Y[:, slot, 2 * c:2 * c + 2, :].rearrange("p t c -> p (t c)"), ps_y[s2][:, 0:T],
                                        b2b[:, slot, :, :].rearrange("p t c -> p (t c)"), ALU.add).then_inc(y_set, 1)

            def bias(e, slot):
                nc.vector.tensor_copy(b1c[:, slot, :], b1T[:, bass.ds(NF * e, NF)]).then_inc(bias_set, 1)

            def body(e, slot, first=False, final=False):
                for c in range(CHUNKS):
                    m, s2 = CHUNKS * e + c, (slot + c) % 2
                    if not final:
                        drain_rows(m + CHUNKS, c, 1 - slot, 1 - s2)
                    if c:
                        drain_outputs(m - 1, e, c - 1, slot, 1 - s2)
                    elif not first:
                        drain_outputs(m - 1, e - 1, CHUNKS - 1, 1 - slot, 1 - s2)
                    if c == 2 and not final:
                        bias(e + 1, 1 - slot)
                    if c == 3 and not final:
                        split_weights(e + 1, 1 - slot)

            split_weights(0, 0)
            dve.wait_ge(b1_set, 1)
            bias(0, 0)
            for c in range(CHUNKS):
                drain_rows(c, c, 0, c % 2)
            body(0, 0, first=True)
            body(1, 1)
            with dve.Fori(2, EXPERTS - 3, 2) as e:
                for u in range(2):
                    body(e + u, u)
            body(EXPERTS - 2, 0)
            body(EXPERTS - 1, 1, final=True)
            drain_outputs(ALL - 1, EXPERTS - 1, CHUNKS - 1, 1, (ALL - 1) % 2)

            def combine(g, slot):
                dve.wait_ge(ld_back[slot], 8 * (g - slot) + 32)
                for t in range(4):
                    at = X[:, bass.ds(4 * g + t, 1), :].rearrange("p a c -> p (a c)")
                    last = nc.vector.scalar_tensor_tensor(at, back[:, slot, 0, t, :], gate[:, 0, bass.ds(4 * g + t, 1)],
                                                          at, ALU.mult, ALU.add)
                last.then_inc(half_added, 1)
                dve.wait_ge(half_added, g + 1)
                dve.wait_ge(weighed, g + 1)
                at = X[:, bass.ds(4 * g, 4), :]
                nc.vector.tensor_tensor(at, at, back[:, slot, 1, :, :], ALU.add).then_inc(added, 1)

            with dve.Fori(0, 5, 4) as g:
                for u in range(4):
                    combine(g + u, u)


def program(nc, io, out):
    with ExitStack() as ctx:
        X = ctx.enter_context(nc.sbuf_tensor("X", [P, 2 * NB, P], F32))
        ident = ctx.enter_context(nc.sbuf_tensor("ident", [P, P], F32))
        CT = ctx.enter_context(nc.sbuf_tensor("CT", [CC + 1, NB * TC], F32))
        identb = ctx.enter_context(nc.sbuf_tensor("identb", [P, P], BF16))
        rows_in = nc.dram_tensor("expert_rows", (EXPERTS * CAP, ROW), F32).ap()
        rows_out = nc.dram_tensor("expert_outputs", (2 * NB * T, P), F32).ap()
        attention0(nc, io, X, CT, ident, identb)
        TOPS = ctx.enter_context(nc.sbuf_tensor("TOPS", [P, TILES, 2], F32))
        LATE = ctx.enter_context(nc.sbuf_tensor("LATE", [P, 2, TILES], F32))
        weights = Weights(nc, ctx)
        with ExitStack() as st:
            XT = st.enter_context(nc.sbuf_tensor("XT", [P, NB, T], F32))
            KT = st.enter_context(nc.sbuf_tensor("KT", [P, NB, TC], F32))
            V = st.enter_context(nc.sbuf_tensor("V", [P, NB, 2, P], F32))
            wrT = st.enter_context(nc.sbuf_tensor("wrT", [P, EXPERTS], F32))
            ffn0(nc, io, X, CT, XT, KT, V, wrT, ident, rows_in, rows_out)
            attention1(nc, io, X, XT, KT, V, wrT, TOPS, LATE, ident, rows_in, weights)
        moe(nc, io, out, X, weights, TOPS, LATE, ident, rows_in, rows_out)


NAMES = ["x", "ctx_512"] + ["L0_xattn_" + n for n in ("Wk", "bk", "Wq", "bq", "Wv", "bv", "Wck", "bck", "Wcq", "bcq",
                                                     "Wcv", "bcv", "Wp", "bp")] + [
    "L0_ffn_" + n for n in ("Wr", "br", "W1", "b1", "W2", "b2")] + [
    "L1_xattn_" + n for n in ("Wq", "bq", "Wk", "bk", "Wv", "bv")] + ["L1_ffn_" + n for n in ("wr", "w1", "b1", "w2", "b2")]


def kernel(**inputs):
    import concourse.bacc as bacc
    from concourse.bass_utils import run_bass_kernel_spmd

    nc = bacc.Bacc("TRN2", target_bir_lowering=False, num_devices=1)
    arrays, io = {}, {}
    for name in NAMES:
        a = np.ascontiguousarray(inputs[name])
        arrays[name + "_dram"] = a
        io[name] = nc.dram_tensor(name + "_dram", a.shape, mybir.dt.from_np(a.dtype), kind="ExternalInput").ap()
    out = nc.dram_tensor("out_dram", (NB, T, P), F32, kind="ExternalOutput").ap()
    program(nc, io, out)
    return run_bass_kernel_spmd(nc, [arrays], core_ids=[0]).results[0]["out_dram"]
```
